# Optimizing a Trainium2 kernel written in Bass

```python
import numpy as np
import jax
import jax.numpy as jnp

def _softmax(x, axis=-1):
    return jax.nn.softmax(x, axis=axis)

def _gelu(x):
    return jax.nn.gelu(x, approximate=True)

def _silu(x):
    return jax.nn.silu(x)

def _sigmoid(x):
    return jax.nn.sigmoid(x)

def _layernorm(x, axis=-1, eps=1e-05):
    m = jnp.mean(x, axis=axis, keepdims=True)
    v = jnp.var(x, axis=axis, keepdims=True)
    return (x - m) / jnp.sqrt(v + eps)

def _scatter_add(tgt, idx, src, axis=0):
    return tgt.at[idx].add(src)

def _segment_sum(src, seg, n):
    return jax.ops.segment_sum(src, seg, n)
kernel_name = 'mk_seq_preln_d1_jaxref_r4_21e067'

def setup_inputs(seed: int=0):
    np.random.seed(seed)
    _w = jnp.asarray

    def _L0_attn_setup():
        import jax, jax.numpy as jnp
        import numpy as np
        B, T, HID = (4, 512, 256)
        H, DK, DV, K = (8, 64, 128, 4)
        EPS = 1e-05

        def _dw_causal_conv(x, w, b):
            xt = jnp.transpose(x, (0, 2, 1))
            y = jax.lax.conv_general_dilated(xt, w, window_strides=(1,), padding=[(K - 1, 0)], dimension_numbers=('NCH', 'OIH', 'NCH'), feature_group_count=x.shape[-1])
            y = y + b[None, :, None]
            return jnp.transpose(y, (0, 2, 1))

        def _forward(x, Wq, Wk, Wv, Wa, ba, Wb, bb, Wg, Wo, qc_w, qc_b, kc_w, kc_b, vc_w, vc_b, ln_w, ln_b):
            b, t = (x.shape[0], x.shape[1])
            scale = DK ** (-0.5)
            q = x @ Wq.T
            k = x @ Wk.T
            v = x @ Wv.T
            q = jax.nn.silu(_dw_causal_conv(q, qc_w, qc_b))
            k = jax.nn.silu(_dw_causal_conv(k, kc_w, kc_b))
            v = jax.nn.silu(_dw_causal_conv(v, vc_w, vc_b))
            q = q.reshape(b, t, H, DK)
            k = (k * scale).reshape(b, t, H, DK)
            v = v.reshape(b, t, H, DV)
            a = jax.nn.sigmoid(x @ Wa.T + ba).reshape(b, t, H, DV)
            beta = jax.nn.sigmoid(x @ Wb.T + bb)

            def step(S, ins):
                q_t, k_t, v_t, a_t, b_t = ins
                read = jnp.einsum('bhk,bhkv->bhv', k_t, S)
                err = read - v_t
                S = a_t[:, :, None, :] * S - b_t[:, :, None, None] * k_t[..., None] * err[:, :, None, :]
                o_t = jnp.einsum('bhk,bhkv->bhv', q_t, S)
                return (S, o_t)
            to_tbh = lambda u: jnp.moveaxis(u, 1, 0)
            S0 = jnp.zeros((b, H, DK, DV), x.dtype)
            _, o = jax.lax.scan(step, S0, (to_tbh(q), to_tbh(k), to_tbh(v), to_tbh(a), to_tbh(beta)))
            o = jnp.moveaxis(o, 0, 1)
            mu = jnp.mean(o, axis=-1, keepdims=True)
            var = jnp.mean((o - mu) ** 2, axis=-1, keepdims=True)
            o = (o - mu) * jax.lax.rsqrt(var + EPS) * ln_w + ln_b
            g = jax.nn.sigmoid(x @ Wg.T).reshape(b, t, H, DV)
            o = (o * g).reshape(b, t, H * DV)
            return o @ Wo.T
        key = jax.random.key(seed)
        ks = jax.random.split(key, 20)
        s = 0.02
        inp = {'x': jax.random.normal(ks[0], (B, T, HID), jnp.float32), 'Wq': jax.random.normal(ks[1], (H * DK, HID), jnp.float32) * s, 'Wk': jax.random.normal(ks[2], (H * DK, HID), jnp.float32) * s, 'Wv': jax.random.normal(ks[3], (H * DV, HID), jnp.float32) * s, 'Wa': jax.random.normal(ks[4], (H * DV, HID), jnp.float32) * s, 'ba': jax.random.normal(ks[5], (H * DV,), jnp.float32) * s, 'Wb': jax.random.normal(ks[6], (H, HID), jnp.float32) * s, 'bb': jax.random.normal(ks[7], (H,), jnp.float32) * s, 'Wg': jax.random.normal(ks[8], (H * DV, HID), jnp.float32) * s, 'Wo': jax.random.normal(ks[9], (HID, H * DV), jnp.float32) * s, 'qc_w': jax.random.normal(ks[10], (H * DK, 1, K), jnp.float32) * 0.3, 'qc_b': jnp.zeros((H * DK,), jnp.float32), 'kc_w': jax.random.normal(ks[11], (H * DK, 1, K), jnp.float32) * 0.3, 'kc_b': jnp.zeros((H * DK,), jnp.float32), 'vc_w': jax.random.normal(ks[12], (H * DV, 1, K), jnp.float32) * 0.3, 'vc_b': jnp.zeros((H * DV,), jnp.float32), 'ln_w': jnp.ones((DV,), jnp.float32), 'ln_b': jnp.zeros((DV,), jnp.float32)}
        return inp
    _L0_attn_in = _L0_attn_setup()

    def _L0_ffn_setup():
        import jax, jax.numpy as jnp
        import numpy as np
        DIM = 256
        DEPTH = 2
        HEADS = 8
        DIM_HEAD = 64
        WINDOW = 128
        INNER = HEADS * DIM_HEAD
        HID = int(DIM * 4 * 2 / 3)
        B, N = (2, 2048)
        QK_SCALE = 8.0

        def shift_token(t):
            t1, t2 = jnp.split(t, 2, axis=-1)
            t2 = jnp.pad(t2, ((0, 0), (1, 0), (0, 0)))[:, :-1]
            return jnp.concatenate([t1, t2], axis=-1)

        def l2norm(t):
            return t / jnp.clip(jnp.linalg.norm(t, axis=-1, keepdims=True), 1e-12)

        def rotate_half(x):
            x1, x2 = jnp.split(x, 2, axis=-1)
            return jnp.concatenate([-x2, x1], axis=-1)

        def rotary_xpos(q, k):
            n = q.shape[-2]
            half_idx = jnp.arange(0, DIM_HEAD, 2, dtype=jnp.float32)
            inv_freq = 1.0 / 10000.0 ** (half_idx / DIM_HEAD)
            t = jnp.arange(n, dtype=jnp.float32)
            freqs = t[:, None] * inv_freq[None, :]
            freqs = jnp.concatenate([freqs, freqs], axis=-1)
            base = (half_idx + 0.4 * DIM_HEAD) / (1.4 * DIM_HEAD)
            power = (t - n // 2) / float(WINDOW // 2)
            scale = base[None, :] ** power[:, None]
            scale = jnp.concatenate([scale, scale], axis=-1)
            cos, sin = (jnp.cos(freqs), jnp.sin(freqs))
            q = q * cos * scale + rotate_half(q) * sin * scale
            k = k * cos / scale + rotate_half(k) * sin / scale
            return (q, k)

        def local_attention(q, k, v):
            b, h, n, d = q.shape
            w = n // WINDOW
            bq = q.reshape(b, h, w, WINDOW, d) * QK_SCALE
            bk = k.reshape(b, h, w, WINDOW, d)
            bv = v.reshape(b, h, w, WINDOW, d)

            def look_around(t):
                p = jnp.pad(t, ((0, 0), (0, 0), (1, 0), (0, 0), (0, 0)))
                return jnp.concatenate([p[:, :, :w], p[:, :, 1:]], axis=3)
            bk, bv = (look_around(bk), look_around(bv))
            bt = jnp.arange(n).reshape(w, WINDOW)
            btp = jnp.pad(bt, ((1, 0), (0, 0)), constant_values=-1)
            btk = jnp.concatenate([btp[:w], btp[1:]], axis=1)
            sim = jnp.einsum('bhwid,bhwjd->bhwij', bq, bk)
            i = bt[:, :, None]
            j = btk[:, None, :]
            mask = (i < j) | (i > j + WINDOW) | (j == -1)
            sim = jnp.where(mask, -jnp.finfo(sim.dtype).max, sim)
            attn = jax.nn.softmax(sim, axis=-1)
            out = jnp.einsum('bhwij,bhwjd->bhwid', attn, bv)
            return out.reshape(b, h, n, d)

        def _layer(x, wqkv, qs, ksc, wo, lg, lb, w1, b1, w2, b2):
            b, n, _ = x.shape
            h = shift_token(x)
            qkv = h @ wqkv
            q, k, v = jnp.split(qkv, 3, axis=-1)
            to_heads = lambda t: t.reshape(b, n, HEADS, DIM_HEAD).transpose(0, 2, 1, 3)
            q, k, v = (to_heads(q), to_heads(k), to_heads(v))
            q = l2norm(q) * qs
            k = l2norm(k) * ksc
            q, k = rotary_xpos(q, k)
            o = local_attention(q, k, v)
            o = o.transpose(0, 2, 1, 3).reshape(b, n, INNER)
            x = x + o @ wo
            h = shift_token(x)
            mu = h.mean(-1, keepdims=True)
            var = h.var(-1, keepdims=True)
            h = (h - mu) / jnp.sqrt(var + 1e-05) * lg + lb
            h = h @ w1 + b1
            a, g = jnp.split(h, 2, axis=-1)
            h = a * jax.nn.gelu(g, approximate=False)
            x = x + h @ w2 + b2
            return x
        key = jax.random.key(seed)
        ks = jax.random.split(key, 6)
        return {'x': jax.random.normal(ks[0], (B, N, DIM), jnp.float32), 'wqkv': jax.random.normal(ks[1], (DEPTH, DIM, 3 * INNER), jnp.float32) * 0.02, 'q_scale': jnp.ones((DEPTH, DIM_HEAD), jnp.float32), 'k_scale': jnp.ones((DEPTH, DIM_HEAD), jnp.float32), 'wo': jax.random.normal(ks[2], (DEPTH, INNER, DIM), jnp.float32) * 0.02, 'ln_g': jnp.ones((DEPTH, DIM), jnp.float32), 'ln_b': jnp.zeros((DEPTH, DIM), jnp.float32), 'w1': jax.random.normal(ks[3], (DEPTH, DIM, 2 * HID), jnp.float32) * 0.02, 'b1': jnp.zeros((DEPTH, 2 * HID), jnp.float32), 'w2': jax.random.normal(ks[4], (DEPTH, HID, DIM), jnp.float32) * 0.02, 'b2': jnp.zeros((DEPTH, DIM), jnp.float32)}
    _L0_ffn_in = _L0_ffn_setup()
    _d = {'L0_attn_x': _L0_attn_in['x'], 'L0_attn_Wq': _L0_attn_in['Wq'], 'L0_attn_Wk': _L0_attn_in['Wk'], 'L0_attn_Wv': _L0_attn_in['Wv'], 'L0_attn_Wa': _L0_attn_in['Wa'], 'L0_attn_ba': _L0_attn_in['ba'], 'L0_attn_Wb': _L0_attn_in['Wb'], 'L0_attn_bb': _L0_attn_in['bb'], 'L0_attn_Wg': _L0_attn_in['Wg'], 'L0_attn_Wo': _L0_attn_in['Wo'], 'L0_attn_qc_w': _L0_attn_in['qc_w'], 'L0_attn_qc_b': _L0_attn_in['qc_b'], 'L0_attn_kc_w': _L0_attn_in['kc_w'], 'L0_attn_kc_b': _L0_attn_in['kc_b'], 'L0_attn_vc_w': _L0_attn_in['vc_w'], 'L0_attn_vc_b': _L0_attn_in['vc_b'], 'L0_attn_ln_w': _L0_attn_in['ln_w'], 'L0_attn_ln_b': _L0_attn_in['ln_b'], 'L0_ffn_wqkv': _L0_ffn_in['wqkv'], 'L0_ffn_q_scale': _L0_ffn_in['q_scale'], 'L0_ffn_k_scale': _L0_ffn_in['k_scale'], 'L0_ffn_wo': _L0_ffn_in['wo'], 'L0_ffn_ln_g': _L0_ffn_in['ln_g'], 'L0_ffn_ln_b': _L0_ffn_in['ln_b'], 'L0_ffn_w1': _L0_ffn_in['w1'], 'L0_ffn_b1': _L0_ffn_in['b1'], 'L0_ffn_w2': _L0_ffn_in['w2'], 'L0_ffn_b2': _L0_ffn_in['b2']}
    _x0 = _d['L0_attn_x']
    _d['L0_attn_x'] = jax.random.normal(jax.random.fold_in(jax.random.key(seed), 1), (8, 512, 256), dtype=_x0.dtype)
    del _x0
    return _d

def reference(L0_attn_x, L0_attn_Wq, L0_attn_Wk, L0_attn_Wv, L0_attn_Wa, L0_attn_ba, L0_attn_Wb, L0_attn_bb, L0_attn_Wg, L0_attn_Wo, L0_attn_qc_w, L0_attn_qc_b, L0_attn_kc_w, L0_attn_kc_b, L0_attn_vc_w, L0_attn_vc_b, L0_attn_ln_w, L0_attn_ln_b, L0_ffn_wqkv, L0_ffn_q_scale, L0_ffn_k_scale, L0_ffn_wo, L0_ffn_ln_g, L0_ffn_ln_b, L0_ffn_w1, L0_ffn_b1, L0_ffn_w2, L0_ffn_b2):

    def _L0_attn_ref(x, Wq, Wk, Wv, Wa, ba, Wb, bb, Wg, Wo, qc_w, qc_b, kc_w, kc_b, vc_w, vc_b, ln_w, ln_b):
        import jax, jax.numpy as jnp
        import numpy as np
        B, T, HID = (4, 512, 256)
        H, DK, DV, K = (8, 64, 128, 4)
        EPS = 1e-05

        def _dw_causal_conv(x, w, b):
            xt = jnp.transpose(x, (0, 2, 1))
            y = jax.lax.conv_general_dilated(xt, w, window_strides=(1,), padding=[(K - 1, 0)], dimension_numbers=('NCH', 'OIH', 'NCH'), feature_group_count=x.shape[-1])
            y = y + b[None, :, None]
            return jnp.transpose(y, (0, 2, 1))

        def _forward(x, Wq, Wk, Wv, Wa, ba, Wb, bb, Wg, Wo, qc_w, qc_b, kc_w, kc_b, vc_w, vc_b, ln_w, ln_b):
            b, t = (x.shape[0], x.shape[1])
            scale = DK ** (-0.5)
            q = x @ Wq.T
            k = x @ Wk.T
            v = x @ Wv.T
            q = jax.nn.silu(_dw_causal_conv(q, qc_w, qc_b))
            k = jax.nn.silu(_dw_causal_conv(k, kc_w, kc_b))
            v = jax.nn.silu(_dw_causal_conv(v, vc_w, vc_b))
            q = q.reshape(b, t, H, DK)
            k = (k * scale).reshape(b, t, H, DK)
            v = v.reshape(b, t, H, DV)
            a = jax.nn.sigmoid(x @ Wa.T + ba).reshape(b, t, H, DV)
            beta = jax.nn.sigmoid(x @ Wb.T + bb)

            def step(S, ins):
                q_t, k_t, v_t, a_t, b_t = ins
                read = jnp.einsum('bhk,bhkv->bhv', k_t, S)
                err = read - v_t
                S = a_t[:, :, None, :] * S - b_t[:, :, None, None] * k_t[..., None] * err[:, :, None, :]
                o_t = jnp.einsum('bhk,bhkv->bhv', q_t, S)
                return (S, o_t)
            to_tbh = lambda u: jnp.moveaxis(u, 1, 0)
            S0 = jnp.zeros((b, H, DK, DV), x.dtype)
            _, o = jax.lax.scan(step, S0, (to_tbh(q), to_tbh(k), to_tbh(v), to_tbh(a), to_tbh(beta)))
            o = jnp.moveaxis(o, 0, 1)
            mu = jnp.mean(o, axis=-1, keepdims=True)
            var = jnp.mean((o - mu) ** 2, axis=-1, keepdims=True)
            o = (o - mu) * jax.lax.rsqrt(var + EPS) * ln_w + ln_b
            g = jax.nn.sigmoid(x @ Wg.T).reshape(b, t, H, DV)
            o = (o * g).reshape(b, t, H * DV)
            return o @ Wo.T
        return _forward(x, Wq, Wk, Wv, Wa, ba, Wb, bb, Wg, Wo, qc_w, qc_b, kc_w, kc_b, vc_w, vc_b, ln_w, ln_b)

    def _L0_ffn_ref(x, wqkv, q_scale, k_scale, wo, ln_g, ln_b, w1, b1, w2, b2):
        import jax, jax.numpy as jnp
        import numpy as np
        DIM = 256
        DEPTH = 2
        HEADS = 8
        DIM_HEAD = 64
        WINDOW = 128
        INNER = HEADS * DIM_HEAD
        HID = int(DIM * 4 * 2 / 3)
        B, N = (2, 2048)
        QK_SCALE = 8.0

        def shift_token(t):
            t1, t2 = jnp.split(t, 2, axis=-1)
            t2 = jnp.pad(t2, ((0, 0), (1, 0), (0, 0)))[:, :-1]
            return jnp.concatenate([t1, t2], axis=-1)

        def l2norm(t):
            return t / jnp.clip(jnp.linalg.norm(t, axis=-1, keepdims=True), 1e-12)

        def rotate_half(x):
            x1, x2 = jnp.split(x, 2, axis=-1)
            return jnp.concatenate([-x2, x1], axis=-1)

        def rotary_xpos(q, k):
            n = q.shape[-2]
            half_idx = jnp.arange(0, DIM_HEAD, 2, dtype=jnp.float32)
            inv_freq = 1.0 / 10000.0 ** (half_idx / DIM_HEAD)
            t = jnp.arange(n, dtype=jnp.float32)
            freqs = t[:, None] * inv_freq[None, :]
            freqs = jnp.concatenate([freqs, freqs], axis=-1)
            base = (half_idx + 0.4 * DIM_HEAD) / (1.4 * DIM_HEAD)
            power = (t - n // 2) / float(WINDOW // 2)
            scale = base[None, :] ** power[:, None]
            scale = jnp.concatenate([scale, scale], axis=-1)
            cos, sin = (jnp.cos(freqs), jnp.sin(freqs))
            q = q * cos * scale + rotate_half(q) * sin * scale
            k = k * cos / scale + rotate_half(k) * sin / scale
            return (q, k)

        def local_attention(q, k, v):
            b, h, n, d = q.shape
            w = n // WINDOW
            bq = q.reshape(b, h, w, WINDOW, d) * QK_SCALE
            bk = k.reshape(b, h, w, WINDOW, d)
            bv = v.reshape(b, h, w, WINDOW, d)

            def look_around(t):
                p = jnp.pad(t, ((0, 0), (0, 0), (1, 0), (0, 0), (0, 0)))
                return jnp.concatenate([p[:, :, :w], p[:, :, 1:]], axis=3)
            bk, bv = (look_around(bk), look_around(bv))
            bt = jnp.arange(n).reshape(w, WINDOW)
            btp = jnp.pad(bt, ((1, 0), (0, 0)), constant_values=-1)
            btk = jnp.concatenate([btp[:w], btp[1:]], axis=1)
            sim = jnp.einsum('bhwid,bhwjd->bhwij', bq, bk)
            i = bt[:, :, None]
            j = btk[:, None, :]
            mask = (i < j) | (i > j + WINDOW) | (j == -1)
            sim = jnp.where(mask, -jnp.finfo(sim.dtype).max, sim)
            attn = jax.nn.softmax(sim, axis=-1)
            out = jnp.einsum('bhwij,bhwjd->bhwid', attn, bv)
            return out.reshape(b, h, n, d)

        def _layer(x, wqkv, qs, ksc, wo, lg, lb, w1, b1, w2, b2):
            b, n, _ = x.shape
            h = shift_token(x)
            qkv = h @ wqkv
            q, k, v = jnp.split(qkv, 3, axis=-1)
            to_heads = lambda t: t.reshape(b, n, HEADS, DIM_HEAD).transpose(0, 2, 1, 3)
            q, k, v = (to_heads(q), to_heads(k), to_heads(v))
            q = l2norm(q) * qs
            k = l2norm(k) * ksc
            q, k = rotary_xpos(q, k)
            o = local_attention(q, k, v)
            o = o.transpose(0, 2, 1, 3).reshape(b, n, INNER)
            x = x + o @ wo
            h = shift_token(x)
            mu = h.mean(-1, keepdims=True)
            var = h.var(-1, keepdims=True)
            h = (h - mu) / jnp.sqrt(var + 1e-05) * lg + lb
            h = h @ w1 + b1
            a, g = jnp.split(h, 2, axis=-1)
            h = a * jax.nn.gelu(g, approximate=False)
            x = x + h @ w2 + b2
            return x
        for l in range(DEPTH):
            x = _layer(x, wqkv[l], q_scale[l], k_scale[l], wo[l], ln_g[l], ln_b[l], w1[l], b1[l], w2[l], b2[l])
        return x
    x = L0_attn_x
    x = x + _L0_attn_ref(_layernorm(x, axis=-1), L0_attn_Wq, L0_attn_Wk, L0_attn_Wv, L0_attn_Wa, L0_attn_ba, L0_attn_Wb, L0_attn_bb, L0_attn_Wg, L0_attn_Wo, L0_attn_qc_w, L0_attn_qc_b, L0_attn_kc_w, L0_attn_kc_b, L0_attn_vc_w, L0_attn_vc_b, L0_attn_ln_w, L0_attn_ln_b)
    x = x + _L0_ffn_ref(_layernorm(x, axis=-1), L0_ffn_wqkv, L0_ffn_q_scale, L0_ffn_k_scale, L0_ffn_wo, L0_ffn_ln_g, L0_ffn_ln_b, L0_ffn_w1, L0_ffn_b1, L0_ffn_w2, L0_ffn_b2)
    return x

_drawn_inputs = setup_inputs


def setup_inputs(seed=0):
    import zlib

    import numpy as np

    out = dict(_drawn_inputs(seed))
    spreads = {'L0_attn_qc_b': (0.0, 0.1),
     'L0_attn_kc_b': (0.0, 0.1),
     'L0_attn_vc_b': (0.0, 0.1),
     'L0_attn_ln_w': (1.0, 0.6),
     'L0_attn_ln_b': (0.0, 0.1),
     'L0_ffn_q_scale': (1.0, 0.6),
     'L0_ffn_k_scale': (1.0, 0.6),
     'L0_ffn_ln_g': (1.0, 0.6),
     'L0_ffn_ln_b': (0.0, 0.8),
     'L0_ffn_b1': (0.0, 0.8),
     'L0_ffn_b2': (0.0, 0.1)}
    factors = {'L0_attn_Wa': 7.304,
     'L0_attn_ba': 59.772,
     'L0_attn_Wb': 4.987,
     'L0_attn_bb': 59.075,
     'L0_attn_Wg': 4.08,
     'L0_ffn_wqkv': 2.995,
     'L0_ffn_wo': 2.984}
    for name, (base, spread) in spreads.items():
        noise = np.random.default_rng([zlib.crc32(name.encode()), seed]).standard_normal(out[name].shape)
        drawn = base * np.exp(spread * noise) if base else spread * noise
        out[name] = jnp.asarray(drawn.astype(out[name].dtype))
    for name, factor in factors.items():
        out[name] = (out[name] * factor).astype(out[name].dtype)
    return out
```

```python
from contextlib import ExitStack

import concourse.bass as bass
from concourse import mybir

F32 = mybir.dt.float32
BF16 = mybir.dt.bfloat16
ALU = mybir.AluOpType
ACT = mybir.ActivationFunctionType
AX = mybir.AxisListType

P = 128
B, T, C = 8, 512, 256
KC = C // P
H, DK, DV, TAPS = 8, 64, 128, 4
EPS = 1e-5

WT, CT, ST = 32, 16, 4
NW, NCH, NSUB = T // WT, T // CT, CT // ST
MCH = WT // CT
NC_ = H // 2 * B
NG = NC_ // 4
TW = B * WT


class Chain:

    def __init__(self, eng, sem):
        self.eng, self.sem, self.k = eng, sem, 0

    def run(self, ins):
        self.k += 1
        ins.then_inc(self.sem, 1)
        self.eng.wait_ge(self.sem, self.k)

    def restart(self):
        self.eng.sem_inc(self.sem, 1)
        self.eng.wait_ge(self.sem, self.k + 1)
        self.eng.sem_clear(self.sem)
        self.k = 0


def clear_after(nc, ctx, sems):
    def clear():
        with nc.Block() as block:
            @block.gpsimd
            def _(pool):
                for s in sems:
                    pool.sem_clear(s)
    ctx.callback(clear)


def norm_and_beta(nc, x, wb, bb, ident, xr_d, xn_d, beta_d, betak_d, o_d):
    with ExitStack() as ctx:
        def sb(name, shape, dt=F32):
            return ctx.enter_context(nc.sbuf_tensor("n_" + name, shape, dt))

        def pb(name, shape=(P, 512)):
            return ctx.enter_context(nc.psum_tensor("n_" + name, list(shape), F32))

        sems = []

        def sem(name):
            sems.append(ctx.enter_context(nc.semaphore("n_" + name)))
            return sems[-1]

        x_in = sb("x_in", [P, 2, T // P, C])
        x_t = sb("x_t", [P, 2, KC, T])
        cen = sb("cen", [P, KC, T])
        sq = sb("sq", [P, KC, T])
        std = sb("std", [P, T])
        rstd = sb("rstd", [P, T])
        xn = sb("xn", [P, 2, KC, T])
        be = sb("be", [H, 2, T])
        bek = sb("bek", [H, 2, T])
        zero = sb("zero", [P, 2 * TW])
        id_sb = sb("id", [P, P])
        mean_w = sb("mean_w", [P, P])
        eps = sb("eps", [P, 1])
        wb_sb = sb("wb", [P, KC, H])
        bb_sb = sb("bb", [H, 1])
        x_ps = [pb("x_ps0"), pb("x_ps1")]
        mu_ps, var_ps, be_ps = pb("mu_ps"), pb("var_ps"), pb("be_ps")

        consts_in, consts = sem("consts_in"), sem("consts")
        x_loaded = [sem("x_loaded0"), sem("x_loaded1")]
        turned, copied = sem("turned"), sem("copied")
        mean_done, centred, squared = sem("mean_done"), sem("centred"), sem("squared")
        var_done, std_done, normed = sem("var_done"), sem("std_done"), sem("normed")
        beta_done, beta_sig = sem("beta_done"), sem("beta_sig")
        stored = [sem("stored0"), sem("stored1")]
        padded = sem("padded")
        dve_own, act_own = sem("dve_own"), sem("act_own")
        STORES = 2 * KC + 4

        clear_after(nc, ctx, sems)
        block = ctx.enter_context(nc.Block())

        def nth(it, u, k=1, per=1):
            return it * (2 * per) + (u * per + k)

        @block.sync
        def _(sp):
            sp.dma_start(id_sb[:, :], ident).then_inc(consts_in, 16)
            sp.dma_start(wb_sb[:, :, :], wb.rearrange("(k p) h -> p k h", p=P)).then_inc(consts_in, 16)
            sp.dma_start(bb_sb[:, :], bb).then_inc(consts_in, 16)
            sp.wait_ge(consts, 1)
            for w in (NW, NW + 1):
                sp.dma_start(xn_d[w].rearrange("p k b t -> p (k b t)"), zero[:, 0:KC * TW]).then_inc(padded, 16)
                for n in range(4):
                    sp.dma_start(o_d[w].rearrange("p h c t -> p (h c t)")[:, n * 2 * TW:(n + 1) * 2 * TW], zero[:, :])\
                        .then_inc(padded, 16)
            sp.dma_start(xr_d[NW].rearrange("p k b t -> p (k b t)"), zero[:, 0:KC * TW]).then_inc(padded, 16)
            for d in (beta_d, betak_d):
                sp.dma_start(d[NW].rearrange("h j b t -> (h j) (b t)"), zero[0:H, 0:TW]).then_inc(padded, 16)
            with sp.Fori(0, B // 2) as it:
                for u in range(2):
                    sp.wait_ge(turned, nth(it, u))
                    sp.dma_start(x_in[:, u, :, :], x[bass.ds(it * 2 + u, 1)].rearrange("o (n p) c -> p (o n) c", p=P))\
                        .then_inc(x_loaded[u], 16)
                for u in range(2):
                    bslice = bass.ds(it * 2 + u, 1)
                    sp.wait_ge(copied, nth(it, u, 2))
                    for k in range(KC):
                        sp.dma_start(xr_d[0:NW, :, k, bslice, :].rearrange("w p o t -> p (w o) t"),
                                     x_t[:, u, k, :].rearrange("p (w t) -> p w t", t=WT)).then_inc(stored[u], 16)
                    sp.wait_ge(normed, nth(it, u, 2))
                    for k in range(KC):
                        sp.dma_start(xn_d[0:NW, :, k, bslice, :].rearrange("w p o t -> p (w o) t"),
                                     xn[:, u, k, :].rearrange("p (w t) -> p w t", t=WT)).then_inc(stored[u], 16)
                    sp.wait_ge(beta_sig, nth(it, u, 2))
                    for hh in range(2):
                        for d, s in ((beta_d, be), (betak_d, bek)):
                            sp.dma_start(d[0:NW, hh, :, bslice, :].rearrange("w j o t -> j (w o) t"),
                                         s[4 * hh:4 * hh + 4, u, :].rearrange("p (w t) -> p w t", t=WT))\
                                .then_inc(stored[u], 16)
            for u in range(2):
                sp.wait_ge(stored[u], 16 * STORES * (B // 2 + 1))
            sp.wait_ge(padded, 16 * 13)

        @block.gpsimd
        def _(pool):
            pool.memset(zero[:, :], 0.0).then_inc(consts, 1)

        @block.tensor
        def _(pe):
            pe.sem_inc(turned, 2)
            pe.wait_ge(consts_in, 48)
            with pe.Fori(0, B // 2) as it:
                for u in range(2):
                    pe.wait_ge(x_loaded[u], it * 16 + 16)
                    pe.wait_ge(copied, nth(it, u))
                    for n in range(T // P):
                        for k in range(KC):
                            mm = pe.transpose(x_ps[k][:, n * P:(n + 1) * P], x_in[:, u, n, k * P:(k + 1) * P], id_sb[:, :])
                    mm.then_inc(turned, 1)
                for u in range(2):
                    pe.wait_ge(copied, nth(it, u, 2))
                    pe.wait_ge(centred, nth(it, u))
                    for k in range(KC):
                        mm = pe.matmul(mu_ps[:, :], mean_w[:, :], x_t[:, u, k, :], start=(k == 0), stop=(k == KC - 1))
                    mm.then_inc(mean_done, 1)
                    pe.wait_ge(squared, nth(it, u, 2))
                    for k in range(KC):
                        mm = pe.matmul(var_ps[:, :], mean_w[:, :], sq[:, k, :], start=(k == 0), stop=(k == KC - 1))
                    mm.then_inc(var_done, 1)
                    pe.wait_ge(normed, nth(it, u, 2))
                    pe.wait_ge(beta_sig, nth(it, u))
                    for k in range(KC):
                        mm = pe.matmul(be_ps[0:H, :], wb_sb[:, k, :], xn[:, u, k, :], start=(k == 0), stop=(k == KC - 1))
                    mm.then_inc(beta_done, 1)

        @block.scalar
        def _(act):
            act.sem_inc(copied, 1)
            act.sem_inc(squared, 1)
            act.sem_inc(beta_sig, 1)
            act.wait_ge(consts_in, 48)
            own = Chain(act, act_own)
            with act.Fori(0, B // 2) as it:
                own.restart()
                for u in range(2):
                    act.wait_ge(stored[u], it * (16 * STORES) + 16 * STORES)
                    act.wait_ge(turned, nth(it, u, 3))
                    own.run(nc.scalar.activation(x_t[:, u, 0, :], x_ps[0][:, :], ACT.Copy))
                    nc.scalar.activation(x_t[:, u, 1, :], x_ps[1][:, :], ACT.Copy).then_inc(copied, 1)
                for u in range(2):
                    act.wait_ge(centred, nth(it, u, 2))
                    act.wait_ge(var_done, nth(it, u))
                    nc.scalar.activation(sq[:, :, :], cen[:, :, :], ACT.Square).then_inc(squared, 1)
                    act.wait_ge(var_done, nth(it, u, 2))
                    nc.scalar.activation(std[:, :], var_ps[:, :], ACT.Sqrt, bias=eps[:, :]).then_inc(std_done, 1)
                    act.wait_ge(beta_done, nth(it, u, 2))
                    own.run(nc.scalar.activation(be[:, u, :], be_ps[0:H, :], ACT.Sigmoid, bias=bb_sb[:, :]))
                    nc.scalar.activation(bek[:, u, :], be[:, u, :], ACT.Copy, scale=-1.0 / DK).then_inc(beta_sig, 1)

        @block.vector
        def _(dve):
            own = Chain(dve, dve_own)
            own.run(dve.memset(mean_w[:, :], 1.0 / C))
            own.run(dve.memset(eps[:, :], EPS))
            dve.sem_inc(centred, 1)
            dve.sem_inc(normed, 1)
            dve.sem_inc(var_done, 1)
            dve.sem_inc(mean_done, 1)
            dve.sem_inc(std_done, 1)
            dve.sem_inc(beta_done, 1)
            for u in range(2):
                dve.sem_inc(stored[u], 16 * STORES)
            with dve.Fori(0, B // 2) as it:
                own.restart()
                for u in range(2):
                    dve.wait_ge(mean_done, nth(it, u, 2))
                    own.run(dve.tensor_tensor(cen[:, 0, :], x_t[:, u, 0, :], mu_ps[:, :], ALU.subtract))
                    dve.tensor_tensor(cen[:, 1, :], x_t[:, u, 1, :], mu_ps[:, :], ALU.subtract).then_inc(centred, 1)
                    dve.wait_ge(centred, nth(it, u, 2))
                    dve.wait_ge(std_done, nth(it, u, 2))
                    dve.wait_ge(stored[u], it * (16 * STORES) + 16 * STORES)
                    own.run(dve.reciprocal(rstd[:, :], std[:, :]))
                    own.run(dve.tensor_tensor(xn[:, u, 0, :], cen[:, 0, :], rstd[:, :], ALU.mult))
                    dve.tensor_tensor(xn[:, u, 1, :], cen[:, 1, :], rstd[:, :], ALU.mult).then_inc(normed, 1)
                    dve.wait_ge(normed, nth(it, u, 2))


def recurrence(nc, wq, wk, wv, wa, ba, cw_qk, cb_qk, cw_v, cb_v, ident, row_mask, xn_d, beta_d, betak_d, o_d):
    HP = H // 2
    QO, GO = (0, 1, 3, 6), (None, 10, 11, 13)
    NPR = 16
    TILES = [("q", j) for j in range(HP)] + [("k", j) for j in range(HP)] + \
            [("v", h) for h in range(H)] + [("a", h) for h in range(H)]
    NT, NCONV = len(TILES), 2 * HP + H
    PER_SUB = (4, 4, 4, 3, 3, 3, 3, 0)
    FIRST = [sum(PER_SUB[:i]) for i in range(len(PER_SUB) + 1)]
    assert FIRST[-1] == NT
    SLOTS = 4

    with ExitStack() as ctx:
        def sb(name, shape, dt=F32):
            return ctx.enter_context(nc.sbuf_tensor("r_" + name, shape, dt))

        sems = []

        def sem(name):
            sems.append(ctx.enter_context(nc.semaphore("r_" + name)))
            return sems[-1]

        id_sb = sb("id", [P, P])
        ones = sb("ones", [P, P])
        rmask = sb("rmask", [P, NSUB - 1, 2, 4])
        w_q, w_k = sb("wq", [P, KC, H * DK]), sb("wk", [P, KC, H * DK])
        w_v, w_a = sb("wv", [P, KC, H * DV]), sb("wa", [P, KC, H * DV])
        b_a = sb("ba", [P, H])
        c_w = sb("cw", [P, NCONV, TAPS])
        c_b = sb("cb", [P, NCONV])
        xn_w = sb("xn_w", [P, 2, KC, TW])
        bt, btk = sb("bt", [P, 2, NC_, WT]), sb("btk", [P, NC_, WT])
        Kw, Kb, Qw = (sb(n, [P, 2, NC_, WT]) for n in ("K", "Kb", "Q"))
        Vw, Aw = (sb(n, [P, 2, 2, NC_, WT]) for n in ("V", "A"))
        raw = sb("raw", [P, SLOTS, B, TAPS - 1 + WT])
        conv = sb("conv", [P, SLOTS, B, WT])
        halo = sb("halo", [P, NCONV, B, TAPS - 1])
        prod = sb("prod", [P, 2, NC_, NPR])
        bd_qk = sb("bd_qk", [P, NC_, 2, 2, CT])
        bd_k = sb("bd_k", [P, NC_, 2, CT])
        k_rows = sb("k_rows", [P, NG, P])
        gram = sb("gram", [P, 2, NC_, CT])
        cross = sb("cross", [P, NSUB - 1, 2, 2, NC_, ST])
        dec = sb("dec", [P, 2, NC_, NSUB, ST + 1])
        dec_c = sb("dec_c", [P, 2, NC_, CT + 1])
        c_exp = sb("c_exp", [P, NC_ // 4, 2, DK])
        S = sb("S", [P, NC_, DV])
        W = sb("W", [P, NC_, 2, CT])
        w_rows = sb("w_rows", [P, NG, P])
        Wh = sb("Wh", [P, 2, NC_, 5])
        TB = sb("TB", [P, 2, NC_, ST, ST])
        QB = sb("QB", [P, 2, NC_, ST, ST + 1])
        xs_tmp = sb("xs_tmp", [P, 2, NC_, CT])
        tmp = xs_tmp[:, :, :, 0:ST]
        O = sb("O", [P, 2, NC_, WT])

        gq_ps = ctx.enter_context(nc.psum_tensor("r_gq_ps", [P, 2, NC_, NPR], F32))
        bank = [ctx.enter_context(nc.psum_tensor(f"r_bank{i}", [P, 512], F32)) for i in range(6)]
        X_PS, T_PS, P_PS, M_PS = bank[0], (bank[1], bank[2]), (bank[3], bank[4]), bank[5]
        XS_PS = (X_PS, M_PS, T_PS[0], T_PS[1])
        CR_PS = (M_PS, T_PS[0], T_PS[1])

        loaded = sem("loaded")
        zeroed = sem("zeroed")
        proj_done, gq_done, turned_w, x_done = sem("proj_done"), sem("gq_done"), sem("turned_w"), sem("x_done")
        upd_done, xs_done, cr_done, gram_done, kt_done = (sem(n) for n in
                                                          ("upd_done", "xs_done", "cr_done", "gram_done", "kt_done"))
        w_ready, gq_used, xk_used, s_added, xs_used, cr_used, conv_done, o_ready = (sem(n) for n in (
            "w_ready", "gq_used", "xk_used", "s_added", "xs_used", "cr_used", "conv_done", "o_ready"))
        proj_used, raw_ready, act_done, w_copied, kt_copied, gram_copied, bd_ready, c_ready = (sem(n) for n in (
            "proj_used", "raw_ready", "act_done", "w_copied", "kt_copied", "gram_copied", "bd_ready", "c_ready"))
        prod_ready, kb_ready, v_ready, cross_ready, dec_ready = (sem(n) for n in (
            "prod_ready", "kb_ready", "v_ready", "cross_ready", "dec_ready"))
        xn_in = [sem("xn_in0"), sem("xn_in1")]
        bt_in, o_out = sem("bt_in"), sem("o_out")
        own_sem = {e: sem("own_" + e) for e in ("act", "dve", "pool")}

        class At:

            def __init__(self, it, q):
                self.it, self.q = it, q
                self.m = q % MCH
                self.par = (q // MCH) % 2
                self.t0 = self.m * CT

            def n(self, per, k, back=0):
                return self.it * (2 * MCH * per) + ((self.q + 1 - back) * per + k)

            def w(self, per, k, back=0):
                return self.it * (2 * per) + ((self.q // MCH + 1 - back) * per + k)

            def next(self):
                return At(self.it, self.q + 1)

        def init(*engine_sems):
            for e, s, per in engine_sems:
                e.sem_inc(s, per)

        with nc.Block() as block:
            @block.sync
            def _(sp):
                for dst, src in ((w_q, wq), (w_k, wk), (w_v, wv), (w_a, wa)):
                    sp.dma_start(dst[:, :, :], src.rearrange("(k p) n -> p k n", p=P)).then_inc(loaded, 16)
                sp.dma_start(id_sb[:, :], ident).then_inc(loaded, 16)
                sp.dma_start(rmask[:, :, :, :], row_mask).then_inc(loaded, 16)
                sp.dma_start(b_a[:, :], ba).then_inc(loaded, 16)
                sp.dma_start(c_w[:, 0:2 * HP, :], cw_qk).then_inc(loaded, 16)
                sp.dma_start(c_w[:, 2 * HP:, :], cw_v).then_inc(loaded, 16)
                sp.dma_start(c_b[:, 0:2 * HP], cb_qk).then_inc(loaded, 16)
                sp.dma_start(c_b[:, 2 * HP:], cb_v).then_inc(loaded, 16)
                for w in range(2):
                    sp.dma_start(xn_w[:, w, :, :], xn_d[w].rearrange("p k b t -> p k (b t)")).then_inc(xn_in[w], 16)
                for hh in range(2):
                    sp.dma_start(btk[64 * hh:64 * hh + 64, :, :].rearrange("p c t -> p (c t)"),
                                 betak_d[0, hh:hh + 1].rearrange("h j b t -> h (j b t)").to_broadcast([DK, NC_ * WT]))\
                        .then_inc(bt_in, 16)
                sp.dma_start(bt[:, :, :, :].rearrange("p h c t -> p (h c t)"),
                             beta_d[0:1].rearrange("w h j b t -> w (h j b t)").to_broadcast([P, 2 * NC_ * WT]))\
                    .then_inc(bt_in, 16)
                sp.wait_ge(loaded, 11 * 16)
                sp.sem_inc(o_out, 16)

            @block.gpsimd
            def _(pool):
                for t in (S, W, k_rows):
                    pool.memset(t[:, :, :] if t is not W else W[:, :, :, :], 0.0)
                pool.memset(bd_k[:, :, :, :], 0.0)
                pool.memset(dec[:, :, :, :, :], 1.0)
                pool.memset(dec_c[:, :, :, :], 1.0).then_inc(zeroed, 1)
                init((pool, prod_ready, 4), (pool, kb_ready, 1), (pool, v_ready, 1), (pool, cross_ready, 1),
                     (pool, dec_ready, 1))

            @block.vector
            def _(dve):
                dve.memset(ones[:, :], 1.0)
                dve.memset(halo[:, :, :, :], 0.0)
                dve.memset(bd_qk[:, :, :, :, :], 0.0).then_inc(zeroed, 1)
                init((dve, w_ready, 4), (dve, gq_used, 4), (dve, xk_used, 3), (dve, s_added, 8), (dve, xs_used, 4),
                     (dve, cr_used, 8), (dve, conv_done, NCONV), (dve, o_ready, 1))

            @block.scalar
            def _(act):
                init((act, proj_used, NT), (act, raw_ready, NCONV), (act, act_done, NCONV), (act, w_copied, 8),
                     (act, kt_copied, 2), (act, gram_copied, 2), (act, bd_ready, 1), (act, c_ready, 4))

            @block.tensor
            def _(pe):
                init((pe, proj_done, NT), (pe, gq_done, 4), (pe, turned_w, 8), (pe, x_done, 3), (pe, upd_done, 8),
                     (pe, xs_done, 4), (pe, cr_done, 8), (pe, gram_done, 2), (pe, kt_done, 2))

        def pe_project(pe, at, i0, i1):
            par = at.par
            for i in range(i0, i1):
                kind, n = TILES[i]
                w_sb = {"q": w_q, "k": w_k, "v": w_v, "a": w_a}[kind]
                if i == 0:
                    pe.wait_ge(xn_in[par], (at.it + at.q // (2 * MCH)) * 16 + 16)
                pe.wait_ge(proj_used, at.w(NT, i - 1))
                for k in range(KC):
                    mm = pe.matmul(P_PS[i % 2][:, 0:TW], w_sb[:, k, n * P:(n + 1) * P], xn_w[:, par, k, :],
                                   start=(k == 0), stop=(k == KC - 1))
                mm.then_inc(proj_done, 1)

        def pe_gq(pe, at, j):
            pe.wait_ge(prod_ready, at.n(4, j + 1))
            pe.wait_ge(gq_used, at.n(4, j))
            for hh in range(2):
                mm = pe.matmul(gq_ps[:, hh, :, :].rearrange("p c n -> p (c n)"), ones[64 * hh:64 * hh + 64, :],
                               prod[64 * hh:64 * hh + 64, j % 2, :, :].rearrange("p c n -> p (c n)"),
                               start=True, stop=True)
            mm.then_inc(gq_done, 1)

        def pe_turn_w(pe, at, j):
            pe.wait_ge(w_ready, at.n(4, j + 1))
            for half in range(2):
                if j == 0:
                    pe.wait_ge(cr_used, at.n(8, 8))
                else:
                    pe.wait_ge(w_copied, at.n(8, 2 * (j - 1) + half + 1))
                for i in range(4):
                    g = 4 * half + i
                    mm = pe.transpose(T_PS[half][:, i * P:(i + 1) * P],
                                      W[:, 4 * g:4 * g + 4, :, :].rearrange("p c h s -> p (c h s)"), id_sb[:, :])
                mm.then_inc(turned_w, 1)

        def pe_cross(pe, at, j):
            if j == 1:
                pe.wait_ge(cross_ready, at.n(1, 1))
                pe.wait_ge(xs_used, at.n(4, 1))
            else:
                pe.wait_ge(xk_used, at.n(3, j - 1))
            for g in range(NG):
                if g % 4 == 0:
                    pe.wait_ge(w_copied, at.n(8, 2 * (j - 1) + g // 4 + 1))
                mm = pe.matmul(X_PS[:, :].rearrange("p (z n) -> p z n", z=4)[:, :, g * 16:(g + 1) * 16],
                               w_rows[:, g, :],
                               cross[:, j - 1, :, :, 4 * g:4 * g + 4, :].rearrange("p k h c t -> p (k h) (c t)"),
                               start=True, stop=True)
            mm.then_inc(x_done, 1)

        def pe_state_read(pe, at, r):
            if r == 0:
                pe.wait_ge(bd_ready, at.n(1, 1))
                pe.wait_ge(s_added, at.n(8, 4, back=1))
                pe.wait_ge(xk_used, at.n(3, 3, back=1))
            elif r == 1:
                pe.wait_ge(gram_copied, at.n(2, 2))
            else:
                pe.wait_ge(s_added, at.n(8, 8, back=1))
            for i in range(8):
                c = 8 * r + i
                mm = pe.matmul(XS_PS[r][:, i * 64:(i + 1) * 64], S[:, c, :],
                               bd_qk[:, c, :, :, :].rearrange("p h k t -> p (h k t)"), start=True, stop=True)
            mm.then_inc(xs_done, 1)

        def pe_decay(pe, at, r):
            pe.wait_ge(c_ready, at.n(4, r // 2 + 1))
            if r == 0:
                pe.wait_ge(kt_copied, at.n(2, 2, back=1))
                pe.wait_ge(xs_used, at.n(4, 2))
            elif r < 3:
                pe.wait_ge(xs_used, at.n(4, r + 2))
            else:
                pe.wait_ge(cr_used, at.n(8, r - 2))
            for i in range(4):
                mm = pe.transpose(CR_PS[r % 3][:, i * P:(i + 1) * P],
                                  c_exp[:, 4 * (r % 2) + i, :, :].rearrange("p h k -> p (h k)"), id_sb[:, :])
            mm.then_inc(cr_done, 1)

        def pe_k_rows(pe, at, half):
            if half == 0:
                pe.wait_ge(cr_used, at.n(8, 7))
            else:
                pe.wait_ge(kt_copied, at.n(2, 1))
            for i in range(4):
                g = 4 * half + i
                mm = pe.transpose(M_PS[:, i * P:(i + 1) * P],
                                  bd_k[:, 4 * g:4 * g + 4, :, :].rearrange("p c h s -> p (c h s)"), id_sb[:, :])
            mm.then_inc(kt_done, 1)

        def pe_gram(pe, at, half, first=False):
            if half == 0:
                pe.wait_ge(bd_ready, at.n(1, 1))
                if not first:
                    pe.wait_ge(kt_copied, at.n(2, 2, back=1))
            else:
                pe.wait_ge(gram_copied, at.n(2, 1))
            for kind, src in enumerate((Kb, Qw)):
                for i in range(4):
                    g = 4 * half + i
                    mm = pe.matmul(M_PS[:, kind * 256 + i * 64:kind * 256 + (i + 1) * 64],
                                   bd_k[:, 4 * g:4 * g + 4, :, :].rearrange("p c h s -> p (c h s)"),
                                   src[:, at.par, 4 * g:4 * g + 4, at.t0:at.t0 + CT], start=True, stop=True)
            mm.then_inc(gram_done, 1)

        def pe_update(pe, at, f):
            b4, half = f % 4, f // 4
            if f < 2:
                pe.wait_ge(w_copied, at.n(8, 8))
            else:
                pe.wait_ge(s_added, at.n(8, f - 1))
            for i in range(4):
                g = 4 * half + i
                mm = pe.matmul(T_PS[f % 2][:, i * P:(i + 1) * P], k_rows[32 * b4:32 * b4 + 32, g, :],
                               w_rows[32 * b4:32 * b4 + 32, g, :], start=True, stop=True)
            mm.then_inc(upd_done, 1)

        def pe_chunk(pe, at):
            nxt, nwin = at.next(), At(at.it, (at.q // MCH + 1) * MCH)
            tiles = [(FIRST[4 * at.m + j], FIRST[4 * at.m + j + 1]) for j in range(4)]
            for r in range(8):
                pe_decay(pe, at, r)
                if r in (2, 5):
                    a = tiles[0][0] + (r // 3)
                    pe_project(pe, nwin, a, a + 1)
            for j in range(4):
                a, b_ = tiles[j]
                if j == 0:
                    a += 2
                mid = min(a + 1, b_)
                pe_project(pe, nwin, a, mid)
                if j < 2:
                    pe_k_rows(pe, at, j)
                if j == 3:
                    pe_gram(pe, nxt, 0)
                pe_turn_w(pe, at, j)
                if j < 3:
                    pe_gq(pe, at, j + 1)
                    pe_cross(pe, at, j + 1)
                    pe_project(pe, nwin, mid, b_)
            pe_gram(pe, nxt, 1)
            for f in range(8):
                pe_update(pe, at, f)
                if f == 5:
                    pe_gq(pe, nxt, 0)
                if f == 6:
                    pe_state_read(pe, nxt, 0)
            pe_project(pe, nwin, tiles[3][0] + min(1, tiles[3][1] - tiles[3][0]), tiles[3][1])
            for r in range(1, 4):
                pe_state_read(pe, nxt, r)

        def act_project(act, own, at, i0, i1):
            par = at.par
            for i in range(i0, i1):
                kind, n = TILES[i]
                act.wait_ge(proj_done, at.w(NT, i + 1))
                ps = P_PS[i % 2][:, 0:TW].rearrange("p (b t) -> p b t", b=B)
                if kind == "a":
                    j, hh = n // 2, n % 2
                    act.wait_ge(dec_ready, at.n(1, 0))
                    nc.scalar.activation(Aw[:, par, hh, j * B:(j + 1) * B, :], ps, ACT.Sigmoid,
                                         bias=b_a[:, n:n + 1]).then_inc(proj_used, 1)
                    continue
                s = i % SLOTS
                if i >= SLOTS:
                    act.wait_ge(conv_done, at.w(NCONV, i - SLOTS + 1))
                else:
                    act.wait_ge(conv_done, at.w(NCONV, NCONV - SLOTS + i + 1, back=1))
                own.run(nc.scalar.activation(raw[:, s, :, TAPS - 1:], ps, ACT.Copy))
                own.run(nc.scalar.activation(raw[:, s, :, 0:TAPS - 1], halo[:, i, :, :], ACT.Copy))
                nc.scalar.activation(conv[:, s, :, :], ps, ACT.Identity, bias=c_b[:, i:i + 1],
                                     scale=c_w[:, i, TAPS - 1:TAPS]).then_inc(proj_used, 1)
                nc.scalar.activation(halo[:, i, :, :], raw[:, s, :, WT:], ACT.Copy).then_inc(raw_ready, 1)

        def act_silu(act, at, i0, i1):
            par = at.par
            for i in range(i0, min(i1, NCONV)):
                kind, n = TILES[i]
                act.wait_ge(conv_done, at.w(NCONV, i + 1))
                if kind == "v":
                    dst = Vw[:, par, n % 2, n // 2 * B:(n // 2 + 1) * B, :]
                else:
                    dst = (Qw if kind == "q" else Kw)[:, par, n * B:(n + 1) * B, :]
                nc.scalar.activation(dst, conv[:, i % SLOTS, :, :], ACT.Silu).then_inc(act_done, 1)

        def act_w(act, at, j):
            for half in range(2):
                act.wait_ge(turned_w, at.n(8, 2 * j + half + 1))
                nc.scalar.activation(w_rows[:, 4 * half:4 * half + 4, :],
                                     T_PS[half][:, :].rearrange("p (g n) -> p g n", g=4), ACT.Copy)\
                    .then_inc(w_copied, 1)

        def act_k_rows(act, at, half):
            act.wait_ge(kt_done, at.n(2, half + 1))
            nc.scalar.activation(k_rows[:, 4 * half:4 * half + 4, :],
                                 M_PS[:, :].rearrange("p (g n) -> p g n", g=4), ACT.Copy).then_inc(kt_copied, 1)

        def act_gram(act, at, half):
            act.wait_ge(gram_done, at.n(2, half + 1))
            act.wait_ge(cross_ready, at.n(1, 0))
            nc.scalar.activation(gram[:, :, 16 * half:16 * half + 16, :].rearrange("p k c t -> p k (c t)"),
                                 M_PS[:, :].rearrange("p (k n) -> p k n", k=2), ACT.Copy).then_inc(gram_copied, 1)

        def act_block_diag(act, own, at, first=False):
            par, t0 = at.par, at.t0
            act.wait_ge(kb_ready, at.w(1, 1))
            if not first:
                act.wait_ge(xs_done, at.n(4, 4, back=1))
                act.wait_ge(kt_done, at.n(2, 2, back=1))
            for hh in range(2):
                rows = slice(64 * hh, 64 * hh + 64)
                own.run(nc.scalar.activation(bd_qk[rows, :, hh, 0, :], Kb[rows, par, :, t0:t0 + CT], ACT.Copy))
                own.run(nc.scalar.activation(bd_qk[rows, :, hh, 1, :], Qw[rows, par, :, t0:t0 + CT], ACT.Copy))
                ins = nc.scalar.activation(bd_k[rows, :, hh, :], Kw[rows, par, :, t0:t0 + CT], ACT.Copy)
                own.run(ins) if hh == 0 else ins.then_inc(bd_ready, 1)

        def act_expand(act, at, r):
            if r == 0:
                act.wait_ge(dec_ready, at.n(1, 1))
                act.wait_ge(cr_done, at.n(8, 8, back=1))
            else:
                act.wait_ge(cr_done, at.n(8, 2 * r))
            src = dec_c[:, :, 8 * r:8 * r + 8, CT:CT + 1].rearrange("p h c o -> p c h o")
            nc.scalar.activation(c_exp[:, :, :, :], src.to_broadcast([P, 8, 2, DK]), ACT.Copy).then_inc(c_ready, 1)

        def act_chunk(act, own, at):
            nxt, nwin = at.next(), At(at.it, (at.q // MCH + 1) * MCH)
            f = [FIRST[4 * at.m + j] for j in range(5)]
            prev = FIRST[4 * at.m - 1] if at.m else 0
            own.restart()
            for r in range(1, 4):
                act_expand(act, at, r)
            if at.m:
                act_silu(act, nwin, prev, f[0])
            for j in range(4):
                if j:
                    act_silu(act, nwin, f[j - 1], f[j])
                a, b_ = f[j], f[j + 1]
                mid = min(a + (3 if j == 0 else 1), b_)
                act_project(act, own, nwin, a, mid)
                if j < 2:
                    act_k_rows(act, at, j)
                if j == 3:
                    act_gram(act, nxt, 0)
                act_w(act, at, j)
                if j < 3:
                    act_project(act, own, nwin, mid, b_)
                if j == 2:
                    act_block_diag(act, own, nxt)
            act_gram(act, nxt, 1)
            act_project(act, own, nwin, mid, b_)
            act_expand(act, nxt, 0)

        def pool_products(pool, own, at, j, first=False):
            par, t0, z = at.par, at.t0 + j * ST, j % 2
            if j == 0 and not first:
                pool.wait_ge(gq_done, at.n(4, -1))
            elif j >= 2:
                pool.wait_ge(gq_done, at.n(4, j - 1))
            elif j == 1 and not first:
                pool.wait_ge(gq_done, at.n(4, 0))
            for t in range(ST):
                ins = pool.tensor_tensor(prod[:, z, :, QO[t]:QO[t] + t + 1],
                                         Qw[:, par, :, t0 + t:t0 + t + 1].to_broadcast([P, NC_, t + 1]),
                                         Kw[:, par, :, t0:t0 + t + 1], ALU.mult)
                if t == 0:
                    own.run(ins)
                    continue
                own.run(ins)
                ins = pool.tensor_tensor(prod[:, z, :, GO[t]:GO[t] + t],
                                         Kb[:, par, :, t0 + t:t0 + t + 1].to_broadcast([P, NC_, t]),
                                         Kw[:, par, :, t0:t0 + t], ALU.mult)
                own.run(ins) if t < ST - 1 else ins.then_inc(prod_ready, 1)

        def pool_cross(pool, own, at, first=False):
            pool.wait_ge(gram_copied, at.n(2, 2))
            if not first:
                pool.wait_ge(x_done, at.n(3, 3, back=1))
            for j in range(1, NSUB):
                for kind in range(2):
                    for hh in range(2):
                        src = gram[:, kind, :, j * ST:(j + 1) * ST].rearrange("p (g b) t -> p g b t", b=4)
                        mask = rmask[:, j - 1, hh, :].rearrange("p (o b q) -> p o b q", o=1, q=1)
                        ins = pool.tensor_tensor(cross[:, j - 1, kind, hh, :, :].rearrange("p (g b) t -> p g b t", b=4),
                                                 src, mask.to_broadcast([P, NG, 4, ST]), ALU.mult)
                        last = (j, kind, hh) == (NSUB - 1, 1, 1)
                        ins.then_inc(cross_ready, 1) if last else own.run(ins)

        def pool_decays(pool, own, at, first=False):
            par, t0 = at.par, at.t0
            pool.wait_ge(proj_used, at.w(NT, NT))
            if not first:
                pool.wait_ge(w_ready, at.n(4, 4, back=1))
                pool.wait_ge(xk_used, at.n(3, 3, back=1))
                pool.wait_ge(c_ready, at.n(4, 4, back=1))
            for hh in range(2):
                a = Aw[:, par, hh, :, t0:t0 + CT].rearrange("p c (j t) -> p c j t", t=ST)
                for t in range(ST):
                    own.run(pool.tensor_tensor(dec[:, hh, :, :, t + 1], dec[:, hh, :, :, t], a[:, :, :, t], ALU.mult))
            dc = dec_c[:, :, :, :].rearrange("p h c n -> p (h c) n")
            ds = dec[:, :, :, :, :].rearrange("p h c j n -> p (h c) j n")
            for j in range(NSUB):
                ins = pool.tensor_tensor(dc[:, :, j * ST + 1:(j + 1) * ST + 1], ds[:, :, j, 1:],
                                         dc[:, :, j * ST:j * ST + 1].to_broadcast([P, 2 * NC_, ST]), ALU.mult)
                own.run(ins) if j < NSUB - 1 else ins.then_inc(dec_ready, 1)

        def pool_beta_k(pool, own, at):
            pool.wait_ge(bt_in, at.w(48, 0))
            pool.wait_ge(act_done, at.w(NCONV, 2 * HP))
            pool.tensor_tensor(Kb[:, at.par, :, :], Kw[:, at.par, :, :], btk[:, :, :], ALU.mult).then_inc(kb_ready, 1)
            pool.wait_ge(kb_ready, at.w(1, 1))

        def pool_beta_v(pool, own, at):
            pool.wait_ge(act_done, at.w(NCONV, NCONV))
            v = Vw[:, at.par, :, :, :].rearrange("p h c t -> p (h c t)")
            pool.tensor_tensor(v, v, bt[:, :, :, :].rearrange("p h c t -> p (h c t)"), ALU.mult).then_inc(v_ready, 1)

        def pool_chunk(pool, own, at):
            nxt, nwin = at.next(), At(at.it, (at.q // MCH + 1) * MCH)
            own.restart()
            for j in range(1, 4):
                pool_products(pool, own, at, j)
                if at.m == 1 and j == 3:
                    pool_beta_v(pool, own, nwin)
            if at.m == 0:
                pool_beta_k(pool, own, nwin)
            pool_products(pool, own, nxt, 0)
            pool_cross(pool, own, nxt)
            pool_decays(pool, own, nxt)

        def dve_conv(dve, own, at, i0, i1):
            for i in range(i0, min(i1, NCONV)):
                s = i % SLOTS
                dve.wait_ge(raw_ready, at.w(NCONV, i + 1))
                for tap in (2, 1, 0):
                    ins = dve.scalar_tensor_tensor(out=conv[:, s, :, :], in0=raw[:, s, :, tap:tap + WT],
                                                   scalar=c_w[:, i, tap:tap + 1], in1=conv[:, s, :, :],
                                                   op0=ALU.mult, op1=ALU.add)
                    own.run(ins) if tap else ins.then_inc(conv_done, 1)

        def w_view(s0, s1):
            return W[:, :, :, s0:s1].rearrange("p c h s -> p h c s")

        def dve_start(dve, own, at):
            par, t0 = at.par, at.t0
            dve.wait_ge(dec_ready, at.n(1, 1))
            if at.m == 0:
                dve.wait_ge(v_ready, at.w(1, 1))
                dve.wait_ge(o_out, at.w(16, 0))
            for r in range(4):
                dve.wait_ge(xs_done, at.n(4, r + 1))
                ps = XS_PS[r][:, :].rearrange("p (c h k t) -> p h c k t", c=8, h=2, k=2)
                cs = slice(8 * r, 8 * r + 8)
                own.run(dve.tensor_tensor(xs_tmp[:, :, cs, :], ps[:, :, :, 0, :], dec_c[:, :, cs, 0:CT], ALU.mult))
                dve.tensor_tensor(O[:, :, cs, t0:t0 + CT], ps[:, :, :, 1, :], dec_c[:, :, cs, 1:], ALU.mult)\
                    .then_inc(xs_used, 1)
            v = Vw[:, par, :, :, t0:t0 + CT]
            own.run(dve.tensor_tensor(v, v, xs_tmp[:, :, :, :], ALU.add))
            for r in range(8):
                dve.wait_ge(cr_done, at.n(8, r + 1))
                s = S[:, 4 * r:4 * r + 4, :]
                dve.tensor_tensor(s, s, CR_PS[r % 3][:, :].rearrange("p (c v) -> p c v", c=4), ALU.mult)\
                    .then_inc(cr_used, 1)

        def dve_sub(dve, own, at, j):
            par, t0 = at.par, at.t0 + j * ST
            v = Vw[:, par, :, :, t0:t0 + ST]
            x = X_PS[:, :].rearrange("p (k h c t) -> p k h c t", k=2, h=2, t=ST)
            if j == 0:
                own.run(dve.tensor_copy(TB[:, :, :, :, ST - 1], v))
            else:
                dve.wait_ge(x_done, at.n(3, j))
                own.run(dve.tensor_tensor(tmp, x[:, 0], dec[:, :, :, j, 0:ST], ALU.mult))
                own.run(dve.tensor_tensor(TB[:, :, :, :, ST - 1], v, tmp, ALU.add))
                dve.tensor_tensor(QB[:, :, :, :, ST], x[:, 1], dec[:, :, :, j, 1:], ALU.mult).then_inc(xk_used, 1)
                w = w_view(0, j * ST)
                own.run(dve.tensor_tensor(w, w, dec[:, :, :, j, ST:ST + 1].to_broadcast([P, 2, NC_, j * ST]), ALU.mult))
            a = Aw[:, par, :, :, t0:t0 + ST]
            dve.wait_ge(gq_done, at.n(4, j + 1))
            rows = [TB[:, :, :, 0, ST - 1:ST], Wh[:, :, :, 0:2], Wh[:, :, :, 2:5], w_view(j * ST, (j + 1) * ST)]
            for t in range(1, ST):
                old = rows[t - 1]
                own.run(dve.tensor_tensor(TB[:, :, :, t, ST - 1 - t:ST - 1], gq_ps[:, :, :, GO[t]:GO[t] + t], old, ALU.mult))
                own.run(dve.tensor_tensor(rows[t][:, :, :, 0:t], old, a[:, :, :, t:t + 1].to_broadcast([P, 2, NC_, t]),
                                          ALU.mult))
                ins = dve.tensor_reduce(rows[t][:, :, :, t], TB[:, :, :, t, ST - 1 - t:], AX.X, ALU.add)
                if t < ST - 1:
                    own.run(ins)
                else:
                    ins.then_inc(w_ready, 1)
                    dve.wait_ge(w_ready, at.n(4, j + 1))
            for t in range(ST):
                ins = dve.tensor_tensor(QB[:, :, :, t, ST - 1 - t:ST], gq_ps[:, :, :, QO[t]:QO[t] + t + 1], rows[t], ALU.mult)
                if t < ST - 1:
                    own.run(ins)
                else:
                    ins.then_inc(gq_used, 1)
                    dve.wait_ge(gq_used, at.n(4, j + 1))
            o = O[:, :, :, t0:t0 + ST]
            if j == 0:
                own.run(dve.tensor_copy(QB[:, :, :, :, ST], o))
            else:
                own.run(dve.tensor_tensor(QB[:, :, :, :, ST], QB[:, :, :, :, ST], o, ALU.add))
            for t in range(ST):
                ins = dve.tensor_reduce(o[:, :, :, t], QB[:, :, :, t, ST - 1 - t:], AX.X, ALU.add)
                ins.then_inc(o_ready, 1) if (j, t) == (NSUB - 1, ST - 1) else own.run(ins)

        def dve_add(dve, own, at, f):
            b4, half = f % 4, f // 4
            dve.wait_ge(upd_done, at.n(8, f + 1))
            s = S[:, 16 * half:16 * half + 16, :].rearrange("p (g b) v -> p g b v", b=4)[:, :, b4, :]
            dve.tensor_tensor(s, s, T_PS[f % 2][:, :].rearrange("p (g v) -> p g v", g=4), ALU.add).then_inc(s_added, 1)

        def dve_chunk(dve, own, at):
            nwin = At(at.it, (at.q // MCH + 1) * MCH)
            own.restart()
            dve_start(dve, own, at)
            for j in range(4):
                dve_sub(dve, own, at, j)
                if j < 3:
                    dve_conv(dve, own, nwin, FIRST[4 * at.m + j], FIRST[4 * at.m + j + 1])
            dve.wait_ge(cr_used, at.n(8, 8))
            for f in range(8):
                dve_add(dve, own, at, f)
            dve.wait_ge(s_added, at.n(8, 8))
            dve_conv(dve, own, nwin, FIRST[4 * at.m + 3], FIRST[4 * at.m + 4])

        FILL = At(0, 0)
        clear_after(nc, ctx, sems)
        with nc.Block() as block:
            @block.sync
            def _(sp):
                with sp.Fori(0, NW // 2) as it:
                    for wq_ in range(2):
                        at = At(it, wq_ * MCH)
                        sp.wait_ge(proj_done, at.w(NT, NT))
                        sp.dma_start(xn_w[:, wq_, :, :].rearrange("p k n -> p (k n)"),
                                     xn_d[bass.ds(it * 2 + (wq_ + 2), 1)].rearrange("o p k b t -> (o p) (k b t)"))\
                            .then_inc(xn_in[wq_], 16)
                        sp.wait_ge(v_ready, at.w(1, 1))
                        sp.wait_ge(kb_ready, at.w(1, 1))
                        for hh in range(2):
                            sp.dma_start(btk[64 * hh:64 * hh + 64, :, :].rearrange("p c t -> p (c t)"),
                                         betak_d[bass.ds(it * 2 + (wq_ + 1), 1), hh].rearrange("o j b t -> o (j b t)")
                                         .to_broadcast([DK, NC_ * WT])).then_inc(bt_in, 16)
                        sp.dma_start(bt[:, :, :, :].rearrange("p h c t -> p (h c t)"),
                                     beta_d[bass.ds(it * 2 + (wq_ + 1), 1)].rearrange("o h j b t -> o (h j b t)")
                                     .to_broadcast([P, 2 * NC_ * WT])).then_inc(bt_in, 16)
                        sp.wait_ge(o_ready, At(it, wq_ * MCH + 1).n(1, 1))
                        sp.dma_start(o_d[bass.ds(it * 2 + wq_, 1)].rearrange("o p h c t -> (o p) (h c t)"),
                                     O[:, :, :, :].rearrange("p h c t -> p (h c t)")).then_inc(o_out, 16)
                sp.wait_ge(o_out, 16 * (NW + 1))
                for s in xn_in:
                    sp.wait_ge(s, 16 * (NW // 2 + 1))
                sp.wait_ge(bt_in, 48 * (NW + 1))

            @block.tensor
            def _(pe):
                pe_project(pe, FILL, 0, NT)
                pe_gram(pe, FILL, 0, first=True)
                pe_gram(pe, FILL, 1)
                pe_gq(pe, FILL, 0)
                for r in range(4):
                    pe_state_read(pe, FILL, r)
                with pe.Fori(0, NW // 2) as it:
                    for q in range(2 * MCH):
                        pe_chunk(pe, At(it, q))

            @block.scalar
            def _(act):
                own = Chain(act, own_sem["act"])
                for i in range(0, NT, 4):
                    act_project(act, own, FILL, i, i + 4)
                    act_silu(act, FILL, i, i + 4)
                act_block_diag(act, own, FILL, first=True)
                act_gram(act, FILL, 0)
                act_gram(act, FILL, 1)
                act_expand(act, FILL, 0)
                own.restart()
                with act.Fori(0, NW // 2) as it:
                    for q in range(2 * MCH):
                        act_chunk(act, own, At(it, q))

            @block.gpsimd
            def _(pool):
                own = Chain(pool, own_sem["pool"])
                pool_beta_k(pool, own, FILL)
                pool_products(pool, own, FILL, 0, first=True)
                pool_beta_v(pool, own, FILL)
                pool_cross(pool, own, FILL, first=True)
                pool_decays(pool, own, FILL, first=True)
                own.restart()
                with pool.Fori(0, NW // 2) as it:
                    for q in range(2 * MCH):
                        pool_chunk(pool, own, At(it, q))

            @block.vector
            def _(dve):
                own = Chain(dve, own_sem["dve"])
                dve_conv(dve, own, FILL, 0, NCONV)
                own.restart()
                with dve.Fori(0, NW // 2) as it:
                    for q in range(2 * MCH):
                        dve_chunk(dve, own, At(it, q))


def gate_and_project(nc, wg, wo, ln_w, ln_b, w_centre, xn_d, xr_d, o_d, x2_d, xf_d):
    HG = H // 2
    with ExitStack() as ctx:
        def sb(name, shape, dt=F32):
            return ctx.enter_context(nc.sbuf_tensor("g_" + name, shape, dt))

        sems = []

        def sem(name):
            sems.append(ctx.enter_context(nc.semaphore("g_" + name)))
            return sems[-1]

        w_g, w_o = sb("wg", [P, KC, H * DV]), sb("wo", [P, H, C])
        w_cen, mean_v, mean_c = sb("w_cen", [P, P]), sb("mean_v", [P, P]), sb("mean_c", [P, P])
        lw, lb, eps = sb("lw", [P, 1]), sb("lb", [P, 1]), sb("eps", [P, 1])
        o_in = sb("o_in", [P, 2, HG, 2 * TW])
        xn_in = sb("xn_in", [P, 2, KC, TW])
        xr_in = sb("xr_in", [P, 2, KC, TW])
        sq, std, rstd = sb("sq", [P, HG, 2 * TW]), sb("std", [P, HG, 2 * TW]), sb("rstd", [P, 2 * TW])
        dn, z, sg = sb("dn", [P, HG, 2 * TW]), sb("z", [P, 2, 2 * TW]), sb("sg", [P, 2, 2 * TW])
        og = sb("og", [P, 2, HG, 2 * TW])
        x2, xf = sb("x2", [P, 2, KC, TW]), sb("xf", [P, 2, KC, TW])
        cenx, sqx = sb("cenx", [P, KC, TW]), sb("sqx", [P, KC, TW])
        stdx, rstdx = sb("stdx", [P, TW]), sb("rstdx", [P, TW])
        ps = [ctx.enter_context(nc.psum_tensor(f"g_ps{i}", [P, 512], F32)) for i in range(8)]
        C_PS, V_PS, M_PS, G_PS, Y_PS = ps[0:4], ps[4], ps[5], ps[6], ps[7]

        names = ("loaded", "consts", "cen_done", "sq_done", "var_done", "std_done", "dn_done", "gate_done", "sg_done",
                 "z_done", "og_done", "y_done", "x2_done", "mean_done", "cenx_done", "sqx_done", "varx_done",
                 "stdx_done", "xf_done", "own_act", "own_dve")
        (loaded, consts, cen_done, sq_done, var_done, std_done, dn_done, gate_done, sg_done, z_done, og_done, y_done,
         x2_done, mean_done, cenx_done, sqx_done, varx_done, stdx_done, xf_done, own_act, own_dve) = map(sem, names)
        front_in = [sem("front_in0"), sem("front_in1")]
        back_in = [sem("back_in0"), sem("back_in1")]
        stored = [sem("stored0"), sem("stored1")]

        class At:

            def __init__(self, it, q):
                self.it, self.q, self.u = it, q, q % 2

            def n(self, per, k, back=0):
                return self.it * (2 * per) + ((self.q + 1 - back) * per + k)

            def d(self, per, back=0):
                return (self.it + (self.q // 2 + 1 - back)) * per

        def window(d, at):
            return d[bass.ds(at.it * 2 + at.q, 1)]

        def sp_front(sp, at, first=False):
            if not first:
                sp.wait_ge(gate_done, at.n(HG, 0, back=1))
            sp.dma_start(o_in[:, at.u, :, :].rearrange("p g n -> p (g n)"),
                         window(o_d, at).rearrange("o p h c t -> (o p) (h c t)")).then_inc(front_in[at.u], 16)
            sp.dma_start(xn_in[:, at.u, :, :].rearrange("p k n -> p (k n)"),
                         window(xn_d, at).rearrange("o p k b t -> (o p) (k b t)")).then_inc(front_in[at.u], 16)

        def sp_back(sp, at, first=False):
            if not first:
                sp.wait_ge(x2_done, at.n(1, 0, back=1))
            sp.dma_start(xr_in[:, at.u, :, :].rearrange("p k n -> p (k n)"),
                         window(xr_d, at).rearrange("o p k b t -> (o p) (k b t)")).then_inc(back_in[at.u], 16)

        def sp_store(sp, at):
            for s, src, d in ((x2_done, x2, x2_d), (xf_done, xf, xf_d)):
                sp.wait_ge(s, at.n(1, 1))
                sp.dma_start(window(d, at).rearrange("o p k b t -> (o p) (k b t)"),
                             src[:, at.u, :, :].rearrange("p k n -> p (k n)")).then_inc(stored[at.u], 16)

        def pe_centre(pe, at):
            pe.wait_ge(front_in[at.u], at.d(32))
            for g in range(HG):
                pe.wait_ge(dn_done, at.n(HG, g + 1, back=1))
                pe.matmul(C_PS[g][:, :], w_cen[:, :], o_in[:, at.u, g, :], start=True, stop=True).then_inc(cen_done, 1)

        def pe_var(pe, at, g):
            pe.wait_ge(sq_done, at.n(HG, g + 1))
            pe.wait_ge(std_done, at.n(HG, g))
            pe.matmul(V_PS[:, :], mean_v[:, :], sq[:, g, :], start=True, stop=True).then_inc(var_done, 1)

        def pe_gate(pe, at, g):
            pe.wait_ge(sg_done, at.n(HG, g))
            for i in range(2):
                h = 2 * (2 * (g % 2) + i) + g // 2
                for k in range(KC):
                    mm = pe.matmul(G_PS[:, i * TW:(i + 1) * TW], w_g[:, k, h * DV:(h + 1) * DV], xn_in[:, at.u, k, :],
                                   start=(k == 0), stop=(k == KC - 1))
            mm.then_inc(gate_done, 1)

        def pe_out(pe, at):
            pe.wait_ge(x2_done, at.n(1, 0))
            for m in range(KC):
                for n in range(H):
                    g, i = n // 2, n % 2
                    h = 2 * (2 * (g % 2) + i) + g // 2
                    pe.wait_ge(og_done, at.n(HG, g + 1))
                    mm = pe.matmul(Y_PS[:, m * TW:(m + 1) * TW], w_o[:, h, m * P:(m + 1) * P],
                                   og[:, at.u, g, i * TW:(i + 1) * TW], start=(n == 0), stop=(n == H - 1))
            mm.then_inc(y_done, 1)

        def pe_stat(pe, at, which):
            if which == "mean":
                pe.wait_ge(x2_done, at.n(1, 1))
                pe.wait_ge(stdx_done, at.n(1, 0))
            else:
                pe.wait_ge(sqx_done, at.n(1, 1))
                pe.wait_ge(cenx_done, at.n(1, 1))
            for k in range(KC):
                mm = pe.matmul(M_PS[:, 0:TW], mean_c[:, :], x2[:, at.u, k, :] if which == "mean" else sqx[:, k, :],
                               start=(k == 0), stop=(k == KC - 1))
            mm.then_inc(mean_done if which == "mean" else varx_done, 1)

        def act_squares(act, at):
            for g in range(HG):
                act.wait_ge(cen_done, at.n(HG, g + 1))
                act.wait_ge(var_done, at.n(HG, g + 1, back=1))
                nc.scalar.activation(sq[:, g, :], C_PS[g][:, :], ACT.Square).then_inc(sq_done, 1)
            for g in range(HG):
                act.wait_ge(var_done, at.n(HG, g + 1))
                act.wait_ge(dn_done, at.n(HG, g + 1, back=1))
                nc.scalar.activation(std[:, g, :], V_PS[:, :], ACT.Sqrt, bias=eps[:, :]).then_inc(std_done, 1)

        def act_gates(act, at):
            for g in range(HG):
                act.wait_ge(gate_done, at.n(HG, g + 1))
                act.wait_ge(og_done, at.n(HG, g - 1))
                nc.scalar.activation(sg[:, g % 2, :], G_PS[:, :], ACT.Sigmoid).then_inc(sg_done, 1)
                act.wait_ge(dn_done, at.n(HG, g + 1))
                nc.scalar.activation(z[:, g % 2, :], dn[:, g, :], ACT.Identity, bias=lb[:, :], scale=lw[:, :])\
                    .then_inc(z_done, 1)

        def act_norm(act, at):
            act.wait_ge(cenx_done, at.n(1, 1))
            act.wait_ge(varx_done, at.n(1, 0))
            nc.scalar.activation(sqx[:, :, :], cenx[:, :, :], ACT.Square).then_inc(sqx_done, 1)
            act.wait_ge(varx_done, at.n(1, 1))
            act.wait_ge(xf_done, at.n(1, 0))
            nc.scalar.activation(stdx[:, :], M_PS[:, 0:TW], ACT.Sqrt, bias=eps[:, :]).then_inc(stdx_done, 1)

        def dve_normed(dve, own, at, g):
            dve.wait_ge(std_done, at.n(HG, g + 1))
            own.run(dve.reciprocal(rstd[:, :], std[:, g, :]))
            dve.wait_ge(z_done, at.n(HG, g + 1, back=1))
            dve.tensor_tensor(dn[:, g, :], C_PS[g][:, :], rstd[:, :], ALU.mult).then_inc(dn_done, 1)
            dve.wait_ge(dn_done, at.n(HG, g + 1))

        def dve_residual(dve, at):
            dve.wait_ge(y_done, at.n(1, 1))
            dve.wait_ge(back_in[at.u], at.d(16))
            dve.wait_ge(stored[at.u], at.d(32))
            dve.tensor_tensor(x2[:, at.u, :, :], Y_PS[:, :].rearrange("p (k n) -> p k n", k=KC), xr_in[:, at.u, :, :],
                              ALU.add).then_inc(x2_done, 1)
            dve.wait_ge(x2_done, at.n(1, 1))

        def dve_centre(dve, at):
            dve.wait_ge(mean_done, at.n(1, 1))
            mu = M_PS[:, 0:TW].rearrange("p (o n) -> p o n", o=1).to_broadcast([P, KC, TW])
            dve.tensor_tensor(cenx[:, :, :], x2[:, at.u, :, :], mu, ALU.subtract).then_inc(cenx_done, 1)
            dve.wait_ge(cenx_done, at.n(1, 1))

        def dve_norm(dve, own, at):
            dve.wait_ge(stdx_done, at.n(1, 1))
            own.run(dve.reciprocal(rstdx[:, :], stdx[:, :]))
            r = rstdx[:, :].rearrange("p (o n) -> p o n", o=1).to_broadcast([P, KC, TW])
            dve.tensor_tensor(xf[:, at.u, :, :], cenx[:, :, :], r, ALU.mult).then_inc(xf_done, 1)
            dve.wait_ge(xf_done, at.n(1, 1))

        FIRST = At(0, 0)
        clear_after(nc, ctx, sems)
        block = ctx.enter_context(nc.Block())

        @block.sync
        def _(sp):
            sp.dma_start(w_cen[:, :], w_centre).then_inc(loaded, 16)
            sp.dma_start(w_g[:, :, :], wg.rearrange("(k p) n -> p k n", p=P)).then_inc(loaded, 16)
            sp.dma_start(w_o[:, :, :], wo.rearrange("(h p) n -> p h n", p=P)).then_inc(loaded, 16)
            sp.dma_start(lw[:, :], ln_w).then_inc(loaded, 16)
            sp.dma_start(lb[:, :], ln_b).then_inc(loaded, 16)
            sp_front(sp, FIRST, first=True)
            sp_front(sp, At(0, 1), first=True)
            sp_back(sp, FIRST, first=True)
            with sp.Fori(0, NW // 2) as it:
                for q in range(2):
                    sp_front(sp, At(it, q + 2))
                    sp_back(sp, At(it, q + 1))
                    sp_store(sp, At(it, q))
            for u in range(2):
                sp.wait_ge(stored[u], 32 * (NW // 2 + 1))
                sp.wait_ge(front_in[u], 32 * (NW // 2 + 1))
            sp.wait_ge(back_in[0], 16 * (NW // 2 + 1))
            sp.wait_ge(back_in[1], 16 * (NW // 2))

        @block.tensor
        def _(pe):
            for s, per in ((cen_done, HG), (var_done, HG), (gate_done, HG), (y_done, 1), (mean_done, 1), (varx_done, 1)):
                pe.sem_inc(s, per)
            pe.wait_ge(loaded, 80)
            pe.wait_ge(consts, 1)
            pe_centre(pe, FIRST)
            for g in range(HG):
                pe_var(pe, FIRST, g)
            for g in range(HG):
                pe_gate(pe, FIRST, g)
            with pe.Fori(0, NW // 2) as it:
                for q in range(2):
                    at, nxt = At(it, q), At(it, q + 1)
                    pe_centre(pe, nxt)
                    pe_out(pe, at)
                    for g in range(HG):
                        pe_var(pe, nxt, g)
                    pe_stat(pe, at, "mean")
                    pe_gate(pe, nxt, 0)
                    pe_stat(pe, at, "var")
                    for g in range(1, HG):
                        pe_gate(pe, nxt, g)

        @block.scalar
        def _(act):
            for s, per in ((sq_done, HG), (std_done, HG), (sg_done, HG), (z_done, HG), (sqx_done, 1), (stdx_done, 1)):
                act.sem_inc(s, per)
            act.wait_ge(loaded, 80)
            act_squares(act, FIRST)
            act_gates(act, FIRST)
            with act.Fori(0, NW // 2) as it:
                for q in range(2):
                    at, nxt = At(it, q), At(it, q + 1)
                    act_squares(act, nxt)
                    act_norm(act, at)
                    act_gates(act, nxt)

        @block.vector
        def _(dve):
            dve.memset(mean_v[:, :], 1.0 / DV)
            dve.memset(mean_c[:, :], 1.0 / C)
            dve.memset(eps[:, :], EPS).then_inc(consts, 1)
            dve.wait_ge(consts, 1)
            for s, per in ((dn_done, HG), (x2_done, 1), (cenx_done, 1), (xf_done, 1), (stored[0], 32), (stored[1], 32)):
                dve.sem_inc(s, per)
            own = Chain(dve, own_dve)
            for g in range(HG):
                dve_normed(dve, own, FIRST, g)
            with dve.Fori(0, NW // 2) as it:
                own.restart()
                for q in range(2):
                    at, nxt = At(it, q), At(it, q + 1)
                    dve_residual(dve, at)
                    for g in range(HG):
                        dve_normed(dve, own, nxt, g)
                        if g == 1:
                            dve_centre(dve, at)
                    dve_norm(dve, own, at)

        @block.gpsimd
        def _(pool):
            pool.sem_inc(og_done, HG)

            def gated(at, first=False):
                for g in range(HG):
                    pool.wait_ge(sg_done, at.n(HG, g + 1))
                    pool.wait_ge(z_done, at.n(HG, g + 1))
                    if not first:
                        pool.wait_ge(y_done, at.n(1, 1, back=2))
                    pool.tensor_tensor(og[:, at.u, g, :], z[:, g % 2, :], sg[:, g % 2, :], ALU.mult).then_inc(og_done, 1)

            gated(FIRST, first=True)
            with pool.Fori(0, NW // 2) as it:
                for q in range(2):
                    gated(At(it, q + 1))


def local_layer(nc, lay, last, wqkv, wo, w1, b1, w2, b2, ln_g, ln_b, scales, tables, ident, mask, x_src, x_dst, x2_d, out):
    NT4 = T // P
    INNER, D, HPAIRS = H * 64, 64, H // 2
    HIDT = w2.shape[0] // P
    HID = HIDT * P

    def uses(names, size):
        at = {name: n for n, name in enumerate(names)}
        assert len(at) == len(names) and len(names) % size == 0
        return at, size, len(names) // size

    U = range(2)
    mm_uses = []
    for u in U:
        mm_uses += [(k, u, t) for t in range(NT4) for k in ("q", "k", "v")]
    mm_uses += [("pv", u, t) for u in U for t in range(NT4)]
    for u in U:
        mm_uses += [("wo", u, 0), ("wo", u, 1), ("mean", u), ("var", u)]
    for u in U:
        mm_uses += [(k, u, i) for i in range(HIDT) for k in ("g", "a")] + [("w2", u, 0), ("w2", u, 1)]
    MM = uses(mm_uses, 2)
    SIM = uses([(u, t, r) for u in U for t in range(NT4) for r in range(2)], 2)
    tr_uses = [(k, u, t) for u in U for t in range(NT4) for k in ("qT", "kT")]
    K = 2 * NT4
    halves = lambda t: (1,) if t == 0 else (0, 1)
    for u in U:
        for k in range(K + 3):
            if 1 <= k <= K:
                tr_uses += [("pT", u, k - 1, half) for half in halves((k - 1) // 2)]
            if k >= 4 and k % 2 == 0:
                tr_uses.append(("oT", u, k // 2 - 2))
    if last:
        tr_uses += [("out", u, k) for u in U for k in range(4)]
    TR = uses(tr_uses, 2)

    with ExitStack() as ctx:
        def sb(name, shape, dt=F32):
            return ctx.enter_context(nc.sbuf_tensor(f"f{lay}_{name}", shape, dt))

        sems = []

        def sem(name):
            sems.append(ctx.enter_context(nc.semaphore(f"f{lay}_{name}")))
            return sems[-1]

        w_qkv, w_o = sb("wqkv", [P, KC, 3 * INNER]), sb("wo", [P, HPAIRS, C])
        w_1, w_2 = sb("w1", [P, KC, 2 * HID]), sb("w2", [P, HIDT, C])
        b_1, b_2 = sb("b1", [P, 2 * HIDT]), sb("b2", [P, KC])
        l_g, l_b, eps = sb("lg", [P, KC]), sb("lb", [P, KC]), sb("eps", [P, 1])
        id_sb, id16 = sb("id", [P, P]), sb("id16", [P, P], BF16)
        mask_sb = sb("mask", [P, 2 * P], BF16)
        mean_w = sb("mean_w", [P, P])
        sc = sb("sc", [P, 2, 2, D])
        cos_t, sin_t = sb("cos", [P, NT4, 2, D]), sb("sin", [P, NT4, 2, D])
        X = sb("X", [P, 2, KC, T + 1])
        V = sb("V", [P, 2, NT4, INNER])
        QT = sb("QT", [P, 2, HPAIRS, T])
        KT = sb("KT", [P, 2, HPAIRS, T])
        qk = sb("qk", [P, 2, 2, INNER])
        sqr = sb("sqr", [P, 2 * INNER])
        rot = sb("rot", [P, 2 * INNER])
        qkr = sb("qkr", [P, 2, 2, INNER])
        nrm = sb("nrm", [P, 2, 2 * H])
        inv = sb("inv", [P, 2, 2 * H])
        ssq = sb("ssq", [P, 2, 2 * H])
        PR = sb("PR", [P, 2, 4, 2 * P])
        PT = sb("PT", [P, 2, 4, 2, P])
        nmax = sb("nmax", [P, 2, 4])
        rsum = sb("rsum", [P, 2, 2, 4])
        rinv = sb("rinv", [P, 2, 2, 4])
        o_sb = sb("o_sb", [P, 2, INNER])
        cen = sb("cen", [P, 2, KC, T])
        std, rstd = sb("std", [P, T]), sb("rstd", [P, T])
        gel = sb("gel", [P, 2, T])
        hid = sb("hid", [P, HIDT, T])
        x2 = sb("x2", [P, KC, T]) if last else None
        out_sb = sb("out_sb", [P, NT4, C]) if last else None
        SQ = sqr[:, :].rearrange("p (k n) -> p k n", k=KC)

        mm_ps = [ctx.enter_context(nc.psum_tensor(f"f{lay}_mm{i}", [P, 512], F32)) for i in range(2)]
        tr_ps = [ctx.enter_context(nc.psum_tensor(f"f{lay}_tr{i}", [P, 512], F32)) for i in range(2)]
        sim_ps = [ctx.enter_context(nc.psum_tensor(f"f{lay}_sim{i}", [P, 2, 2, 2 * P], F32)) for i in range(2)]

        names = ("loaded", "consts", "sq_done", "ssq_done", "nrm_done", "inv_done", "rope_done", "rot_used", "qk_ready",
                 "max_done", "exp_done", "pv_half", "rinv_done", "o_done", "csq_done", "cn_done", "hn_ready", "fin_done",
                 "own_act", "own_dve", "own_pool", "x2_in", "out_st")
        s = {n: sem(n) for n in names}
        x_in, x_st = [sem("x_in0"), sem("x_in1")], [sem("x_st0"), sem("x_st1")]
        mm_done, mm_free = [sem(f"mm_done{i}") for i in range(2)], [sem(f"mm_free{i}") for i in range(2)]
        sim_done, sim_free = [sem(f"sim_done{i}") for i in range(2)], [sem(f"sim_free{i}") for i in range(2)]
        tr_done, tr_free = [sem(f"tr_done{i}") for i in range(2)], [sem(f"tr_free{i}") for i in range(2)]

        class Bank:

            def __init__(self, it, table, banks, done, free, name):
                at, size, per = table
                n = at[name]
                self.ps, self.done, self.free = banks[n % size], done[n % size], free[n % size]
                self.mine = it * per + (n // size + 1)

            def claim(self, pe):
                pe.wait_ge(self.free, self.mine)

            def written(self, eng):
                eng.wait_ge(self.done, self.mine)

            def released(self, eng):
                eng.wait_ge(self.free, self.mine + 1)

        mm = lambda it, *name: Bank(it, MM, mm_ps, mm_done, mm_free, name)
        tr = lambda it, *name: Bank(it, TR, tr_ps, tr_done, tr_free, name)
        sim = lambda it, *name: Bank(it, SIM, sim_ps, sim_done, sim_free, name)

        def n(it, per, k):
            return it * per + (per + k)

        class Own:

            def __init__(self, eng, sem_):
                self.chain, self.eng = Chain(eng, sem_), eng

            def run(self, ins):
                self.chain.run(ins)

            def order(self, ins, sem_, value):
                ins.then_inc(sem_, 1)
                self.eng.wait_ge(sem_, value)

        TT, RR, FF = 2 * NT4, 4 * NT4, 2 * HIDT

        def before(u, k, step=2, per=2 * NT4):
            return (u, k - step) if k >= step else (u - 1, k - step + per) if u else (u, None)

        def pe_qkv(pe, it, u, t):
            if t == 0:
                per = 32 if lay == 0 else 16
                pe.wait_ge(x_in[u], it * per + per)
            for kind, name in enumerate(("q", "k", "v")):
                b = mm(it, name, u, t)
                b.claim(pe)
                for k in range(KC):
                    off = 1 - k + t * P
                    m = pe.matmul(b.ps[:, :], X[:, u, k, off:off + P], w_qkv[:, k, kind * INNER:(kind + 1) * INNER],
                                  start=(k == 0), stop=(k == KC - 1))
                m.then_inc(b.done, 1)

        def pe_turn_qk(pe, it, u, t):
            pe.wait_ge(s["qk_ready"], n(it, TT, u * NT4 + t + 1))
            for kind, name in enumerate(("qT", "kT")):
                b = tr(it, name, u, t)
                b.claim(pe)
                for hp in range(HPAIRS):
                    m = pe.transpose(b.ps[:, hp * P:(hp + 1) * P], qkr[:, t % 2, kind, hp * P:(hp + 1) * P], id_sb[:, :])
                m.then_inc(b.done, 1)

        def pe_sim(pe, it, u, t, r):
            if t == 0 and r == 0:
                tr(it, "qT", u, NT4 - 1).released(pe)
                tr(it, "kT", u, NT4 - 1).released(pe)
            b = sim(it, u, t, r)
            b.claim(pe)
            lo = P * halves(t)[0]
            for hh in range(2):
                rows = slice(64 * hh, 64 * hh + 64)
                for i in range(2):
                    hp = 2 * r + i
                    pe.matmul(b.ps[:, hh, i, lo:], QT[rows, u, hp, t * P:(t + 1) * P],
                              KT[rows, u, hp, (t - 1) * P + lo:(t + 1) * P], start=(i == 0), stop=False,
                              skip_group_check=True)
            for hh in range(2):
                for i in range(2):
                    m = pe.matmul(b.ps[:, hh, i, lo:], id16[:, :], mask_sb[:, lo:], start=False, stop=True,
                                  skip_group_check=True)
            m.then_inc(b.done, 1)

        def pe_turn_p(pe, it, u, k):
            t, r = k // 2, k % 2
            idx = u * 2 * NT4 + k
            pe.wait_ge(s["exp_done"], n(it, 4 * RR, 4 * (idx + 1)))
            for half in halves(t):
                b = tr(it, "pT", u, k, half)
                b.claim(pe)
                for i in range(4):
                    m = pe.transpose(b.ps[:, i * P:(i + 1) * P], PR[:, k % 2, i, half * P:(half + 1) * P], id_sb[:, :])
                m.then_inc(b.done, 1)

        def pe_pv(pe, it, u, k):
            t, r = k // 2, k % 2
            idx = u * 2 * NT4 + k
            for half in halves(t):
                tr(it, "pT", u, k, half).released(pe)
            b = mm(it, "pv", u, t)
            if r == 0:
                b.claim(pe)
            for hh in range(2):
                for i in range(2):
                    h = 2 * (2 * r + i) + hh
                    for half in halves(t):
                        m = pe.matmul(b.ps[:, h * D:(h + 1) * D], PT[:, k % 2, 2 * hh + i, half, :],
                                      V[:, u, t - 1 + half, h * D:(h + 1) * D],
                                      start=(half == halves(t)[0]), stop=(half == 1))
            if r == 1:
                m.then_inc(b.done, 1)
            else:
                m.then_inc(s["pv_half"], 1)

        def pe_turn_o(pe, it, u, t):
            pe.wait_ge(s["o_done"], n(it, TT, u * NT4 + t + 1))
            b = tr(it, "oT", u, t)
            b.claim(pe)
            for hp in range(HPAIRS):
                m = pe.transpose(b.ps[:, hp * P:(hp + 1) * P], o_sb[:, t % 2, hp * P:(hp + 1) * P], id_sb[:, :])
            m.then_inc(b.done, 1)

        def pe_attention(pe, it, u):
            for k in range(K + 3):
                if k < K:
                    pe_sim(pe, it, u, k // 2, k % 2)
                if 1 <= k <= K:
                    pe_turn_p(pe, it, u, k - 1)
                if 2 <= k <= K + 1:
                    pe_pv(pe, it, u, k - 2)
                if k >= 4 and k % 2 == 0:
                    pe_turn_o(pe, it, u, k // 2 - 2)

        def pe_wo_norm(pe, it, u):
            for m_ in range(KC):
                b = mm(it, "wo", u, m_)
                b.claim(pe)
                tr(it, "oT", u, NT4 - 1).released(pe)
                for hp in range(HPAIRS):
                    m = pe.matmul(b.ps[:, :], w_o[:, hp, m_ * P:(m_ + 1) * P], QT[:, u, hp, :],
                                  start=(hp == 0), stop=(hp == HPAIRS - 1))
                m.then_inc(b.done, 1)
            for name in ("mean", "var"):
                b = mm(it, name, u)
                b.claim(pe)
                if name == "mean":
                    mm(it, "wo", u, 0).released(pe)
                    mm(it, "wo", u, 1).released(pe)
                else:
                    pe.wait_ge(s["csq_done"], n(it, 2, u + 1))
                for k in range(KC):
                    src = X[:, u, k, 1 - k:1 - k + T] if name == "mean" else SQ[:, k, :]
                    m = pe.matmul(b.ps[:, :], mean_w[:, :], src, start=(k == 0), stop=(k == KC - 1))
                m.then_inc(b.done, 1)

        def pe_mlp(pe, it, u):
            pe.wait_ge(s["hn_ready"], n(it, 2, u + 1))
            for i in range(HIDT):
                for part, name in ((1, "g"), (0, "a")):
                    b = mm(it, name, u, i)
                    b.claim(pe)
                    for k in range(KC):
                        col = part * HID + i * P
                        m = pe.matmul(b.ps[:, :], w_1[:, k, col:col + P], cen[:, u, k, :], start=(k == 0), stop=(k == KC - 1))
                    m.then_inc(b.done, 1)
            for m_ in range(KC):
                b = mm(it, "w2", u, m_)
                b.claim(pe)
                mm(it, "a", u, HIDT - 1).released(pe)
                for i in range(HIDT):
                    m = pe.matmul(b.ps[:, :], w_2[:, i, m_ * P:(m_ + 1) * P], hid[:, i, :], start=(i == 0), stop=(i == HIDT - 1))
                m.then_inc(b.done, 1)

        def pe_out(pe, it, u):
            pe.wait_ge(s["fin_done"], n(it, 2, u + 1))
            for t in range(NT4):
                b = tr(it, "out", u, t)
                b.claim(pe)
                for k in range(KC):
                    m = pe.transpose(b.ps[:, k * P:(k + 1) * P], X[:, u, k, 1 + t * P:1 + (t + 1) * P], id_sb[:, :])
                m.then_inc(b.done, 1)

        clear_after(nc, ctx, sems)
        block = ctx.enter_context(nc.Block())

        @block.sync
        def _(sp):
            dmas = ((w_qkv[:, :, :], wqkv.rearrange("(k p) n -> p k n", p=P)), (w_o[:, :, :], wo.rearrange("(k p) n -> p k n", p=P)),
                    (w_1[:, :, :], w1.rearrange("(k p) n -> p k n", p=P)), (w_2[:, :, :], w2.rearrange("(k p) n -> p k n", p=P)),
                    (b_1[:, :], b1), (b_2[:, :], b2), (l_g[:, :], ln_g), (l_b[:, :], ln_b), (id_sb[:, :], ident),
                    (mask_sb[:, :], mask[:, 0:2 * P]), (id16[:, :], mask[:, 2 * P:]),
                    (sc[:, :, :, :].rearrange("p a k d -> p (a k d)"), scales.to_broadcast([P, 4 * D])),
                    (cos_t[:, :, :, :].rearrange("p t k d -> p (t k d)"), tables[:, 0:NT4 * 2 * D]),
                    (sin_t[:, :, :, :].rearrange("p t k d -> p (t k d)"), tables[:, NT4 * 2 * D:]))
            for dst, src in dmas:
                sp.dma_start(dst, src).then_inc(s["loaded"], 16)
            assert len(dmas) == 14
            with sp.Fori(0, B // 2) as it:
                for u in U:
                    bsl = bass.ds(it * 2 + u, 1)
                    sp.wait_ge(x_st[u], it * 16 + 16)
                    if lay == 0:
                        for k in range(KC):
                            sp.dma_start(X[:, u, k, 1:].rearrange("p (w t) -> p w t", t=WT),
                                         x_src[0:NW, :, k, bsl, :].rearrange("w p o t -> p (w o) t")).then_inc(x_in[u], 16)
                    else:
                        sp.dma_start(X[:, u, :, 1:], x_src[bsl].rearrange("o p k t -> (o p) k t")).then_inc(x_in[u], 16)
                for u in U:
                    bsl = bass.ds(it * 2 + u, 1)
                    if not last:
                        mm(it, "w2", u, 0).released(sp)
                        mm(it, "w2", u, 1).released(sp)
                        sp.dma_start(x_dst[bsl].rearrange("o p k t -> (o p) k t"), X[:, u, :, 1:]).then_inc(x_st[u], 16)
                    else:
                        sp.wait_ge(s["fin_done"], n(it, 2, u))
                        for k in range(KC):
                            sp.dma_start(x2[:, k, :].rearrange("p (w t) -> p w t", t=WT),
                                         x2_d[0:NW, :, k, bsl, :].rearrange("w p o t -> p (w o) t")).then_inc(s["x2_in"], 16)
                        tr(it, "out", u, NT4 - 2).released(sp)
                        tr(it, "out", u, NT4 - 1).released(sp)
                        sp.dma_start(out[bsl].rearrange("o (n p) c -> p (o n) c", p=P), out_sb[:, :, :]).then_inc(s["out_st"], 16)
                        sp.sem_inc(x_st[u], 16)
            for u in U:
                sp.wait_ge(x_st[u], 16 * (B // 2 + 1))
            if last:
                sp.wait_ge(s["out_st"], 16 * (B + 1))

        @block.tensor
        def _(pe):
            pe.sem_inc(s["pv_half"], TT)
            pe.wait_ge(s["loaded"], 14 * 16)
            pe.wait_ge(s["consts"], 1)
            with pe.Fori(0, B // 2) as it:
                for u in U:
                    for t in range(NT4 + 1):
                        if t < NT4:
                            pe_qkv(pe, it, u, t)
                        if t >= 1:
                            pe_turn_qk(pe, it, u, t - 1)
                for u in U:
                    pe_attention(pe, it, u)
                for u in U:
                    pe_wo_norm(pe, it, u)
                for u in U:
                    pe_mlp(pe, it, u)
                if last:
                    for u in U:
                        pe_out(pe, it, u)

        @block.scalar
        def _(act):
            own = Own(act, s["own_act"])
            act.wait_ge(s["loaded"], 14 * 16)
            act.wait_ge(s["consts"], 1)
            act.sem_inc(s["nrm_done"], TT)
            act.sem_inc(s["exp_done"], 4 * RR)
            act.sem_inc(s["csq_done"], 2)
            act.sem_inc(s["hn_ready"], 2)

            def copy(b, out_, in_):
                b.written(act)
                nc.scalar.activation(out_, in_, ACT.Copy).then_inc(b.free, 1)

            def qkv(it, u, t):
                i = u * NT4 + t
                act.wait_ge(s["rope_done"], n(it, TT, i - 1))
                act.wait_ge(s["sq_done"], n(it, TT, i - 1))
                for kind, name in enumerate(("q", "k")):
                    b = mm(it, name, u, t)
                    copy(b, qk[:, t % 2, kind, :], b.ps[:, :])
                b = mm(it, "v", u, t)
                copy(b, V[:, u, t, :], b.ps[:, :])

            def norm(it, u, t):
                i = u * NT4 + t
                act.wait_ge(s["ssq_done"], n(it, TT, i + 1))
                act.wait_ge(s["inv_done"], n(it, TT, i - 1))
                nc.scalar.activation(nrm[:, t % 2, :], ssq[:, t % 2, :], ACT.Sqrt).then_inc(s["nrm_done"], 1)

            def turned(it, u, t):
                for dst, name in ((QT, "qT"), (KT, "kT")):
                    b = tr(it, name, u, t)
                    b.written(act)
                    nc.scalar.activation(dst[:, u, :, t * P:(t + 1) * P], b.ps[:, :].rearrange("p (h n) -> p h n", h=HPAIRS),
                                         ACT.Copy).then_inc(b.free, 1)

            def exps(it, u, k):
                t, r = k // 2, k % 2
                idx = u * 2 * NT4 + k
                b = sim(it, u, t, r)
                lo = P * halves(t)[0]
                act.wait_ge(s["max_done"], n(it, RR, idx + 1))
                ub, kb = before(u, k)
                if kb is not None:
                    for half in halves(kb // 2):
                        tr(it, "pT", ub, kb, half).written(act)
                if k % 2 == 0:
                    act.wait_ge(s["rinv_done"], n(it, TT, u * NT4 + t - 1))
                for hh in range(2):
                    for i in range(2):
                        h4 = 2 * hh + i
                        nc.scalar.activation(PR[:, k % 2, h4, lo:], b.ps[:, hh, i, lo:], ACT.Exp, bias=nmax[:, k % 2, h4:h4 + 1],
                                             accum_out=rsum[:, t % 2, r, h4:h4 + 1]).then_inc(s["exp_done"], 1)
                act.wait_ge(s["exp_done"], n(it, 4 * RR, 4 * (idx + 1)))
                act.sem_inc(b.free, 1)

            def o_turned(it, u, t):
                b = tr(it, "oT", u, t)
                b.written(act)
                nc.scalar.activation(QT[:, u, :, t * P:(t + 1) * P], b.ps[:, :].rearrange("p (h n) -> p h n", h=HPAIRS),
                                     ACT.Copy).then_inc(b.free, 1)

            with act.Fori(0, B // 2) as it:
                for u in U:
                    for t in range(NT4 + 2):
                        if t < NT4:
                            qkv(it, u, t)
                        if 1 <= t <= NT4:
                            norm(it, u, t - 1)
                        if t >= 2:
                            turned(it, u, t - 2)
                for u in U:
                    for k in range(K + 3):
                        if k < K:
                            exps(it, u, k)
                        if k >= 4 and k % 2 == 0:
                            o_turned(it, u, k // 2 - 2)
                for u in U:
                    mm(it, "mean", u).released(act)
                    if u:
                        mm(it, "var", 0).written(act)
                    nc.scalar.activation(SQ, cen[:, u, :, :], ACT.Square).then_inc(s["csq_done"], 1)
                    b = mm(it, "var", u)
                    b.written(act)
                    act.wait_ge(s["cn_done"], n(it, 4, 2 * u))
                    nc.scalar.activation(std[:, :], b.ps[:, :], ACT.Sqrt, bias=eps[:, :]).then_inc(b.free, 1)
                    act.wait_ge(s["cn_done"], n(it, 4, 2 * (u + 1)))
                    for k in range(KC):
                        ins = nc.scalar.activation(cen[:, u, k, :], cen[:, u, k, :], ACT.Identity, bias=l_b[:, k:k + 1],
                                                   scale=l_g[:, k:k + 1])
                        own.run(ins) if k == 0 else ins.then_inc(s["hn_ready"], 1)
                for u in U:
                    for i in range(HIDT):
                        b = mm(it, "g", u, i)
                        b.written(act)
                        ub, ib = before(u, i, per=HIDT)
                        if ib is not None:
                            mm(it, "a", ub, ib).released(act)
                        nc.scalar.activation(gel[:, i % 2, :], b.ps[:, :], ACT.Gelu, bias=b_1[:, HIDT + i:HIDT + i + 1])\
                            .then_inc(b.free, 1)
                if last:
                    for u in U:
                        for k in range(4):
                            b = tr(it, "out", u, k)
                            b.written(act)
                            if k == 0:
                                act.wait_ge(s["out_st"], it * 32 + (u * 16 + 16))
                            nc.scalar.activation(out_sb[:, k, :], b.ps[:, 0:C], ACT.Copy).then_inc(b.free, 1)
                own.chain.restart()

        @block.gpsimd
        def _(pool):
            own = Own(pool, s["own_pool"])
            pool.memset(X[:, :, :, 0:1], 0.0)
            pool.memset(mean_w[:, :], 1.0 / C)
            pool.memset(eps[:, :], EPS).then_inc(s["consts"], 1)
            pool.wait_ge(s["consts"], 1)
            pool.sem_inc(s["sq_done"], TT)
            pool.sem_inc(s["qk_ready"], TT)
            pool.sem_inc(s["rot_used"], TT)
            for u in U:
                pool.sem_inc(x_st[u], 16)
            if last:
                pool.sem_inc(s["out_st"], 16)
            for b in range(2):
                for f in (mm_free, tr_free, sim_free):
                    pool.sem_inc(f[b], 1)

            def squares(it, u, t):
                i = u * NT4 + t
                mm(it, "q", u, t).released(pool)
                mm(it, "k", u, t).released(pool)
                pool.wait_ge(s["ssq_done"], n(it, TT, i))
                q = qk[:, t % 2, :, :].rearrange("p k n -> p (k n)")
                own.order(pool.tensor_tensor(sqr[:, :], q, q, ALU.mult), s["sq_done"], n(it, TT, i + 1))

            def rotated(it, u, t):
                i = u * NT4 + t
                pool.wait_ge(s["rope_done"], n(it, TT, i + 1))
                r = qkr[:, t % 2, :, :].rearrange("p k (h d) -> p (k h) d", d=D)
                own.order(pool.tensor_tensor(r, r, rot[:, :].rearrange("p (h d) -> p h d", d=D), ALU.add),
                           s["rot_used"], n(it, TT, i + 1))

            def normed(it, u, t):
                i = u * NT4 + t
                pool.wait_ge(s["inv_done"], n(it, TT, i + 1))
                r = qkr[:, t % 2, :, :].rearrange("p k (h d) -> p (k h) d", d=D)
                iv = inv[:, t % 2, :].rearrange("p (h o) -> p h o", o=1).to_broadcast([P, 2 * H, D])
                own.order(pool.tensor_tensor(r, r, iv, ALU.mult), s["qk_ready"], n(it, TT, i + 1))

            with pool.Fori(0, B // 2) as it:
                for u in U:
                    for t in range(NT4 + 1):
                        if t < NT4:
                            squares(it, u, t)
                            rotated(it, u, t)
                        if t >= 1:
                            normed(it, u, t - 1)

        @block.vector
        def _(dve):
            own = Own(dve, s["own_dve"])
            for name, k in (("ssq_done", TT), ("inv_done", TT), ("rope_done", TT), ("max_done", RR),
                            ("rinv_done", TT), ("o_done", TT), ("cn_done", 4), ("fin_done", 2)):
                dve.sem_inc(s[name], k)
            dve.wait_ge(s["loaded"], 14 * 16)
            dve.wait_ge(s["consts"], 1)
            for t in range(NT4):
                own.run(dve.tensor_tensor(cos_t[:, t, :, :], cos_t[:, t, :, :], sc[:, 0, :, :], ALU.mult))
                own.run(dve.tensor_tensor(sin_t[:, t, :, :], sin_t[:, t, :, :], sc[:, 1, :, :], ALU.mult))
            own.chain.restart()

            def rope(it, u, t):
                i = u * NT4 + t
                mm(it, "q", u, t).released(dve)
                mm(it, "k", u, t).released(dve)
                ub, tb = before(u, t, per=NT4)
                if tb is not None:
                    tr(it, "kT", ub, tb).written(dve)
                dve.wait_ge(s["rot_used"], n(it, TT, i))
                q = qk[:, t % 2, :, :].rearrange("p k (h d) -> p k h d", d=D)
                bc = lambda tab, lo, hi: tab[:, t, :, lo:hi].rearrange("p k (o d) -> p k o d", o=1).to_broadcast([P, 2, H, hi - lo])
                o_ = qkr[:, t % 2, :, :].rearrange("p k (h d) -> p k h d", d=D)
                ro = rot[:, :].rearrange("p (k h d) -> p k h d", k=2, d=D)
                own.run(dve.tensor_tensor(o_, q, bc(cos_t, 0, D), ALU.mult))
                own.run(dve.tensor_tensor(ro[:, :, :, 0:32], q[:, :, :, 32:64], bc(sin_t, 0, 32), ALU.mult))
                own.order(dve.tensor_tensor(ro[:, :, :, 32:64], q[:, :, :, 0:32], bc(sin_t, 32, 64), ALU.mult),
                           s["rope_done"], n(it, TT, i + 1))
                dve.wait_ge(s["sq_done"], n(it, TT, i + 1))
                dve.wait_ge(s["nrm_done"], n(it, TT, i - 1))
                own.order(dve.tensor_reduce(ssq[:, t % 2, :], sqr[:, :].rearrange("p (h d) -> p h d", d=D), AX.X, ALU.add),
                           s["ssq_done"], n(it, TT, i + 1))

            def inverse(it, u, t):
                i = u * NT4 + t
                dve.wait_ge(s["nrm_done"], n(it, TT, i + 1))
                dve.wait_ge(s["qk_ready"], n(it, TT, i - 1))
                v = inv[:, t % 2, :]
                own.run(dve.tensor_scalar(v, nrm[:, t % 2, :], 1e-12, None, ALU.max))
                own.run(dve.reciprocal(v, v))
                own.order(dve.tensor_scalar(v[:, 0:H], v[:, 0:H], 8.0, None, ALU.mult), s["inv_done"], n(it, TT, i + 1))

            def row_max(it, u, k):
                t, r = k // 2, k % 2
                idx = u * 2 * NT4 + k
                b = sim(it, u, t, r)
                b.written(dve)
                lo = P * halves(t)[0]
                dve.wait_ge(s["exp_done"], n(it, 4 * RR, 4 * (idx - 1)))
                own.order(dve.tensor_reduce(nmax[:, k % 2, :], b.ps[:, :, :, lo:].rearrange("p a b n -> p (a b) n"), AX.X,
                                             ALU.max, negate=True), s["max_done"], n(it, RR, idx + 1))

            def p_out(it, u, k):
                ub, kb = before(u, k)
                if kb is not None and kb % 2:
                    mm(it, "pv", ub, kb // 2).written(dve)
                elif kb is not None:
                    dve.wait_ge(s["pv_half"], n(it, TT, ub * NT4 + kb // 2 + 1))
                for half in halves(k // 2):
                    b = tr(it, "pT", u, k, half)
                    b.written(dve)
                    dve.tensor_copy(PT[:, k % 2, :, half, :], b.ps[:, :].rearrange("p (h n) -> p h n", h=4)).then_inc(b.free, 1)

            def o_out(it, u, t):
                i = u * NT4 + t
                dve.wait_ge(s["exp_done"], n(it, 4 * RR, 8 * (i + 1)))
                own.order(dve.reciprocal(rinv[:, t % 2, :, :], rsum[:, t % 2, :, :]), s["rinv_done"], n(it, TT, i + 1))
                b = mm(it, "pv", u, t)
                b.written(dve)
                ub, tb = before(u, t, per=NT4)
                if tb is not None:
                    tr(it, "oT", ub, tb).written(dve)
                for r in range(2):
                    o_ = o_sb[:, t % 2, r * 4 * D:(r + 1) * 4 * D].rearrange("p (i h d) -> p h i d", h=2, d=D)
                    p_ = b.ps[:, r * 4 * D:(r + 1) * 4 * D].rearrange("p (i h d) -> p h i d", h=2, d=D)
                    ri = rinv[:, t % 2, r, :].rearrange("p (h i o) -> p h i o", h=2, o=1).to_broadcast([P, 2, 2, D])
                    ins = dve.tensor_tensor(o_, p_, ri, ALU.mult)
                    own.run(ins) if r == 0 else own.order(ins, b.free, b.mine + 1)
                dve.sem_inc(s["o_done"], 1)

            with dve.Fori(0, B // 2) as it:
                own.chain.restart()
                for u in U:
                    for t in range(NT4 + 1):
                        if t < NT4:
                            rope(it, u, t)
                        if t >= 1:
                            inverse(it, u, t - 1)
                for u in U:
                    for k in range(K + 3):
                        if k < K:
                            row_max(it, u, k)
                        if 1 <= k <= K:
                            p_out(it, u, k - 1)
                        if k >= 4 and k % 2 == 0:
                            o_out(it, u, k // 2 - 2)
                own.chain.restart()
                for u in U:
                    for m_ in range(KC):
                        b = mm(it, "wo", u, m_)
                        b.written(dve)
                        xv = X[:, u, m_, 1:]
                        own.order(dve.tensor_tensor(xv, b.ps[:, :], xv, ALU.add), b.free, b.mine + 1)
                    b = mm(it, "mean", u)
                    b.written(dve)
                    for k in range(KC):
                        ins = dve.tensor_tensor(cen[:, u, k, :], X[:, u, k, 1 - k:1 - k + T], b.ps[:, :], ALU.subtract)
                        own.run(ins) if k == 0 else own.order(ins, b.free, b.mine + 1)
                    mm(it, "var", u).released(dve)
                    own.run(dve.reciprocal(rstd[:, :], std[:, :]))
                    for k in range(KC):
                        own.order(dve.tensor_tensor(cen[:, u, k, :], cen[:, u, k, :], rstd[:, :], ALU.mult),
                                   s["cn_done"], n(it, 4, 2 * u + k + 1))
                for u in U:
                    for i in range(HIDT):
                        b = mm(it, "a", u, i)
                        b.written(dve)
                        mm(it, "g", u, i).released(dve)
                        if u and i == 0:
                            mm(it, "w2", 0, 1).written(dve)
                        ins = dve.scalar_tensor_tensor(out=hid[:, i, :], in0=b.ps[:, :], scalar=b_1[:, i:i + 1], in1=gel[:, i % 2, :],
                                                       op0=ALU.add, op1=ALU.mult)
                        own.order(ins, b.free, b.mine + 1)
                    for m_ in range(KC):
                        b = mm(it, "w2", u, m_)
                        b.written(dve)
                        xv = X[:, u, m_, 1:]
                        own.order(dve.scalar_tensor_tensor(out=xv, in0=b.ps[:, :], scalar=b_2[:, m_:m_ + 1], in1=xv,
                                                            op0=ALU.add, op1=ALU.add), b.free, b.mine + 1)
                    if last:
                        dve.wait_ge(s["x2_in"], it * 64 + (u * 32 + 32))
                        xv = X[:, u, :, 1:]
                        own.order(dve.tensor_tensor(xv, xv, x2[:, :, :], ALU.add), s["fin_done"], n(it, 2, u + 1))
                own.chain.restart()


def program(nc, a, out):
    dram = lambda name, shape: nc.dram_tensor(name, shape, F32, kind="Internal").ap()
    xr_d = dram("xr_d", (NW + 1, P, KC, B, WT))
    xn_d = dram("xn_d", (NW + 2, P, KC, B, WT))
    beta_d = dram("beta_d", (NW + 1, 2, H // 2, B, WT))
    betak_d = dram("betak_d", (NW + 1, 2, H // 2, B, WT))
    o_d = dram("o_d", (NW + 2, P, 2, NC_, WT))
    x2_d = dram("x2_d", (NW, P, KC, B, WT))
    xf_d = dram("xf_d", (NW, P, KC, B, WT))
    x1_d = dram("x1_d", (B, P, KC, T))
    norm_and_beta(nc, a["x"], a["wb"], a["bb"], a["ident"], xr_d, xn_d, beta_d, betak_d, o_d)
    recurrence(nc, a["wq"], a["wk"], a["wv"], a["wa"], a["ba"], a["cw_qk"], a["cb_qk"], a["cw_v"], a["cb_v"],
               a["ident"], a["row_mask"], xn_d, beta_d, betak_d, o_d)
    gate_and_project(nc, a["wg"], a["wo"], a["ln_w"], a["ln_b"], a["w_centre"], xn_d, xr_d, o_d, x2_d, xf_d)
    for lay in range(2):
        last = lay == 1
        w = lambda name: a[f"{name}{lay}"]
        local_layer(nc, lay, last, w("wqkv"), w("wo"), w("w1"), w("b1"), w("w2"), w("b2"), w("lg"), w("lb"), w("scales"),
                    a["tables"], a["ident"], a["mask"], x1_d if last else xf_d, x1_d, x2_d, out)


def kernel(**inputs):
    import ml_dtypes
    import numpy as np
    import concourse.bacc as bacc
    from concourse.bass_utils import run_bass_kernel_spmd

    g = {k: np.asarray(v) for k, v in inputs.items()}
    f32 = np.float32
    hperm = [2 * j + hh for hh in range(2) for j in range(H // 2)]
    tile_cols = lambda v, n: np.ascontiguousarray(v.reshape((n, P) + v.shape[1:]).swapaxes(0, 1))

    row = np.arange(P)
    rb, rh, rs = row // (2 * CT), row // CT % 2, row % CT
    row_mask = np.zeros((P, NSUB - 1, 2, 4), f32)
    for j in range(1, NSUB):
        row_mask[row, j - 1, rh, rb] = rs // ST < j

    D, HID, HIDP = 64, g["L0_ffn_w2"].shape[1], 768
    half_idx = np.arange(0, D, 2, dtype=f32)
    t = np.arange(T, dtype=f32)
    freqs = t[:, None] * (1.0 / f32(10000.0) ** (half_idx / f32(D))).astype(f32)[None, :]
    scale = ((half_idx + 0.4 * D) / (1.4 * D)).astype(f32)[None, :] ** ((t - T // 2) / 64.0).astype(f32)[:, None]
    cos, sin = np.cos(freqs).astype(f32), np.sin(freqs).astype(f32)
    both = lambda lo, hi: np.stack([np.concatenate([lo * m, hi * m], 1) for m in (scale, 1.0 / scale)], 1)
    tiles = lambda v: v.reshape(T // P, P, 2 * D).transpose(1, 0, 2).reshape(P, -1)
    tables = np.concatenate([tiles(both(cos, cos)), tiles(both(-sin, sin))], 1).astype(f32)
    qi, kk = np.arange(P)[:, None], np.arange(2 * P)[None, :]
    mask = np.where((kk >= qi) & (kk - P <= qi), 0.0, -1e30)
    mask = np.concatenate([mask, np.eye(P)], 1).astype(ml_dtypes.bfloat16)

    def pad_halves(v):
        v = v.reshape(v.shape[:-1] + (2, HID))
        return np.pad(v, [(0, 0)] * (v.ndim - 1) + [(0, HIDP - HID)]).reshape(v.shape[:-2] + (2 * HIDP,))

    arrays = {
        "x": g["L0_attn_x"],
        "wq": g["L0_attn_Wq"].T, "wk": g["L0_attn_Wk"].T, "wv": g["L0_attn_Wv"].T, "wa": g["L0_attn_Wa"].T,
        "ba": tile_cols(g["L0_attn_ba"], H), "wb": g["L0_attn_Wb"].T[:, hperm], "bb": g["L0_attn_bb"][hperm][:, None],
        "cw_qk": np.concatenate([tile_cols(g["L0_attn_qc_w"][:, 0, :], 4), tile_cols(g["L0_attn_kc_w"][:, 0, :], 4)], 1),
        "cb_qk": np.concatenate([tile_cols(g["L0_attn_qc_b"], 4), tile_cols(g["L0_attn_kc_b"], 4)], 1),
        "cw_v": tile_cols(g["L0_attn_vc_w"][:, 0, :], 8), "cb_v": tile_cols(g["L0_attn_vc_b"], 8),
        "ident": np.eye(P, dtype=f32), "row_mask": row_mask,
        "wg": g["L0_attn_Wg"].T, "wo": g["L0_attn_Wo"].T,
        "ln_w": g["L0_attn_ln_w"][:, None], "ln_b": g["L0_attn_ln_b"][:, None],
        "w_centre": ((np.eye(P) - 1.0 / P) / DK ** 0.5).astype(f32),
        "tables": tables, "mask": mask,
    }
    for lay in range(2):
        w = lambda name: g["L0_ffn_" + name][lay]
        swap = lambda v: np.concatenate([v[D // 2:], v[:D // 2]])
        arrays.update({
            f"wqkv{lay}": w("wqkv"), f"wo{lay}": w("wo"),
            f"w1{lay}": pad_halves(w("w1")), f"b1{lay}": tile_cols(pad_halves(w("b1")), 2 * HIDP // P),
            f"w2{lay}": np.pad(w("w2"), ((0, HIDP - HID), (0, 0))), f"b2{lay}": tile_cols(w("b2"), KC),
            f"lg{lay}": tile_cols(w("ln_g"), KC), f"lb{lay}": tile_cols(w("ln_b"), KC),
            f"scales{lay}": np.concatenate([w("q_scale"), w("k_scale"), swap(w("q_scale")), swap(w("k_scale"))])[None, :],
        })
    arrays = {k: np.ascontiguousarray(v) for k, v in arrays.items()}
    nc = bacc.Bacc("TRN2", target_bir_lowering=False, num_devices=1)
    aps = {k: nc.dram_tensor("in_" + k, v.shape, mybir.dt.from_np(v.dtype), kind="ExternalInput").ap()
           for k, v in arrays.items()}
    out = nc.dram_tensor("out", (B, T, C), F32, kind="ExternalOutput").ap()
    program(nc, aps, out)
    r = run_bass_kernel_spmd(nc, [{"in_" + k: v for k, v in arrays.items()}], core_ids=[0])
    return r.results[0]["out"]
```

```python
from contextlib import ExitStack

import concourse.bass as bass
from concourse import mybir

F32 = mybir.dt.float32
BF16 = mybir.dt.bfloat16
ALU = mybir.AluOpType
ACT = mybir.ActivationFunctionType
AX = mybir.AxisListType

P = 128
B, T, C = 8, 512, 256
KC = C // P
H, DK, DV, TAPS = 8, 64, 128, 4
EPS = 1e-5

WT, CT, ST = 32, 16, 4
NW, NCH, NSUB = T // WT, T // CT, CT // ST
MCH = WT // CT
NC_ = H // 2 * B
NG = NC_ // 4
TW = B * WT


class Chain:

    def __init__(self, eng, sem):
        self.eng, self.sem, self.k = eng, sem, 0

    def run(self, ins):
        self.k += 1
        ins.then_inc(self.sem, 1)
        self.eng.wait_ge(self.sem, self.k)

    def restart(self):
        self.eng.sem_inc(self.sem, 1)
        self.eng.wait_ge(self.sem, self.k + 1)
        self.eng.sem_clear(self.sem)
        self.k = 0


def clear_after(nc, ctx, sems):
    def clear():
        with nc.Block() as block:
            @block.gpsimd
            def _(pool):
                for s in sems:
                    pool.sem_clear(s)
    ctx.callback(clear)


def norm_and_beta(nc, x, wb, bb, ident, xr_d, xn_d, beta_d, betak_d, o_d):
    with ExitStack() as ctx:
        def sb(name, shape, dt=F32):
            return ctx.enter_context(nc.sbuf_tensor("n_" + name, shape, dt))

        def pb(name, shape=(P, 512)):
            return ctx.enter_context(nc.psum_tensor("n_" + name, list(shape), F32))

        sems = []

        def sem(name):
            sems.append(ctx.enter_context(nc.semaphore("n_" + name)))
            return sems[-1]

        x_in = sb("x_in", [P, 2, T // P, C])
        x_t = sb("x_t", [P, 2, KC, T])
        cen = sb("cen", [P, 2, KC, T])
        sq = sb("sq", [P, 2, KC, T])
        std = sb("std", [P, 2, T])
        rstd = sb("rstd", [P, T])
        xn = sb("xn", [P, 2, KC, T])
        be = sb("be", [H, 2, T])
        bek = sb("bek", [H, 2, T])
        zero = sb("zero", [P, 2 * TW])
        id_sb = sb("id", [P, P])
        mean_w = sb("mean_w", [P, P])
        eps = sb("eps", [P, 1])
        wb_sb = sb("wb", [P, KC, H])
        bb_sb = sb("bb", [H, 1])
        x_ps = [pb("x_ps0"), pb("x_ps1")]
        mu_ps, var_ps, be_ps = pb("mu_ps"), pb("var_ps"), pb("be_ps")

        consts_in, consts = sem("consts_in"), sem("consts")
        x_loaded = [sem("x_loaded0"), sem("x_loaded1")]
        turned, copied = sem("turned"), sem("copied")
        mean_done, centred, squared = sem("mean_done"), sem("centred"), sem("squared")
        var_done, std_done, normed = sem("var_done"), sem("std_done"), sem("normed")
        beta_done, beta_sig = sem("beta_done"), sem("beta_sig")
        stored = [sem("stored0"), sem("stored1")]
        padded = sem("padded")
        dve_own, act_own = sem("dve_own"), sem("act_own")
        STORES = 2 * KC + 4

        clear_after(nc, ctx, sems)
        block = ctx.enter_context(nc.Block())

        def nth(it, u, k=1, per=1):
            return it * (2 * per) + (u * per + k)

        @block.sync
        def _(sp):
            sp.dma_start(id_sb[:, :], ident).then_inc(consts_in, 16)
            sp.dma_start(wb_sb[:, :, :], wb.rearrange("(k p) h -> p k h", p=P)).then_inc(consts_in, 16)
            sp.dma_start(bb_sb[:, :], bb).then_inc(consts_in, 16)
            for u in range(2):
                sp.dma_start(x_in[:, u, :, :], x[u:u + 1].rearrange("o (n p) c -> p (o n) c", p=P)).then_inc(x_loaded[u], 16)
            sp.wait_ge(consts, 1)
            for w in (NW, NW + 1):
                sp.dma_start(xn_d[w].rearrange("p k b t -> p (k b t)"), zero[:, 0:KC * TW]).then_inc(padded, 16)
                for n in range(4):
                    sp.dma_start(o_d[w].rearrange("p h c t -> p (h c t)")[:, n * 2 * TW:(n + 1) * 2 * TW], zero[:, :])\
                        .then_inc(padded, 16)
            sp.dma_start(xr_d[NW].rearrange("p k b t -> p (k b t)"), zero[:, 0:KC * TW]).then_inc(padded, 16)
            for d in (beta_d, betak_d):
                sp.dma_start(d[NW].rearrange("h j b t -> (h j) (b t)"), zero[0:H, 0:TW]).then_inc(padded, 16)

            def load(b, u):
                sp.dma_start(x_in[:, u, :, :], x[bass.ds(b, 1)].rearrange("o (n p) c -> p (o n) c", p=P))\
                    .then_inc(x_loaded[u], 16)

            def store(it, u):
                bslice = bass.ds(it * 2 + u, 1)
                sp.wait_ge(copied, nth(it, u, 2))
                for k in range(KC):
                    sp.dma_start(xr_d[0:NW, :, k, bslice, :].rearrange("w p o t -> p (w o) t"),
                                 x_t[:, u, k, :].rearrange("p (w t) -> p w t", t=WT)).then_inc(stored[u], 16)
                sp.wait_ge(normed, nth(it, u, 2))
                for k in range(KC):
                    sp.dma_start(xn_d[0:NW, :, k, bslice, :].rearrange("w p o t -> p (w o) t"),
                                 xn[:, u, k, :].rearrange("p (w t) -> p w t", t=WT)).then_inc(stored[u], 16)
                sp.wait_ge(beta_sig, nth(it, u, 2))
                for hh in range(2):
                    for d, s in ((beta_d, be), (betak_d, bek)):
                        sp.dma_start(d[0:NW, hh, :, bslice, :].rearrange("w j o t -> j (w o) t"),
                                     s[4 * hh:4 * hh + 4, u, :].rearrange("p (w t) -> p w t", t=WT))\
                            .then_inc(stored[u], 16)

            with sp.Fori(0, B // 2 - 1) as it:
                for u in range(2):
                    sp.wait_ge(turned, nth(it, u, 3))
                    load(it * 2 + (u + 2), u)
                for u in range(2):
                    store(it, u)
            for u in range(2):
                store(B // 2 - 1, u)
            for u in range(2):
                sp.wait_ge(stored[u], 16 * STORES * (B // 2 + 1))
            sp.wait_ge(padded, 16 * 13)

        @block.gpsimd
        def _(pool):
            pool.memset(zero[:, :], 0.0).then_inc(consts, 1)

        @block.tensor
        def _(pe):
            pe.sem_inc(turned, 2)
            pe.wait_ge(consts_in, 48)
            with pe.Fori(0, B // 2) as it:
                for u in range(2):
                    pe.wait_ge(x_loaded[u], it * 16 + 16)
                    pe.wait_ge(copied, nth(it, u))
                    for n in range(T // P):
                        for k in range(KC):
                            mm = pe.transpose(x_ps[k][:, n * P:(n + 1) * P], x_in[:, u, n, k * P:(k + 1) * P], id_sb[:, :])
                    mm.then_inc(turned, 1)
                for u in range(2):
                    pe.wait_ge(copied, nth(it, u, 2))
                    pe.wait_ge(centred, nth(it, u))
                    for k in range(KC):
                        mm = pe.matmul(mu_ps[:, :], mean_w[:, :], x_t[:, u, k, :], start=(k == 0), stop=(k == KC - 1))
                    mm.then_inc(mean_done, 1)
                for u in range(2):
                    pe.wait_ge(squared, nth(it, u, 2))
                    pe.wait_ge(std_done, nth(it, u))
                    for k in range(KC):
                        mm = pe.matmul(var_ps[:, :], mean_w[:, :], sq[:, u, k, :], start=(k == 0), stop=(k == KC - 1))
                    mm.then_inc(var_done, 1)
                for u in range(2):
                    pe.wait_ge(normed, nth(it, u, 2))
                    pe.wait_ge(beta_sig, nth(it, u))
                    for k in range(KC):
                        mm = pe.matmul(be_ps[0:H, :], wb_sb[:, k, :], xn[:, u, k, :], start=(k == 0), stop=(k == KC - 1))
                    mm.then_inc(beta_done, 1)

        @block.scalar
        def _(act):
            act.sem_inc(copied, 1)
            act.sem_inc(squared, 1)
            act.sem_inc(beta_sig, 1)
            act.wait_ge(consts_in, 48)
            own = Chain(act, act_own)
            with act.Fori(0, B // 2) as it:
                own.restart()
                for u in range(2):
                    act.wait_ge(stored[u], it * (16 * STORES) + 16 * STORES)
                    act.wait_ge(turned, nth(it, u, 3))
                    own.run(nc.scalar.activation(x_t[:, u, 0, :], x_ps[0][:, :], ACT.Copy))
                    nc.scalar.activation(x_t[:, u, 1, :], x_ps[1][:, :], ACT.Copy).then_inc(copied, 1)
                for u in range(2):
                    act.wait_ge(centred, nth(it, u, 2))
                    act.wait_ge(var_done, nth(it, 0))
                    nc.scalar.activation(sq[:, u, :, :], cen[:, u, :, :], ACT.Square).then_inc(squared, 1)
                for u in range(2):
                    act.wait_ge(var_done, nth(it, u, 2))
                    act.wait_ge(normed, nth(it, 0))
                    nc.scalar.activation(std[:, u, :], var_ps[:, :], ACT.Sqrt, bias=eps[:, :]).then_inc(std_done, 1)
                for u in range(2):
                    act.wait_ge(beta_done, nth(it, u, 2))
                    own.run(nc.scalar.activation(be[:, u, :], be_ps[0:H, :], ACT.Sigmoid, bias=bb_sb[:, :]))
                    nc.scalar.activation(bek[:, u, :], be[:, u, :], ACT.Copy, scale=-1.0 / DK).then_inc(beta_sig, 1)

        @block.vector
        def _(dve):
            own = Chain(dve, dve_own)
            own.run(dve.memset(mean_w[:, :], 1.0 / C))
            own.run(dve.memset(eps[:, :], EPS))
            dve.sem_inc(centred, 1)
            dve.sem_inc(normed, 1)
            dve.sem_inc(var_done, 1)
            dve.sem_inc(mean_done, 1)
            dve.sem_inc(std_done, 1)
            dve.sem_inc(beta_done, 1)
            for u in range(2):
                dve.sem_inc(stored[u], 16 * STORES)
            with dve.Fori(0, B // 2) as it:
                own.restart()
                for u in range(2):
                    dve.wait_ge(mean_done, nth(it, u, 2))
                    dve.wait_ge(squared, nth(it, 0))
                    own.run(dve.tensor_tensor(cen[:, u, 0, :], x_t[:, u, 0, :], mu_ps[:, :], ALU.subtract))
                    dve.tensor_tensor(cen[:, u, 1, :], x_t[:, u, 1, :], mu_ps[:, :], ALU.subtract).then_inc(centred, 1)
                for u in range(2):
                    dve.wait_ge(centred, nth(it, u, 2))
                    dve.wait_ge(std_done, nth(it, u, 2))
                    dve.wait_ge(stored[u], it * (16 * STORES) + 16 * STORES)
                    own.run(dve.reciprocal(rstd[:, :], std[:, u, :]))
                    own.run(dve.tensor_tensor(xn[:, u, 0, :], cen[:, u, 0, :], rstd[:, :], ALU.mult))
                    dve.tensor_tensor(xn[:, u, 1, :], cen[:, u, 1, :], rstd[:, :], ALU.mult).then_inc(normed, 1)
                    dve.wait_ge(normed, nth(it, u, 2))


def recurrence(nc, wq, wk, wv, wa, ba, cw_qk, cb_qk, cw_v, cb_v, ident, row_mask, xn_d, beta_d, betak_d, o_d):
    HP = H // 2
    QO, GO = (0, 1, 3, 6), (None, 10, 11, 13)
    NPR = 16
    TILES = [("q", j) for j in range(HP)] + [("k", j) for j in range(HP)] + \
            [("v", h) for h in range(H)] + [("a", h) for h in range(H)]
    NT, NCONV = len(TILES), 2 * HP + H
    PER_SUB = (3, 3, 3, 3, 4, 4, 4, 0)
    FIRST = [sum(PER_SUB[:i]) for i in range(len(PER_SUB) + 1)]
    assert FIRST[-1] == NT
    SLOTS = 4

    with ExitStack() as ctx:
        def sb(name, shape, dt=F32):
            return ctx.enter_context(nc.sbuf_tensor("r_" + name, shape, dt))

        sems = []

        def sem(name):
            sems.append(ctx.enter_context(nc.semaphore("r_" + name)))
            return sems[-1]

        id_sb = sb("id", [P, P])
        ones = sb("ones", [P, 2, P])
        rmask = sb("rmask", [P, NSUB - 1, 2, 4])
        w_q, w_k = sb("wq", [P, KC, H * DK]), sb("wk", [P, KC, H * DK])
        w_v, w_a = sb("wv", [P, KC, H * DV]), sb("wa", [P, KC, H * DV])
        b_a = sb("ba", [P, H])
        c_w = sb("cw", [P, NCONV, TAPS])
        c_b = sb("cb", [P, NCONV])
        xn_w = sb("xn_w", [P, 2, KC, TW])
        bt, btk = sb("bt", [P, 2, NC_, WT]), sb("btk", [P, NC_, WT])
        Kw, Kb, Qw = (sb(n, [P, 2, NC_, WT]) for n in ("K", "Kb", "Q"))
        Vw, Aw = (sb(n, [P, 2, 2, NC_, WT]) for n in ("V", "A"))
        raw = sb("raw", [P, SLOTS, B, TAPS - 1 + WT])
        conv = sb("conv", [P, SLOTS, B, WT])
        halo = sb("halo", [P, NCONV, B, TAPS - 1])
        prod = sb("prod", [P, 2, NC_, NPR])
        bd_qk = sb("bd_qk", [P, NC_, 2, 2, CT])
        bd_k = sb("bd_k", [P, NC_, 2, CT])
        k_rows = sb("k_rows", [P, NG, 4, P])
        gram = sb("gram", [P, 2, NC_, CT])
        cross = sb("cross", [P, NSUB - 1, 2, 2, NC_, ST])
        dec = sb("dec", [P, 2, NC_, NSUB, ST + 1])
        dec_c = sb("dec_c", [P, 2, NC_, CT + 1])
        c_exp = sb("c_exp", [P, NC_ // 4, 2, DK])
        S = sb("S", [P, NC_, DV])
        W = sb("W", [P, NC_, 2, CT])
        w_rows = sb("w_rows", [P, NG, P])
        Wh = sb("Wh", [P, 2, NC_, 5])
        TB = sb("TB", [P, 2, NC_, ST, ST])
        QB = sb("QB", [P, 2, NC_, ST, ST + 1])
        xs_tmp = QB[:, :, :, :, :].rearrange("p h c t s -> p (h c t s)")[:, 0:2 * NC_ * CT]\
            .rearrange("p (h c t) -> p h c t", h=2, c=NC_)
        tmp = sb("tmp", [P, 2, NC_, ST])[:, :, :, :]
        O = sb("O", [P, 2, NC_, WT])

        gq_ps = ctx.enter_context(nc.psum_tensor("r_gq_ps", [P, 2, NC_, NPR], F32))
        bank = [ctx.enter_context(nc.psum_tensor(f"r_bank{i}", [P, 512], F32)) for i in range(6)]
        X_PS, T_PS, P_PS, M_PS = bank[0], (bank[1], bank[2]), (bank[3], bank[4]), bank[5]
        XS_PS = (X_PS, M_PS, T_PS[0], T_PS[1])
        CR_PS = (M_PS, T_PS[0], T_PS[1])
        UP_PS = (T_PS[0], T_PS[1], M_PS)

        loaded = sem("loaded")
        zeroed = sem("zeroed")
        proj_done, gq_done, turned_w, x_done = sem("proj_done"), sem("gq_done"), sem("turned_w"), sem("x_done")
        upd_done, xs_done, cr_done, gram_done, kt_done = (sem(n) for n in
                                                          ("upd_done", "xs_done", "cr_done", "gram_done", "kt_done"))
        w_ready, gq_used, xk_used, s_added, xs_used, cr_used, conv_done, o_ready = (sem(n) for n in (
            "w_ready", "gq_used", "xk_used", "s_added", "xs_used", "cr_used", "conv_done", "o_ready"))
        proj_used, raw_ready, act_done, w_copied, kt_copied, gram_copied, bd_ready, c_ready = (sem(n) for n in (
            "proj_used", "raw_ready", "act_done", "w_copied", "kt_copied", "gram_copied", "bd_ready", "c_ready"))
        prod_ready, kb_ready, v_ready, cross_ready, dec_ready = (sem(n) for n in (
            "prod_ready", "kb_ready", "v_ready", "cross_ready", "dec_ready"))
        xn_in = [sem("xn_in0"), sem("xn_in1")]
        bt_in, o_out = sem("bt_in"), sem("o_out")
        own_sem = {e: sem("own_" + e) for e in ("act", "dve", "pool")}

        class At:

            def __init__(self, it, q):
                self.it, self.q = it, q
                self.m = q % MCH
                self.par = (q // MCH) % 2
                self.t0 = self.m * CT

            def n(self, per, k, back=0):
                return self.it * (2 * MCH * per) + ((self.q + 1 - back) * per + k)

            def w(self, per, k, back=0):
                return self.it * (2 * per) + ((self.q // MCH + 1 - back) * per + k)

            def next(self):
                return At(self.it, self.q + 1)

        def init(*engine_sems):
            for e, s, per in engine_sems:
                e.sem_inc(s, per)

        with nc.Block() as block:
            @block.sync
            def _(sp):
                for dst, src in ((w_q, wq), (w_k, wk), (w_v, wv), (w_a, wa)):
                    sp.dma_start(dst[:, :, :], src.rearrange("(k p) n -> p k n", p=P)).then_inc(loaded, 16)
                sp.dma_start(id_sb[:, :], ident).then_inc(loaded, 16)
                sp.dma_start(rmask[:, :, :, :], row_mask).then_inc(loaded, 16)
                sp.dma_start(b_a[:, :], ba).then_inc(loaded, 16)
                sp.dma_start(c_w[:, 0:2 * HP, :], cw_qk).then_inc(loaded, 16)
                sp.dma_start(c_w[:, 2 * HP:, :], cw_v).then_inc(loaded, 16)
                sp.dma_start(c_b[:, 0:2 * HP], cb_qk).then_inc(loaded, 16)
                sp.dma_start(c_b[:, 2 * HP:], cb_v).then_inc(loaded, 16)
                for w in range(2):
                    sp.dma_start(xn_w[:, w, :, :], xn_d[w].rearrange("p k b t -> p k (b t)")).then_inc(xn_in[w], 16)
                for hh in range(2):
                    sp.dma_start(btk[64 * hh:64 * hh + 64, :, :].rearrange("p c t -> p (c t)"),
                                 betak_d[0, hh:hh + 1].rearrange("h j b t -> h (j b t)").to_broadcast([DK, NC_ * WT]))\
                        .then_inc(bt_in, 16)
                sp.dma_start(bt[:, :, :, :].rearrange("p h c t -> p (h c t)"),
                             beta_d[0:1].rearrange("w h j b t -> w (h j b t)").to_broadcast([P, 2 * NC_ * WT]))\
                    .then_inc(bt_in, 16)
                sp.wait_ge(loaded, 11 * 16)
                sp.sem_inc(o_out, 16)

            @block.gpsimd
            def _(pool):
                pool.memset(S[:, :, :], 0.0)
                pool.memset(W[:, :, :, :], 0.0)
                pool.memset(k_rows[:, :, :, :], 0.0)
                pool.memset(bd_k[:, :, :, :], 0.0)
                pool.memset(dec[:, :, :, :, :], 1.0)
                pool.memset(dec_c[:, :, :, :], 1.0).then_inc(zeroed, 1)
                init((pool, prod_ready, 4), (pool, kb_ready, 1), (pool, v_ready, 1), (pool, cross_ready, 1),
                     (pool, dec_ready, 1))

            @block.vector
            def _(dve):
                for hh in range(2):
                    dve.memset(ones[64 * hh:64 * hh + 64, hh, :], 1.0)
                    dve.memset(ones[64 * (1 - hh):64 * (1 - hh) + 64, hh, :], 0.0)
                dve.memset(halo[:, :, :, :], 0.0)
                dve.memset(bd_qk[:, :, :, :, :], 0.0).then_inc(zeroed, 1)
                init((dve, w_ready, 4), (dve, gq_used, 4), (dve, xk_used, 3), (dve, s_added, 8), (dve, xs_used, 4),
                     (dve, cr_used, 8), (dve, conv_done, NCONV), (dve, o_ready, 1))

            @block.scalar
            def _(act):
                init((act, proj_used, NT), (act, raw_ready, NCONV), (act, act_done, NCONV), (act, w_copied, 8),
                     (act, kt_copied, 8), (act, gram_copied, 2), (act, bd_ready, 1), (act, c_ready, 8))

            @block.tensor
            def _(pe):
                init((pe, proj_done, NT), (pe, gq_done, 4), (pe, turned_w, 8), (pe, x_done, 3), (pe, upd_done, 8),
                     (pe, xs_done, 4), (pe, cr_done, 8), (pe, gram_done, 2), (pe, kt_done, 2))

        def pe_project(pe, at, i0, i1):
            par = at.par
            for i in range(i0, i1):
                kind, n = TILES[i]
                w_sb = {"q": w_q, "k": w_k, "v": w_v, "a": w_a}[kind]
                if i == 0:
                    pe.wait_ge(xn_in[par], (at.it + at.q // (2 * MCH)) * 16 + 16)
                pe.wait_ge(proj_used, at.w(NT, i - 1))
                for k in range(KC):
                    mm = pe.matmul(P_PS[i % 2][:, 0:TW], w_sb[:, k, n * P:(n + 1) * P], xn_w[:, par, k, :],
                                   start=(k == 0), stop=(k == KC - 1))
                mm.then_inc(proj_done, 1)

        def pe_gq(pe, at, j):
            pe.wait_ge(prod_ready, at.n(4, j + 1))
            pe.wait_ge(gq_used, at.n(4, j))
            for hh in range(2):
                mm = pe.matmul(gq_ps[:, hh, :, :].rearrange("p c n -> p (c n)"), ones[:, hh, :],
                               prod[:, j % 2, :, :].rearrange("p c n -> p (c n)"),
                               start=True, stop=True)
            mm.then_inc(gq_done, 1)

        def pe_turn_w(pe, at, j):
            pe.wait_ge(w_ready, at.n(4, j + 1))
            for half in range(2):
                if j == 0:
                    pe.wait_ge(cr_used, at.n(8, 8))
                else:
                    pe.wait_ge(w_copied, at.n(8, 2 * (j - 1) + half + 1))
                for i in range(4):
                    g = 4 * half + i
                    mm = pe.transpose(T_PS[half][:, i * P:(i + 1) * P],
                                      W[:, 4 * g:4 * g + 4, :, :].rearrange("p c h s -> p (c h s)"), id_sb[:, :])
                mm.then_inc(turned_w, 1)

        def pe_cross(pe, at, j):
            if j == 1:
                pe.wait_ge(cross_ready, at.n(1, 1))
                pe.wait_ge(xs_used, at.n(4, 1))
            else:
                pe.wait_ge(xk_used, at.n(3, j - 1))
            for g in range(NG):
                if g % 4 == 0:
                    pe.wait_ge(w_copied, at.n(8, 2 * (j - 1) + g // 4 + 1))
                mm = pe.matmul(X_PS[:, :].rearrange("p (z n) -> p z n", z=4)[:, :, g * 16:(g + 1) * 16],
                               w_rows[:, g, :],
                               cross[:, j - 1, :, :, 4 * g:4 * g + 4, :].rearrange("p k h c t -> p (k h) (c t)"),
                               start=True, stop=True)
            mm.then_inc(x_done, 1)

        def pe_state_read(pe, at, r):
            if r == 0:
                pe.wait_ge(bd_ready, at.n(1, 1))
                pe.wait_ge(s_added, at.n(8, 4, back=1))
                pe.wait_ge(xk_used, at.n(3, 3, back=1))
            elif r == 1:
                pe.wait_ge(gram_copied, at.n(2, 2))
                pe.wait_ge(s_added, at.n(8, 6, back=1))
            else:
                pe.wait_ge(s_added, at.n(8, 8, back=1))
            for i in range(8):
                c = 8 * r + i
                mm = pe.matmul(XS_PS[r][:, i * 64:(i + 1) * 64], S[:, c, :],
                               bd_qk[:, c, :, :, :].rearrange("p h k t -> p (h k t)"), start=True, stop=True)
            mm.then_inc(xs_done, 1)

        def pe_decay(pe, at, r):
            pe.wait_ge(c_ready, at.n(8, r + 1))
            if r == 0:
                pe.wait_ge(kt_copied, at.n(8, 8, back=1))
                pe.wait_ge(xs_used, at.n(4, 2))
            elif r < 3:
                pe.wait_ge(xs_used, at.n(4, r + 2))
            else:
                pe.wait_ge(cr_used, at.n(8, r - 2))
            for i in range(4):
                mm = pe.transpose(CR_PS[r % 3][:, i * P:(i + 1) * P],
                                  c_exp[:, 4 * (r % 2) + i, :, :].rearrange("p h k -> p (h k)"), id_sb[:, :])
            mm.then_inc(cr_done, 1)

        def pe_k_rows(pe, at, half):
            if half == 0:
                pe.wait_ge(cr_used, at.n(8, 7))
            else:
                pe.wait_ge(kt_copied, at.n(8, 4))
            for i in range(4):
                g = 4 * half + i
                mm = pe.transpose(M_PS[:, i * P:(i + 1) * P],
                                  bd_k[:, 4 * g:4 * g + 4, :, :].rearrange("p c h s -> p (c h s)"), id_sb[:, :])
            mm.then_inc(kt_done, 1)

        def pe_gram(pe, at, half, first=False):
            if half == 0:
                pe.wait_ge(bd_ready, at.n(1, 1))
                if not first:
                    pe.wait_ge(kt_copied, at.n(8, 8, back=1))
            else:
                pe.wait_ge(gram_copied, at.n(2, 1))
            for kind, src in enumerate((Kb, Qw)):
                for i in range(4):
                    g = 4 * half + i
                    mm = pe.matmul(M_PS[:, kind * 256 + i * 64:kind * 256 + (i + 1) * 64],
                                   bd_k[:, 4 * g:4 * g + 4, :, :].rearrange("p c h s -> p (c h s)"),
                                   src[:, at.par, 4 * g:4 * g + 4, at.t0:at.t0 + CT], start=True, stop=True)
            mm.then_inc(gram_done, 1)

        def pe_update(pe, at, f):
            b4, half = f % 4, f // 4
            if f == 0:
                pe.wait_ge(w_copied, at.n(8, 8))
            elif f == 2:
                pe.wait_ge(gram_copied, at.next().n(2, 2))
            elif f > 2:
                pe.wait_ge(s_added, at.n(8, f - 2))
            for i in range(4):
                g = 4 * half + i
                mm = pe.matmul(UP_PS[f % 3][:, i * P:(i + 1) * P], k_rows[:, g, b4, :], w_rows[:, g, :], start=True, stop=True)
            mm.then_inc(upd_done, 1)

        def pe_chunk(pe, at):
            nxt, nwin = at.next(), At(at.it, (at.q // MCH + 1) * MCH)
            tiles = [(FIRST[4 * at.m + j], FIRST[4 * at.m + j + 1]) for j in range(4)]
            for r in range(8):
                pe_decay(pe, at, r)
                if r in (2, 5):
                    a = tiles[0][0] + (r // 3)
                    pe_project(pe, nwin, a, a + 1)
            for j in range(4):
                a, b_ = tiles[j]
                if j == 0:
                    a += 2
                mid = min(a + (2 if j == 3 else 1), b_)
                pe_project(pe, nwin, a, mid)
                if j < 2:
                    pe_k_rows(pe, at, j)
                if j == 3:
                    pe_gram(pe, nxt, 0)
                    pe_project(pe, nwin, mid, b_)
                    pe_gram(pe, nxt, 1)
                pe_turn_w(pe, at, j)
                if j < 3:
                    pe_project(pe, nwin, mid, b_)
                    pe_cross(pe, at, j + 1)
                    pe_gq(pe, at, j + 1)
            for f in range(8):
                pe_update(pe, at, f)
                if f == 6:
                    pe_state_read(pe, nxt, 0)
            pe_state_read(pe, nxt, 1)
            pe_state_read(pe, nxt, 2)
            pe_state_read(pe, nxt, 3)
            pe_gq(pe, nxt, 0)

        def act_project(act, own, at, i0, i1):
            par = at.par
            for i in range(i0, i1):
                kind, n = TILES[i]
                act.wait_ge(proj_done, at.w(NT, i + 1))
                ps = P_PS[i % 2][:, 0:TW].rearrange("p (b t) -> p b t", b=B)
                if kind == "a":
                    j, hh = n // 2, n % 2
                    act.wait_ge(dec_ready, at.n(1, 0))
                    nc.scalar.activation(Aw[:, par, hh, j * B:(j + 1) * B, :], ps, ACT.Sigmoid,
                                         bias=b_a[:, n:n + 1]).then_inc(proj_used, 1)
                    continue
                s = i % SLOTS
                if i >= SLOTS:
                    act.wait_ge(conv_done, at.w(NCONV, i - SLOTS + 1))
                else:
                    act.wait_ge(conv_done, at.w(NCONV, NCONV - SLOTS + i + 1, back=1))
                own.run(nc.scalar.activation(raw[:, s, :, TAPS - 1:], ps, ACT.Copy))
                own.run(nc.scalar.activation(raw[:, s, :, 0:TAPS - 1], halo[:, i, :, :], ACT.Copy))
                nc.scalar.activation(conv[:, s, :, :], ps, ACT.Identity, bias=c_b[:, i:i + 1],
                                     scale=c_w[:, i, TAPS - 1:TAPS]).then_inc(proj_used, 1)
                nc.scalar.activation(halo[:, i, :, :], raw[:, s, :, WT:], ACT.Copy).then_inc(raw_ready, 1)

        def act_silu(act, at, i0, i1):
            par = at.par
            for i in range(i0, min(i1, NCONV)):
                kind, n = TILES[i]
                act.wait_ge(conv_done, at.w(NCONV, i + 1))
                if kind == "v":
                    dst = Vw[:, par, n % 2, n // 2 * B:(n // 2 + 1) * B, :]
                else:
                    dst = (Qw if kind == "q" else Kw)[:, par, n * B:(n + 1) * B, :]
                nc.scalar.activation(dst, conv[:, i % SLOTS, :, :], ACT.Silu).then_inc(act_done, 1)

        def act_w(act, at, j):
            for half in range(2):
                act.wait_ge(turned_w, at.n(8, 2 * j + half + 1))
                nc.scalar.activation(w_rows[:, 4 * half:4 * half + 4, :],
                                     T_PS[half][:, :].rearrange("p (g n) -> p g n", g=4), ACT.Copy)\
                    .then_inc(w_copied, 1)

        def act_k_rows(act, at, half):
            act.wait_ge(kt_done, at.n(2, half + 1))
            for b4 in range(4):
                rows = slice(32 * b4, 32 * b4 + 32)
                nc.scalar.activation(k_rows[rows, 4 * half:4 * half + 4, b4, :],
                                     M_PS[rows, :].rearrange("p (g n) -> p g n", g=4), ACT.Copy).then_inc(kt_copied, 1)

        def act_gram(act, at, half):
            act.wait_ge(gram_done, at.n(2, half + 1))
            act.wait_ge(cross_ready, at.n(1, 0))
            nc.scalar.activation(gram[:, :, 16 * half:16 * half + 16, :].rearrange("p k c t -> p k (c t)"),
                                 M_PS[:, :].rearrange("p (k n) -> p k n", k=2), ACT.Copy).then_inc(gram_copied, 1)

        def act_block_diag(act, own, at, first=False):
            par, t0 = at.par, at.t0
            act.wait_ge(kb_ready, at.w(1, 1))
            if not first:
                act.wait_ge(xs_done, at.n(4, 4, back=1))
                act.wait_ge(kt_done, at.n(2, 2, back=1))
            for hh in range(2):
                rows = slice(64 * hh, 64 * hh + 64)
                own.run(nc.scalar.activation(bd_qk[rows, :, hh, 0, :], Kb[rows, par, :, t0:t0 + CT], ACT.Copy))
                own.run(nc.scalar.activation(bd_qk[rows, :, hh, 1, :], Qw[rows, par, :, t0:t0 + CT], ACT.Copy))
                ins = nc.scalar.activation(bd_k[rows, :, hh, :], Kw[rows, par, :, t0:t0 + CT], ACT.Copy)
                own.run(ins) if hh == 0 else ins.then_inc(bd_ready, 1)

        def act_expand(act, at, r):
            if r == 0:
                act.wait_ge(dec_ready, at.n(1, 1))
            act.wait_ge(cr_done, at.n(8, r + 7, back=1) if r < 2 else at.n(8, r - 1))
            src = dec_c[:, :, 4 * r:4 * r + 4, CT:CT + 1].rearrange("p h c o -> p c h o")
            nc.scalar.activation(c_exp[:, 4 * (r % 2):4 * (r % 2) + 4, :, :], src.to_broadcast([P, 4, 2, DK]), ACT.Copy)\
                .then_inc(c_ready, 1)

        def act_chunk(act, own, at):
            nxt, nwin = at.next(), At(at.it, (at.q // MCH + 1) * MCH)
            f = [FIRST[4 * at.m + j] for j in range(5)]
            prev = FIRST[4 * at.m - 1] if at.m else 0
            own.restart()
            for r in range(2, 8):
                act_expand(act, at, r)
            if at.m:
                act_silu(act, nwin, prev, f[0])
            for j in range(4):
                if j:
                    act_silu(act, nwin, f[j - 1], f[j])
                a, b_ = f[j], f[j + 1]
                mid = min(a + (3, 1, 1, 2)[j], b_)
                act_project(act, own, nwin, a, mid)
                if j < 2:
                    act_k_rows(act, at, j)
                if j == 3:
                    act_gram(act, nxt, 0)
                    act_gram(act, nxt, 1)
                act_w(act, at, j)
                if j < 3:
                    act_project(act, own, nwin, mid, b_)
                if j == 2:
                    act_block_diag(act, own, nxt)
            act_project(act, own, nwin, mid, b_)
            act_expand(act, nxt, 0)
            act_expand(act, nxt, 1)

        def pool_products(pool, own, at, j, first=False):
            par, t0, z = at.par, at.t0 + j * ST, j % 2
            if j == 0 and not first:
                pool.wait_ge(gq_done, at.n(4, -1))
            elif j >= 2:
                pool.wait_ge(gq_done, at.n(4, j - 1))
            elif j == 1 and not first:
                pool.wait_ge(gq_done, at.n(4, 0))
            for t in range(ST):
                ins = pool.tensor_tensor(prod[:, z, :, QO[t]:QO[t] + t + 1],
                                         Qw[:, par, :, t0 + t:t0 + t + 1].to_broadcast([P, NC_, t + 1]),
                                         Kw[:, par, :, t0:t0 + t + 1], ALU.mult)
                if t == 0:
                    own.run(ins)
                    continue
                own.run(ins)
                ins = pool.tensor_tensor(prod[:, z, :, GO[t]:GO[t] + t],
                                         Kb[:, par, :, t0 + t:t0 + t + 1].to_broadcast([P, NC_, t]),
                                         Kw[:, par, :, t0:t0 + t], ALU.mult)
                own.run(ins) if t < ST - 1 else ins.then_inc(prod_ready, 1)

        def pool_cross(pool, own, at, first=False):
            pool.wait_ge(gram_copied, at.n(2, 2))
            if not first:
                pool.wait_ge(x_done, at.n(3, 3, back=1))
            for j in range(1, NSUB):
                for kind in range(2):
                    for hh in range(2):
                        src = gram[:, kind, :, j * ST:(j + 1) * ST].rearrange("p (g b) t -> p g b t", b=4)
                        mask = rmask[:, j - 1, hh, :].rearrange("p (o b q) -> p o b q", o=1, q=1)
                        ins = pool.tensor_tensor(cross[:, j - 1, kind, hh, :, :].rearrange("p (g b) t -> p g b t", b=4),
                                                 src, mask.to_broadcast([P, NG, 4, ST]), ALU.mult)
                        last = (j, kind, hh) == (NSUB - 1, 1, 1)
                        ins.then_inc(cross_ready, 1) if last else own.run(ins)

        def pool_decays(pool, own, at, first=False):
            par, t0 = at.par, at.t0
            pool.wait_ge(proj_used, at.w(NT, NT))
            if not first:
                pool.wait_ge(w_ready, at.n(4, 4, back=1))
                pool.wait_ge(xk_used, at.n(3, 3, back=1))
                pool.wait_ge(c_ready, at.n(8, 8, back=1))
            for hh in range(2):
                a = Aw[:, par, hh, :, t0:t0 + CT].rearrange("p c (j t) -> p c j t", t=ST)
                for t in range(ST):
                    own.run(pool.tensor_tensor(dec[:, hh, :, :, t + 1], dec[:, hh, :, :, t], a[:, :, :, t], ALU.mult))
            dc = dec_c[:, :, :, :].rearrange("p h c n -> p (h c) n")
            ds = dec[:, :, :, :, :].rearrange("p h c j n -> p (h c) j n")
            for j in range(NSUB):
                ins = pool.tensor_tensor(dc[:, :, j * ST + 1:(j + 1) * ST + 1], ds[:, :, j, 1:],
                                         dc[:, :, j * ST:j * ST + 1].to_broadcast([P, 2 * NC_, ST]), ALU.mult)
                own.run(ins) if j < NSUB - 1 else ins.then_inc(dec_ready, 1)

        def pool_beta_k(pool, own, at):
            pool.wait_ge(bt_in, at.w(48, 0))
            pool.wait_ge(act_done, at.w(NCONV, 2 * HP))
            pool.tensor_tensor(Kb[:, at.par, :, :], Kw[:, at.par, :, :], btk[:, :, :], ALU.mult).then_inc(kb_ready, 1)
            pool.wait_ge(kb_ready, at.w(1, 1))

        def pool_beta_v(pool, own, at):
            pool.wait_ge(act_done, at.w(NCONV, NCONV))
            v = Vw[:, at.par, :, :, :].rearrange("p h c t -> p (h c t)")
            pool.tensor_tensor(v, v, bt[:, :, :, :].rearrange("p h c t -> p (h c t)"), ALU.mult).then_inc(v_ready, 1)

        def pool_chunk(pool, own, at):
            nxt, nwin = at.next(), At(at.it, (at.q // MCH + 1) * MCH)
            own.restart()
            for j in range(1, 4):
                pool_products(pool, own, at, j)
                if at.m == 1 and j == 3:
                    pool_beta_v(pool, own, nwin)
            if at.m == 0:
                pool_beta_k(pool, own, nwin)
            pool_products(pool, own, nxt, 0)
            pool_decays(pool, own, nxt)
            pool_cross(pool, own, nxt)

        def dve_conv(dve, own, at, i0, i1):
            for i in range(i0, min(i1, NCONV)):
                s = i % SLOTS
                dve.wait_ge(raw_ready, at.w(NCONV, i + 1))
                for tap in (2, 1, 0):
                    ins = dve.scalar_tensor_tensor(out=conv[:, s, :, :], in0=raw[:, s, :, tap:tap + WT],
                                                   scalar=c_w[:, i, tap:tap + 1], in1=conv[:, s, :, :],
                                                   op0=ALU.mult, op1=ALU.add)
                    own.run(ins) if tap else ins.then_inc(conv_done, 1)

        def w_view(s0, s1):
            return W[:, :, :, s0:s1].rearrange("p c h s -> p h c s")

        def dve_start(dve, own, at):
            par, t0 = at.par, at.t0
            dve.wait_ge(dec_ready, at.n(1, 1))
            if at.m == 0:
                dve.wait_ge(v_ready, at.w(1, 1))
                dve.wait_ge(o_out, at.w(16, 0))
            for r in range(4):
                dve.wait_ge(xs_done, at.n(4, r + 1))
                ps = XS_PS[r][:, :].rearrange("p (c h k t) -> p h c k t", c=8, h=2, k=2)
                cs = slice(8 * r, 8 * r + 8)
                own.run(dve.tensor_tensor(xs_tmp[:, :, cs, :], ps[:, :, :, 0, :], dec_c[:, :, cs, 0:CT], ALU.mult))
                dve.tensor_tensor(O[:, :, cs, t0:t0 + CT], ps[:, :, :, 1, :], dec_c[:, :, cs, 1:], ALU.mult)\
                    .then_inc(xs_used, 1)
            v = Vw[:, par, :, :, t0:t0 + CT]
            own.run(dve.tensor_tensor(v, v, xs_tmp[:, :, :, :], ALU.add))
            for r in range(8):
                dve.wait_ge(cr_done, at.n(8, r + 1))
                s = S[:, 4 * r:4 * r + 4, :]
                dve.tensor_tensor(s, s, CR_PS[r % 3][:, :].rearrange("p (c v) -> p c v", c=4), ALU.mult)\
                    .then_inc(cr_used, 1)

        def dve_sub(dve, own, at, j):
            par, t0 = at.par, at.t0 + j * ST
            v = Vw[:, par, :, :, t0:t0 + ST]
            x = X_PS[:, :].rearrange("p (k h c t) -> p k h c t", k=2, h=2, t=ST)
            if j == 0:
                own.run(dve.tensor_copy(TB[:, :, :, :, ST - 1], v))
            else:
                dve.wait_ge(x_done, at.n(3, j))
                own.run(dve.tensor_tensor(tmp, x[:, 0], dec[:, :, :, j, 0:ST], ALU.mult))
                own.run(dve.tensor_tensor(TB[:, :, :, :, ST - 1], v, tmp, ALU.add))
                dve.tensor_tensor(QB[:, :, :, :, ST], x[:, 1], dec[:, :, :, j, 1:], ALU.mult).then_inc(xk_used, 1)
                w = w_view(0, j * ST)
                own.run(dve.tensor_tensor(w, w, dec[:, :, :, j, ST:ST + 1].to_broadcast([P, 2, NC_, j * ST]), ALU.mult))
            a = Aw[:, par, :, :, t0:t0 + ST]
            dve.wait_ge(gq_done, at.n(4, j + 1))
            rows = [TB[:, :, :, 0, ST - 1:ST], Wh[:, :, :, 0:2], Wh[:, :, :, 2:5], w_view(j * ST, (j + 1) * ST)]
            for t in range(1, ST):
                old = rows[t - 1]
                own.run(dve.tensor_tensor(TB[:, :, :, t, ST - 1 - t:ST - 1], gq_ps[:, :, :, GO[t]:GO[t] + t], old, ALU.mult))
                own.run(dve.tensor_tensor(rows[t][:, :, :, 0:t], old, a[:, :, :, t:t + 1].to_broadcast([P, 2, NC_, t]),
                                          ALU.mult))
                ins = dve.tensor_reduce(rows[t][:, :, :, t], TB[:, :, :, t, ST - 1 - t:], AX.X, ALU.add)
                if t < ST - 1:
                    own.run(ins)
                else:
                    ins.then_inc(w_ready, 1)
                    dve.wait_ge(w_ready, at.n(4, j + 1))
            for t in range(ST):
                ins = dve.tensor_tensor(QB[:, :, :, t, ST - 1 - t:ST], gq_ps[:, :, :, QO[t]:QO[t] + t + 1], rows[t], ALU.mult)
                if t < ST - 1:
                    own.run(ins)
                else:
                    ins.then_inc(gq_used, 1)
                    dve.wait_ge(gq_used, at.n(4, j + 1))
            o = O[:, :, :, t0:t0 + ST]
            if j == 0:
                own.run(dve.tensor_copy(QB[:, :, :, :, ST], o))
            else:
                own.run(dve.tensor_tensor(QB[:, :, :, :, ST], QB[:, :, :, :, ST], o, ALU.add))
            for t in range(ST):
                ins = dve.tensor_reduce(o[:, :, :, t], QB[:, :, :, t, ST - 1 - t:], AX.X, ALU.add)
                ins.then_inc(o_ready, 1) if (j, t) == (NSUB - 1, ST - 1) else own.run(ins)

        def dve_add(dve, own, at, f):
            b4, half = f % 4, f // 4
            dve.wait_ge(upd_done, at.n(8, f + 1))
            s = S[:, 16 * half:16 * half + 16, :].rearrange("p (g b) v -> p g b v", b=4)[:, :, b4, :]
            dve.tensor_tensor(s, s, UP_PS[f % 3][:, :].rearrange("p (g v) -> p g v", g=4), ALU.add).then_inc(s_added, 1)

        def dve_chunk(dve, own, at):
            nwin = At(at.it, (at.q // MCH + 1) * MCH)
            own.restart()
            dve_start(dve, own, at)
            for j in range(4):
                dve_sub(dve, own, at, j)
                if j < 3:
                    dve_conv(dve, own, nwin, FIRST[4 * at.m + j], FIRST[4 * at.m + j + 1])
            a, b_ = FIRST[4 * at.m + 3], FIRST[4 * at.m + 4]
            dve_conv(dve, own, nwin, a, b_)
            dve.wait_ge(cr_used, at.n(8, 8))
            for f in range(8):
                dve_add(dve, own, at, f)
            dve.wait_ge(s_added, at.n(8, 8))

        FILL = At(0, 0)
        clear_after(nc, ctx, sems)
        with nc.Block() as block:
            @block.sync
            def _(sp):
                with sp.Fori(0, NW // 2) as it:
                    for wq_ in range(2):
                        at = At(it, wq_ * MCH)
                        sp.wait_ge(proj_done, at.w(NT, NT))
                        sp.dma_start(xn_w[:, wq_, :, :].rearrange("p k n -> p (k n)"),
                                     xn_d[bass.ds(it * 2 + (wq_ + 2), 1)].rearrange("o p k b t -> (o p) (k b t)"))\
                            .then_inc(xn_in[wq_], 16)
                        sp.wait_ge(v_ready, at.w(1, 1))
                        sp.wait_ge(kb_ready, at.w(1, 1))
                        for hh in range(2):
                            sp.dma_start(btk[64 * hh:64 * hh + 64, :, :].rearrange("p c t -> p (c t)"),
                                         betak_d[bass.ds(it * 2 + (wq_ + 1), 1), hh].rearrange("o j b t -> o (j b t)")
                                         .to_broadcast([DK, NC_ * WT])).then_inc(bt_in, 16)
                        sp.dma_start(bt[:, :, :, :].rearrange("p h c t -> p (h c t)"),
                                     beta_d[bass.ds(it * 2 + (wq_ + 1), 1)].rearrange("o h j b t -> o (h j b t)")
                                     .to_broadcast([P, 2 * NC_ * WT])).then_inc(bt_in, 16)
                        sp.wait_ge(o_ready, At(it, wq_ * MCH + 1).n(1, 1))
                        sp.dma_start(o_d[bass.ds(it * 2 + wq_, 1)].rearrange("o p h c t -> (o p) (h c t)"),
                                     O[:, :, :, :].rearrange("p h c t -> p (h c t)")).then_inc(o_out, 16)
                sp.wait_ge(o_out, 16 * (NW + 1))
                for s in xn_in:
                    sp.wait_ge(s, 16 * (NW // 2 + 1))
                sp.wait_ge(bt_in, 48 * (NW + 1))

            @block.tensor
            def _(pe):
                pe_project(pe, FILL, 0, NT)
                pe_gram(pe, FILL, 0, first=True)
                pe_gram(pe, FILL, 1)
                pe_gq(pe, FILL, 0)
                for r in range(4):
                    pe_state_read(pe, FILL, r)
                with pe.Fori(0, NW // 2) as it:
                    for q in range(2 * MCH):
                        pe_chunk(pe, At(it, q))

            @block.scalar
            def _(act):
                own = Chain(act, own_sem["act"])
                for i in range(0, NT, 4):
                    act_project(act, own, FILL, i, i + 4)
                    act_silu(act, FILL, i, i + 4)
                act_block_diag(act, own, FILL, first=True)
                act_gram(act, FILL, 0)
                act_gram(act, FILL, 1)
                act_expand(act, FILL, 0)
                act_expand(act, FILL, 1)
                own.restart()
                with act.Fori(0, NW // 2) as it:
                    for q in range(2 * MCH):
                        act_chunk(act, own, At(it, q))

            @block.gpsimd
            def _(pool):
                own = Chain(pool, own_sem["pool"])
                pool_beta_k(pool, own, FILL)
                pool_products(pool, own, FILL, 0, first=True)
                pool_beta_v(pool, own, FILL)
                pool_decays(pool, own, FILL, first=True)
                pool_cross(pool, own, FILL, first=True)
                own.restart()
                with pool.Fori(0, NW // 2) as it:
                    for q in range(2 * MCH):
                        pool_chunk(pool, own, At(it, q))

            @block.vector
            def _(dve):
                own = Chain(dve, own_sem["dve"])
                dve_conv(dve, own, FILL, 0, NCONV)
                own.restart()
                with dve.Fori(0, NW // 2) as it:
                    for q in range(2 * MCH):
                        dve_chunk(dve, own, At(it, q))


def gate_and_project(nc, wg, wo, ln_w, ln_b, w_centre, xn_d, xr_d, o_d, x2_d, xf_d):
    HG = H // 2
    with ExitStack() as ctx:
        def sb(name, shape, dt=F32):
            return ctx.enter_context(nc.sbuf_tensor("g_" + name, shape, dt))

        sems = []

        def sem(name):
            sems.append(ctx.enter_context(nc.semaphore("g_" + name)))
            return sems[-1]

        w_g, w_o = sb("wg", [P, KC, H * DV]), sb("wo", [P, H, C])
        w_cen, mean_v, mean_c = sb("w_cen", [P, P]), sb("mean_v", [P, P]), sb("mean_c", [P, P])
        lw, lb, eps = sb("lw", [P, 1]), sb("lb", [P, 1]), sb("eps", [P, 1])
        o_in = sb("o_in", [P, 2, HG, 2 * TW])
        xn_in = sb("xn_in", [P, 2, KC, TW])
        xr_in = sb("xr_in", [P, 2, KC, TW])
        sq, std, rstd = sb("sq", [P, HG, 2 * TW]), sb("std", [P, HG, 2 * TW]), sb("rstd", [P, 2 * TW])
        dn, z, sg = sb("dn", [P, HG, 2 * TW]), sb("z", [P, 2, 2 * TW]), sb("sg", [P, 2, 2 * TW])
        og = sb("og", [P, 2, HG, 2 * TW])
        x2, xf = sb("x2", [P, 2, KC, TW]), sb("xf", [P, 2, KC, TW])
        cenx, sqx = sb("cenx", [P, KC, TW]), sb("sqx", [P, KC, TW])
        stdx, rstdx = sb("stdx", [P, TW]), sb("rstdx", [P, TW])
        ps = [ctx.enter_context(nc.psum_tensor(f"g_ps{i}", [P, 512], F32)) for i in range(8)]
        C_PS, VG_PS, M_PS, Y_PS = ps[0:4], ps[4:6], ps[6], ps[7]

        names = ("loaded", "consts", "cen_done", "sq_done", "var_done", "std_done", "dn_done", "gate_done", "sg_done",
                 "z_done", "og_done", "y_done", "x2_done", "mean_done", "cenx_done", "sqx_done", "varx_done",
                 "stdx_done", "xf_done", "own_act", "own_dve")
        (loaded, consts, cen_done, sq_done, var_done, std_done, dn_done, gate_done, sg_done, z_done, og_done, y_done,
         x2_done, mean_done, cenx_done, sqx_done, varx_done, stdx_done, xf_done, own_act, own_dve) = map(sem, names)
        front_in = [sem("front_in0"), sem("front_in1")]
        back_in = [sem("back_in0"), sem("back_in1")]
        stored = [sem("stored0"), sem("stored1")]

        class At:

            def __init__(self, it, q):
                self.it, self.q, self.u = it, q, q % 2

            def n(self, per, k, back=0):
                return self.it * (2 * per) + ((self.q + 1 - back) * per + k)

            def d(self, per, back=0):
                return (self.it + (self.q // 2 + 1 - back)) * per

        def window(d, at):
            return d[bass.ds(at.it * 2 + at.q, 1)]

        def sp_front(sp, at, first=False):
            if not first:
                sp.wait_ge(gate_done, at.n(HG, 0, back=1))
            sp.dma_start(o_in[:, at.u, :, :].rearrange("p g n -> p (g n)"),
                         window(o_d, at).rearrange("o p h c t -> (o p) (h c t)")).then_inc(front_in[at.u], 16)
            sp.dma_start(xn_in[:, at.u, :, :].rearrange("p k n -> p (k n)"),
                         window(xn_d, at).rearrange("o p k b t -> (o p) (k b t)")).then_inc(front_in[at.u], 16)

        def sp_back(sp, at, first=False):
            if not first:
                sp.wait_ge(x2_done, at.n(1, 0, back=1))
            sp.dma_start(xr_in[:, at.u, :, :].rearrange("p k n -> p (k n)"),
                         window(xr_d, at).rearrange("o p k b t -> (o p) (k b t)")).then_inc(back_in[at.u], 16)

        def sp_store(sp, at):
            for s, src, d in ((x2_done, x2, x2_d), (xf_done, xf, xf_d)):
                sp.wait_ge(s, at.n(1, 1))
                sp.dma_start(window(d, at).rearrange("o p k b t -> (o p) (k b t)"),
                             src[:, at.u, :, :].rearrange("p k n -> p (k n)")).then_inc(stored[at.u], 16)

        def pe_centre(pe, at):
            pe.wait_ge(front_in[at.u], at.d(32))
            for g in range(HG):
                pe.wait_ge(dn_done, at.n(HG, g + 1, back=1))
                pe.matmul(C_PS[g][:, :], w_cen[:, :], o_in[:, at.u, g, :], start=True, stop=True).then_inc(cen_done, 1)

        def pe_var(pe, at, g):
            pe.wait_ge(sq_done, at.n(HG, g + 1))
            if g < 2:
                pe.wait_ge(sg_done, at.n(HG, g + 3, back=1))
            else:
                pe.wait_ge(std_done, at.n(HG, g - 1))
            pe.matmul(VG_PS[g % 2][:, :], mean_v[:, :], sq[:, g, :], start=True, stop=True).then_inc(var_done, 1)

        def pe_gate(pe, at, g):
            if g < 2:
                pe.wait_ge(std_done, at.n(HG, g + 3))
            else:
                pe.wait_ge(sg_done, at.n(HG, g - 1))
            for i in range(2):
                h = 2 * (2 * (g % 2) + i) + g // 2
                for k in range(KC):
                    mm = pe.matmul(VG_PS[g % 2][:, i * TW:(i + 1) * TW], w_g[:, k, h * DV:(h + 1) * DV], xn_in[:, at.u, k, :],
                                   start=(k == 0), stop=(k == KC - 1))
            mm.then_inc(gate_done, 1)

        def pe_out(pe, at):
            pe.wait_ge(x2_done, at.n(1, 0))
            for m in range(KC):
                for n in range(H):
                    g, i = n // 2, n % 2
                    h = 2 * (2 * (g % 2) + i) + g // 2
                    pe.wait_ge(og_done, at.n(HG, g + 1))
                    mm = pe.matmul(Y_PS[:, m * TW:(m + 1) * TW], w_o[:, h, m * P:(m + 1) * P],
                                   og[:, at.u, g, i * TW:(i + 1) * TW], start=(n == 0), stop=(n == H - 1))
            mm.then_inc(y_done, 1)

        def pe_stat(pe, at, which):
            if which == "mean":
                pe.wait_ge(x2_done, at.n(1, 1))
                pe.wait_ge(stdx_done, at.n(1, 0))
            else:
                pe.wait_ge(sqx_done, at.n(1, 1))
                pe.wait_ge(cenx_done, at.n(1, 1))
            for k in range(KC):
                mm = pe.matmul(M_PS[:, 0:TW], mean_c[:, :], x2[:, at.u, k, :] if which == "mean" else sqx[:, k, :],
                               start=(k == 0), stop=(k == KC - 1))
            mm.then_inc(mean_done if which == "mean" else varx_done, 1)

        def act_squares(act, at):
            for g in range(HG):
                act.wait_ge(cen_done, at.n(HG, g + 1))
                act.wait_ge(var_done, at.n(HG, g + 1, back=1))
                nc.scalar.activation(sq[:, g, :], C_PS[g][:, :], ACT.Square).then_inc(sq_done, 1)
            for g in range(HG):
                act.wait_ge(var_done, at.n(HG, g + 1))
                act.wait_ge(dn_done, at.n(HG, g + 1, back=1))
                nc.scalar.activation(std[:, g, :], VG_PS[g % 2][:, :], ACT.Sqrt, bias=eps[:, :]).then_inc(std_done, 1)

        def act_gates(act, at, g0=0, g1=HG):
            for g in range(g0, g1):
                act.wait_ge(gate_done, at.n(HG, g + 1))
                act.wait_ge(og_done, at.n(HG, g - 1))
                nc.scalar.activation(sg[:, g % 2, :], VG_PS[g % 2][:, :], ACT.Sigmoid).then_inc(sg_done, 1)
                act.wait_ge(dn_done, at.n(HG, g + 1))
                nc.scalar.activation(z[:, g % 2, :], dn[:, g, :], ACT.Identity, bias=lb[:, :], scale=lw[:, :])\
                    .then_inc(z_done, 1)

        def act_square(act, at):
            act.wait_ge(cenx_done, at.n(1, 1))
            act.wait_ge(varx_done, at.n(1, 0))
            nc.scalar.activation(sqx[:, :, :], cenx[:, :, :], ACT.Square).then_inc(sqx_done, 1)

        def act_std(act, at):
            act.wait_ge(varx_done, at.n(1, 1))
            act.wait_ge(xf_done, at.n(1, 0))
            nc.scalar.activation(stdx[:, :], M_PS[:, 0:TW], ACT.Sqrt, bias=eps[:, :]).then_inc(stdx_done, 1)

        def dve_normed(dve, own, at, g):
            dve.wait_ge(std_done, at.n(HG, g + 1))
            own.run(dve.reciprocal(rstd[:, :], std[:, g, :]))
            dve.wait_ge(z_done, at.n(HG, g + 1, back=1))
            dve.tensor_tensor(dn[:, g, :], C_PS[g][:, :], rstd[:, :], ALU.mult).then_inc(dn_done, 1)
            dve.wait_ge(dn_done, at.n(HG, g + 1))

        def dve_residual(dve, at):
            dve.wait_ge(y_done, at.n(1, 1))
            dve.wait_ge(back_in[at.u], at.d(16))
            dve.wait_ge(stored[at.u], at.d(32))
            dve.tensor_tensor(x2[:, at.u, :, :], Y_PS[:, :].rearrange("p (k n) -> p k n", k=KC), xr_in[:, at.u, :, :],
                              ALU.add).then_inc(x2_done, 1)
            dve.wait_ge(x2_done, at.n(1, 1))

        def dve_centre(dve, at):
            dve.wait_ge(mean_done, at.n(1, 1))
            mu = M_PS[:, 0:TW].rearrange("p (o n) -> p o n", o=1).to_broadcast([P, KC, TW])
            dve.tensor_tensor(cenx[:, :, :], x2[:, at.u, :, :], mu, ALU.subtract).then_inc(cenx_done, 1)
            dve.wait_ge(cenx_done, at.n(1, 1))

        def dve_norm(dve, own, at):
            dve.wait_ge(stdx_done, at.n(1, 1))
            own.run(dve.reciprocal(rstdx[:, :], stdx[:, :]))
            r = rstdx[:, :].rearrange("p (o n) -> p o n", o=1).to_broadcast([P, KC, TW])
            dve.tensor_tensor(xf[:, at.u, :, :], cenx[:, :, :], r, ALU.mult).then_inc(xf_done, 1)
            dve.wait_ge(xf_done, at.n(1, 1))

        FIRST = At(0, 0)
        clear_after(nc, ctx, sems)
        block = ctx.enter_context(nc.Block())

        @block.sync
        def _(sp):
            sp.dma_start(w_cen[:, :], w_centre).then_inc(loaded, 16)
            sp.dma_start(w_g[:, :, :], wg.rearrange("(k p) n -> p k n", p=P)).then_inc(loaded, 16)
            sp.dma_start(w_o[:, :, :], wo.rearrange("(h p) n -> p h n", p=P)).then_inc(loaded, 16)
            sp.dma_start(lw[:, :], ln_w).then_inc(loaded, 16)
            sp.dma_start(lb[:, :], ln_b).then_inc(loaded, 16)
            sp_front(sp, FIRST, first=True)
            sp_front(sp, At(0, 1), first=True)
            sp_back(sp, FIRST, first=True)
            with sp.Fori(0, NW // 2) as it:
                for q in range(2):
                    sp_front(sp, At(it, q + 2))
                    sp_back(sp, At(it, q + 1))
                    sp_store(sp, At(it, q))
            for u in range(2):
                sp.wait_ge(stored[u], 32 * (NW // 2 + 1))
                sp.wait_ge(front_in[u], 32 * (NW // 2 + 1))
            sp.wait_ge(back_in[0], 16 * (NW // 2 + 1))
            sp.wait_ge(back_in[1], 16 * (NW // 2))

        @block.tensor
        def _(pe):
            for s, per in ((cen_done, HG), (var_done, HG), (gate_done, HG), (y_done, 1), (mean_done, 1), (varx_done, 1)):
                pe.sem_inc(s, per)
            pe.wait_ge(loaded, 80)
            pe.wait_ge(consts, 1)
            pe_centre(pe, FIRST)
            for g in range(HG):
                pe_var(pe, FIRST, g)
            for g in range(HG):
                pe_gate(pe, FIRST, g)
            with pe.Fori(0, NW // 2) as it:
                for q in range(2):
                    at, nxt = At(it, q), At(it, q + 1)
                    pe_centre(pe, nxt)
                    for g in range(HG):
                        pe_var(pe, nxt, g)
                    pe_out(pe, at)
                    pe_stat(pe, at, "mean")
                    for g in range(HG):
                        if g == HG - 1:
                            pe_stat(pe, at, "var")
                        pe_gate(pe, nxt, g)

        @block.scalar
        def _(act):
            for s, per in ((sq_done, HG), (std_done, HG), (sg_done, HG), (z_done, HG), (sqx_done, 1), (stdx_done, 1)):
                act.sem_inc(s, per)
            act.wait_ge(loaded, 80)
            act_squares(act, FIRST)
            act_gates(act, FIRST)
            with act.Fori(0, NW // 2) as it:
                for q in range(2):
                    at, nxt = At(it, q), At(it, q + 1)
                    act_squares(act, nxt)
                    act_gates(act, nxt, 0, 2)
                    act_square(act, at)
                    act_gates(act, nxt, 2, HG)
                    act_std(act, at)

        @block.vector
        def _(dve):
            dve.memset(mean_v[:, :], 1.0 / DV)
            dve.memset(mean_c[:, :], 1.0 / C)
            dve.memset(eps[:, :], EPS).then_inc(consts, 1)
            dve.wait_ge(consts, 1)
            for s, per in ((dn_done, HG), (x2_done, 1), (cenx_done, 1), (xf_done, 1), (stored[0], 32), (stored[1], 32)):
                dve.sem_inc(s, per)
            own = Chain(dve, own_dve)
            for g in range(HG):
                dve_normed(dve, own, FIRST, g)
            with dve.Fori(0, NW // 2) as it:
                own.restart()
                for q in range(2):
                    at, nxt = At(it, q), At(it, q + 1)
                    for g in range(HG):
                        dve_normed(dve, own, nxt, g)
                        if g == 1:
                            dve_residual(dve, at)
                        if g == 2:
                            dve_centre(dve, at)
                    dve_norm(dve, own, at)

        @block.gpsimd
        def _(pool):
            pool.sem_inc(og_done, HG)

            def gated(at, first=False):
                for g in range(HG):
                    pool.wait_ge(sg_done, at.n(HG, g + 1))
                    pool.wait_ge(z_done, at.n(HG, g + 1))
                    if not first:
                        pool.wait_ge(y_done, at.n(1, 1, back=2))
                    pool.tensor_tensor(og[:, at.u, g, :], z[:, g % 2, :], sg[:, g % 2, :], ALU.mult).then_inc(og_done, 1)

            gated(FIRST, first=True)
            with pool.Fori(0, NW // 2) as it:
                for q in range(2):
                    gated(At(it, q + 1))


def local_layer(nc, lay, last, wqkv, wo, w1, b1, w2, b2, ln_g, ln_b, scales, tables, ident, mask, x_src, x_dst, x2_d, out):
    NT4 = T // P
    INNER, D, HPAIRS = H * 64, 64, H // 2
    HIDT = w2.shape[0] // P
    HID = HIDT * P

    def uses(names, size):
        at = {name: n for n, name in enumerate(names)}
        assert len(at) == len(names) and len(names) % size == 0
        return at, size, len(names) // size

    U = range(2)
    mm_uses = []
    for u in U:
        mm_uses += [(k, u, t) for t in range(NT4) for k in ("q", "k", "v")]
    mm_uses += [("pv", u, t) for u in U for t in range(NT4)]
    norm_order = [("wo", 0, 0), ("wo", 0, 1), ("wo", 1, 0), ("mean", 0), ("wo", 1, 1), ("var", 0), ("mean", 1), ("var", 1)]
    mm_uses += norm_order
    for u in U:
        mm_uses += [(k, u, i) for i in range(HIDT) for k in ("g", "a")] + [("w2", u, 0), ("w2", u, 1)]
    MM = uses(mm_uses, 2)
    SIM = uses([(u, t, r) for u in U for t in range(NT4) for r in range(2)], 2)
    tr_uses = [(k, u, t) for u in U for t in range(NT4) for k in ("qT", "kT")]
    K = 2 * NT4
    halves = lambda t: (1,) if t == 0 else (0, 1)
    for u in U:
        for k in range(K + 3):
            if 1 <= k <= K:
                tr_uses += [("pT", u, k - 1, half) for half in halves((k - 1) // 2)]
            if k >= 4 and k % 2 == 0:
                tr_uses.append(("oT", u, k // 2 - 2))
    if last:
        tr_uses += [("out", u, k) for u in U for k in range(4)]
    TR = uses(tr_uses, 2)

    with ExitStack() as ctx:
        def sb(name, shape, dt=F32):
            return ctx.enter_context(nc.sbuf_tensor(f"f{lay}_{name}", shape, dt))

        sems = []

        def sem(name):
            sems.append(ctx.enter_context(nc.semaphore(f"f{lay}_{name}")))
            return sems[-1]

        w_qkv, w_o = sb("wqkv", [P, KC, 3 * INNER]), sb("wo", [P, HPAIRS, C])
        w_1, w_2 = sb("w1", [P, KC, 2 * HID]), sb("w2", [P, HIDT, C])
        b_1, b_2 = sb("b1", [P, 2 * HIDT]), sb("b2", [P, KC])
        l_g, l_b, eps = sb("lg", [P, KC]), sb("lb", [P, KC]), sb("eps", [P, 1])
        id_sb, id16 = sb("id", [P, P]), sb("id16", [P, P], BF16)
        mask_sb = sb("mask", [P, 2 * P], BF16)
        mean_w = sb("mean_w", [P, P])
        sc = sb("sc", [P, 2, 2, D])
        cos_t, sin_t = sb("cos", [P, NT4, 2, D]), sb("sin", [P, NT4, 2, D])
        x_next = sb("x_next", [P, 2, KC, T])
        X = sb("X", [P, 2, KC, T + 1])
        V = sb("V", [P, 2, NT4, INNER])
        QZ = sb("QZ", [P, 2, 2, HPAIRS, T])
        KT = sb("KT", [P, 2, HPAIRS, T])
        qk_all = sb("qk_all", [P, 5, 2, INNER])
        qk, qkr = qk_all[:, 0:2, :, :], qk_all[:, 2:5, :, :]
        OT = qk_all[:, 0:4, :, :].rearrange("p a k n -> p (a k n)").rearrange("p (u h n) -> p u h n", u=2, h=HPAIRS)
        sqr_rot = sb("sqr_rot", [P, 2, 2 * INNER])
        sqr, rot = sqr_rot[:, 0, :], sqr_rot[:, 1, :]
        nrm = sb("nrm", [P, 2, 2 * H])
        inv = sb("inv", [P, 2, 2 * H])
        ssq = sb("ssq", [P, 2, 2 * H])
        PR = sb("PR", [P, 2, 4, 2 * P])
        PT = sb("PT", [P, 2, 4, 2, P])
        nmax = sb("nmax", [P, 2, 4])
        rsum = sb("rsum", [P, 2, 2, 4])
        rinv = sb("rinv", [P, 2, 2, 4])
        o_sb = sb("o_sb", [P, 2, INNER])
        cen = sb("cen", [P, 2, KC, T])
        std, rstd = sb("std", [P, 2, T]), sb("rstd", [P, T])
        gel = sb("gel", [P, 2, T])
        hid = sb("hid", [P, HIDT, T])
        x2 = sb("x2", [P, KC, T]) if last else None
        out_sb = sb("out_sb", [P, NT4, C]) if last else None
        SQ = sqr_rot[:, :, :].rearrange("p u (k n) -> p u k n", k=KC)

        mm_ps = [ctx.enter_context(nc.psum_tensor(f"f{lay}_mm{i}", [P, 512], F32)) for i in range(2)]
        tr_ps = [ctx.enter_context(nc.psum_tensor(f"f{lay}_tr{i}", [P, 512], F32)) for i in range(2)]
        sim_ps = [ctx.enter_context(nc.psum_tensor(f"f{lay}_sim{i}", [P, 2, 2, 2 * P], F32)) for i in range(2)]

        names = ("loaded", "loaded_late", "consts", "x_ready", "sq_done", "ssq_done", "nrm_done", "inv_done", "rope_done", "rot_used", "qk_ready",
                 "max_done", "exp_done", "pv_half", "rinv_done", "o_done", "csq_done", "cn_done", "hn_ready", "fin_done",
                 "own_act", "own_dve", "own_pool", "x2_in", "out_st")
        s = {n: sem(n) for n in names}
        x_in, x_st = [sem("x_in0"), sem("x_in1")], [sem("x_st0"), sem("x_st1")]
        mm_done, mm_free = [sem(f"mm_done{i}") for i in range(2)], [sem(f"mm_free{i}") for i in range(2)]
        sim_done, sim_free = [sem(f"sim_done{i}") for i in range(2)], [sem(f"sim_free{i}") for i in range(2)]
        tr_done, tr_free = [sem(f"tr_done{i}") for i in range(2)], [sem(f"tr_free{i}") for i in range(2)]

        EARLY, LATE = 5, 9

        class Bank:

            def __init__(self, it, table, banks, done, free, name):
                at, size, per = table
                n = at[name]
                self.ps, self.done, self.free = banks[n % size], done[n % size], free[n % size]
                self.mine = it * per + (n // size + 1)

            def claim(self, pe):
                pe.wait_ge(self.free, self.mine)

            def written(self, eng):
                eng.wait_ge(self.done, self.mine)

            def released(self, eng):
                eng.wait_ge(self.free, self.mine + 1)

        mm = lambda it, *name: Bank(it, MM, mm_ps, mm_done, mm_free, name)
        tr = lambda it, *name: Bank(it, TR, tr_ps, tr_done, tr_free, name)
        sim = lambda it, *name: Bank(it, SIM, sim_ps, sim_done, sim_free, name)

        def n(it, per, k):
            return it * per + (per + k)

        class Own:

            def __init__(self, eng, sem_):
                self.chain, self.eng = Chain(eng, sem_), eng

            def run(self, ins):
                self.chain.run(ins)

            def order(self, ins, sem_, value):
                ins.then_inc(sem_, 1)
                self.eng.wait_ge(sem_, value)

        TT, RR = 2 * NT4, 4 * NT4

        def before(u, k, step=2, per=2 * NT4):
            return (u, k - step) if k >= step else (u - 1, k - step + per) if u else (u, None)

        def pe_qkv(pe, it, u, t):
            if t == 0:
                pe.wait_ge(s["x_ready"], n(it, 2, u + 1))
            for kind, name in enumerate(("q", "k", "v")):
                b = mm(it, name, u, t)
                b.claim(pe)
                for k in range(KC):
                    off = 1 - k + t * P
                    m = pe.matmul(b.ps[:, :], X[:, u, k, off:off + P], w_qkv[:, k, kind * INNER:(kind + 1) * INNER],
                                  start=(k == 0), stop=(k == KC - 1))
                m.then_inc(b.done, 1)

        def pe_turn_qk(pe, it, u, t):
            pe.wait_ge(s["qk_ready"], n(it, TT, u * NT4 + t + 1))
            for kind, name in enumerate(("qT", "kT")):
                b = tr(it, name, u, t)
                b.claim(pe)
                for hp in range(HPAIRS):
                    m = pe.transpose(b.ps[:, hp * P:(hp + 1) * P], qkr[:, (u * NT4 + t) % 3, kind, hp * P:(hp + 1) * P], id_sb[:, :])
                m.then_inc(b.done, 1)

        def pe_sim(pe, it, u, t, r):
            if t == 0 and r == 0:
                tr(it, "qT", u, NT4 - 1).released(pe)
                tr(it, "kT", u, NT4 - 1).released(pe)
            b = sim(it, u, t, r)
            b.claim(pe)
            lo = P * halves(t)[0]
            for hh in range(2):
                for i in range(2):
                    hp = 2 * r + i
                    pe.matmul(b.ps[:, hh, i, lo:], QZ[:, u, hh, hp, t * P:(t + 1) * P],
                              KT[:, u, hp, (t - 1) * P + lo:(t + 1) * P], start=(i == 0), stop=False,
                              skip_group_check=True)
            for hh in range(2):
                for i in range(2):
                    m = pe.matmul(b.ps[:, hh, i, lo:], id16[:, :], mask_sb[:, lo:], start=False, stop=True,
                                  skip_group_check=True)
            m.then_inc(b.done, 1)

        def pe_turn_p(pe, it, u, k):
            t, r = k // 2, k % 2
            idx = u * 2 * NT4 + k
            pe.wait_ge(s["exp_done"], n(it, 4 * RR, 4 * (idx + 1)))
            for half in halves(t):
                b = tr(it, "pT", u, k, half)
                b.claim(pe)
                for i in range(4):
                    m = pe.transpose(b.ps[:, i * P:(i + 1) * P], PR[:, k % 2, i, half * P:(half + 1) * P], id_sb[:, :])
                m.then_inc(b.done, 1)

        def pe_pv(pe, it, u, k):
            t, r = k // 2, k % 2
            idx = u * 2 * NT4 + k
            for half in halves(t):
                tr(it, "pT", u, k, half).released(pe)
            b = mm(it, "pv", u, t)
            if r == 0:
                b.claim(pe)
            for hh in range(2):
                for i in range(2):
                    h = 2 * (2 * r + i) + hh
                    for half in halves(t):
                        m = pe.matmul(b.ps[:, h * D:(h + 1) * D], PT[:, k % 2, 2 * hh + i, half, :],
                                      V[:, u, t - 1 + half, h * D:(h + 1) * D],
                                      start=(half == halves(t)[0]), stop=(half == 1))
            if r == 1:
                m.then_inc(b.done, 1)
            else:
                m.then_inc(s["pv_half"], 1)

        def pe_turn_o(pe, it, u, t):
            pe.wait_ge(s["o_done"], n(it, TT, u * NT4 + t + 1))
            b = tr(it, "oT", u, t)
            b.claim(pe)
            for hp in range(HPAIRS):
                m = pe.transpose(b.ps[:, hp * P:(hp + 1) * P], o_sb[:, t % 2, hp * P:(hp + 1) * P], id_sb[:, :])
            m.then_inc(b.done, 1)

        def pe_attention(pe, it, u):
            for k in range(K + 3):
                if k < K:
                    pe_sim(pe, it, u, k // 2, k % 2)
                if 1 <= k <= K:
                    pe_turn_p(pe, it, u, k - 1)
                if 2 <= k <= K + 1:
                    pe_pv(pe, it, u, k - 2)
                if k >= 4 and k % 2 == 0:
                    pe_turn_o(pe, it, u, k // 2 - 2)

        def pe_wo(pe, it, u, m_):
            b = mm(it, "wo", u, m_)
            b.claim(pe)
            tr(it, "oT", u, NT4 - 1).released(pe)
            for hp in range(HPAIRS):
                m = pe.matmul(b.ps[:, :], w_o[:, hp, m_ * P:(m_ + 1) * P], OT[:, u, hp, :],
                              start=(hp == 0), stop=(hp == HPAIRS - 1))
            m.then_inc(b.done, 1)

        def pe_stat(pe, it, name, u):
            b = mm(it, name, u)
            b.claim(pe)
            if name == "var":
                pe.wait_ge(s["csq_done"], n(it, 2, u + 1))
            for k in range(KC):
                src = X[:, u, k, 1 - k:1 - k + T] if name == "mean" else SQ[:, u, k, :]
                m = pe.matmul(b.ps[:, :], mean_w[:, :], src, start=(k == 0), stop=(k == KC - 1))
            m.then_inc(b.done, 1)

        def pe_mlp(pe, it, u):
            pe.wait_ge(s["hn_ready"], n(it, 2, u + 1))
            for i in range(HIDT):
                for part, name in ((1, "g"), (0, "a")):
                    b = mm(it, name, u, i)
                    b.claim(pe)
                    for k in range(KC):
                        col = part * HID + i * P
                        m = pe.matmul(b.ps[:, :], w_1[:, k, col:col + P], cen[:, u, k, :], start=(k == 0), stop=(k == KC - 1))
                    m.then_inc(b.done, 1)
            for m_ in range(KC):
                b = mm(it, "w2", u, m_)
                b.claim(pe)
                mm(it, "a", u, HIDT - 1).released(pe)
                for i in range(HIDT):
                    m = pe.matmul(b.ps[:, :], w_2[:, i, m_ * P:(m_ + 1) * P], hid[:, i, :], start=(i == 0), stop=(i == HIDT - 1))
                m.then_inc(b.done, 1)

        def pe_out(pe, it, u):
            pe.wait_ge(s["fin_done"], n(it, 2, u + 1))
            for t in range(NT4):
                b = tr(it, "out", u, t)
                b.claim(pe)
                for k in range(KC):
                    m = pe.transpose(b.ps[:, k * P:(k + 1) * P], X[:, u, k, 1 + t * P:1 + (t + 1) * P], id_sb[:, :])
                m.then_inc(b.done, 1)

        clear_after(nc, ctx, sems)
        block = ctx.enter_context(nc.Block())

        @block.sync
        def _(sp):
            early = ((w_qkv[:, :, :], wqkv.rearrange("(k p) n -> p k n", p=P)), (id_sb[:, :], ident),
                     (sc[:, :, :, :].rearrange("p a k d -> p (a k d)"), scales.to_broadcast([P, 4 * D])),
                     (cos_t[:, :, :, :].rearrange("p t k d -> p (t k d)"), tables[:, 0:NT4 * 2 * D]),
                     (sin_t[:, :, :, :].rearrange("p t k d -> p (t k d)"), tables[:, NT4 * 2 * D:]))
            late = ((mask_sb[:, :], mask[:, 0:2 * P]), (id16[:, :], mask[:, 2 * P:]),
                    (w_o[:, :, :], wo.rearrange("(k p) n -> p k n", p=P)), (l_g[:, :], ln_g), (l_b[:, :], ln_b),
                    (b_1[:, :], b1), (b_2[:, :], b2), (w_1[:, :, :], w1.rearrange("(k p) n -> p k n", p=P)),
                    (w_2[:, :, :], w2.rearrange("(k p) n -> p k n", p=P)))
            assert (len(early), len(late)) == (EARLY, LATE)

            def load(it, u):
                bsl = bass.ds(it * 2 + u, 1)
                if lay == 0:
                    for k in range(KC):
                        sp.dma_start(x_next[:, u, k, :].rearrange("p (w t) -> p w t", t=WT),
                                     x_src[0:NW, :, k, bsl, :].rearrange("w p o t -> p (w o) t")).then_inc(x_in[u], 16)
                else:
                    sp.dma_start(x_next[:, u, :, :], x_src[bsl].rearrange("o p k t -> (o p) k t")).then_inc(x_in[u], 16)

            def store(it, u):
                bsl = bass.ds(it * 2 + u, 1)
                if not last:
                    mm(it, "w2", u, 0).released(sp)
                    mm(it, "w2", u, 1).released(sp)
                    sp.dma_start(x_dst[bsl].rearrange("o p k t -> (o p) k t"), X[:, u, :, 1:]).then_inc(x_st[u], 16)
                    return
                sp.wait_ge(s["fin_done"], n(it, 2, u))
                for k in range(KC):
                    sp.dma_start(x2[:, k, :].rearrange("p (w t) -> p w t", t=WT),
                                 x2_d[0:NW, :, k, bsl, :].rearrange("w p o t -> p (w o) t")).then_inc(s["x2_in"], 16)
                tr(it, "out", u, NT4 - 2).released(sp)
                tr(it, "out", u, NT4 - 1).released(sp)
                sp.dma_start(out[bsl].rearrange("o (n p) c -> p (o n) c", p=P), out_sb[:, :, :]).then_inc(s["out_st"], 16)
                sp.sem_inc(x_st[u], 16)

            for dst, src in early[:2]:
                sp.dma_start(dst, src).then_inc(s["loaded"], 16)
            load(0, 0)
            for dst, src in early[2:]:
                sp.dma_start(dst, src).then_inc(s["loaded"], 16)
            load(0, 1)
            for dst, src in late:
                sp.dma_start(dst, src).then_inc(s["loaded_late"], 16)
            with sp.Fori(0, B // 2 - 1) as it:
                for u in U:
                    sp.wait_ge(s["x_ready"], n(it, 2, u + 1))
                    load(it + 1, u)
                for u in U:
                    store(it, u)
            for u in U:
                store(B // 2 - 1, u)
            for u in U:
                sp.wait_ge(x_st[u], 16 * (B // 2 + 1))
            if last:
                sp.wait_ge(s["out_st"], 16 * (B + 1))

        @block.tensor
        def _(pe):
            pe.sem_inc(s["pv_half"], TT)
            pe.wait_ge(s["loaded"], EARLY * 16)
            pe.wait_ge(s["consts"], 1)
            with pe.Fori(0, B // 2) as it:
                for i in range(TT + 3):
                    if i >= 3:
                        pe_turn_qk(pe, it, *divmod(i - 3, NT4))
                    if i < TT:
                        pe_qkv(pe, it, *divmod(i, NT4))
                pe.wait_ge(s["loaded_late"], LATE * 16)
                for u in U:
                    pe_attention(pe, it, u)
                for name, u, *m in norm_order:
                    pe_wo(pe, it, u, *m) if name == "wo" else pe_stat(pe, it, name, u)
                for u in U:
                    pe_mlp(pe, it, u)
                if last:
                    for u in U:
                        pe_out(pe, it, u)

        @block.scalar
        def _(act):
            own = Own(act, s["own_act"])
            act.wait_ge(s["loaded"], EARLY * 16)
            act.wait_ge(s["consts"], 1)
            act.sem_inc(s["nrm_done"], TT)
            act.sem_inc(s["sq_done"], 2 * TT)
            act.sem_inc(s["exp_done"], 4 * RR)
            act.sem_inc(s["csq_done"], 2)
            act.sem_inc(s["hn_ready"], 2)

            def copy(b, out_, in_):
                b.written(act)
                nc.scalar.activation(out_, in_, ACT.Copy).then_inc(b.free, 1)

            def qkv(it, u, t):
                i = u * NT4 + t
                act.wait_ge(s["ssq_done"], n(it, TT, i))
                act.wait_ge(s["rope_done"], n(it, TT, i - 1))
                for kind, name in enumerate(("q", "k")):
                    b = mm(it, name, u, t)
                    b.written(act)
                    nc.scalar.activation(sqr[:, kind * INNER:(kind + 1) * INNER], b.ps[:, :], ACT.Square)\
                        .then_inc(s["sq_done"], 1)
                    copy(b, qk[:, t % 2, kind, :], b.ps[:, :])
                b = mm(it, "v", u, t)
                copy(b, V[:, u, t, :], b.ps[:, :])

            def norm(it, u, t):
                i = u * NT4 + t
                act.wait_ge(s["ssq_done"], n(it, TT, i + 1))
                act.wait_ge(s["inv_done"], n(it, TT, i - 1))
                nc.scalar.activation(nrm[:, t % 2, :], ssq[:, t % 2, :], ACT.Sqrt).then_inc(s["nrm_done"], 1)

            def turned(it, u, t):
                b = tr(it, "qT", u, t)
                b.written(act)
                for hh in range(2):
                    rows = slice(64 * hh, 64 * hh + 64)
                    ins = nc.scalar.activation(QZ[rows, u, hh, :, t * P:(t + 1) * P],
                                               b.ps[rows, :].rearrange("p (h n) -> p h n", h=HPAIRS), ACT.Copy)
                    own.run(ins) if hh == 0 else ins.then_inc(b.free, 1)
                b = tr(it, "kT", u, t)
                b.written(act)
                nc.scalar.activation(KT[:, u, :, t * P:(t + 1) * P], b.ps[:, :].rearrange("p (h n) -> p h n", h=HPAIRS),
                                     ACT.Copy).then_inc(b.free, 1)

            def exps(it, u, k):
                t, r = k // 2, k % 2
                idx = u * 2 * NT4 + k
                b = sim(it, u, t, r)
                lo = P * halves(t)[0]
                act.wait_ge(s["max_done"], n(it, RR, idx + 1))
                ub, kb = before(u, k)
                if kb is not None:
                    for half in halves(kb // 2):
                        tr(it, "pT", ub, kb, half).written(act)
                if k % 2 == 0:
                    act.wait_ge(s["rinv_done"], n(it, TT, u * NT4 + t - 1))
                for hh in range(2):
                    for i in range(2):
                        h4 = 2 * hh + i
                        nc.scalar.activation(PR[:, k % 2, h4, lo:], b.ps[:, hh, i, lo:], ACT.Exp, bias=nmax[:, k % 2, h4:h4 + 1],
                                             accum_out=rsum[:, t % 2, r, h4:h4 + 1]).then_inc(s["exp_done"], 1)
                act.wait_ge(s["exp_done"], n(it, 4 * RR, 4 * (idx + 1)))
                act.sem_inc(b.free, 1)

            def o_turned(it, u, t):
                b = tr(it, "oT", u, t)
                b.written(act)
                nc.scalar.activation(OT[:, u, :, t * P:(t + 1) * P], b.ps[:, :].rearrange("p (h n) -> p h n", h=HPAIRS),
                                     ACT.Copy).then_inc(b.free, 1)

            def squares(it, u):
                mm(it, "mean", u).released(act)
                nc.scalar.activation(SQ[:, u, :, :], cen[:, u, :, :], ACT.Square).then_inc(s["csq_done"], 1)

            def std_devs(it, u):
                b = mm(it, "var", u)
                b.written(act)
                nc.scalar.activation(std[:, u, :], b.ps[:, :], ACT.Sqrt, bias=eps[:, :]).then_inc(b.free, 1)

            def affine(it, u):
                act.wait_ge(s["cn_done"], n(it, 4, 2 * (u + 1)))
                for k in range(KC):
                    ins = nc.scalar.activation(cen[:, u, k, :], cen[:, u, k, :], ACT.Identity, bias=l_b[:, k:k + 1],
                                               scale=l_g[:, k:k + 1])
                    own.run(ins) if k == 0 else ins.then_inc(s["hn_ready"], 1)

            with act.Fori(0, B // 2) as it:
                for i in range(TT + 3):
                    if 1 <= i <= TT:
                        norm(it, *divmod(i - 1, NT4))
                    if i >= 3:
                        turned(it, *divmod(i - 3, NT4))
                    if i < TT:
                        qkv(it, *divmod(i, NT4))
                for u in U:
                    for k in range(K + 3):
                        if k < K:
                            exps(it, u, k)
                        if k >= 4 and k % 2 == 0:
                            o_turned(it, u, k // 2 - 2)
                for u in U:
                    squares(it, u)
                    if u == 0:
                        std_devs(it, 0)
                std_devs(it, 1)
                act.wait_ge(s["loaded_late"], LATE * 16)
                for u in U:
                    affine(it, u)
                for u in U:
                    for i in range(HIDT):
                        b = mm(it, "g", u, i)
                        b.written(act)
                        ub, ib = before(u, i, per=HIDT)
                        if ib is not None:
                            mm(it, "a", ub, ib).released(act)
                        nc.scalar.activation(gel[:, i % 2, :], b.ps[:, :], ACT.Gelu, bias=b_1[:, HIDT + i:HIDT + i + 1])\
                            .then_inc(b.free, 1)
                if last:
                    for u in U:
                        for k in range(4):
                            b = tr(it, "out", u, k)
                            b.written(act)
                            if k == 0:
                                act.wait_ge(s["out_st"], it * 32 + (u * 16 + 16))
                            nc.scalar.activation(out_sb[:, k, :], b.ps[:, 0:C], ACT.Copy).then_inc(b.free, 1)
                own.chain.restart()

        @block.gpsimd
        def _(pool):
            own = Own(pool, s["own_pool"])
            pool.memset(X[:, :, :, 0:1], 0.0)
            pool.memset(mean_w[:, :], 1.0 / C)
            pool.memset(eps[:, :], EPS).then_inc(s["consts"], 1)
            pool.wait_ge(s["consts"], 1)
            pool.sem_inc(s["x_ready"], 2)
            pool.sem_inc(s["qk_ready"], TT)
            pool.sem_inc(s["rot_used"], TT)
            for u in U:
                pool.sem_inc(x_st[u], 16)
            if last:
                pool.sem_inc(s["out_st"], 16)
            for b in range(2):
                for f in (mm_free, tr_free, sim_free):
                    pool.sem_inc(f[b], 1)

            def rotated(it, u, t):
                i = u * NT4 + t
                pool.wait_ge(s["rope_done"], n(it, TT, i + 1))
                r = qkr[:, i % 3, :, :].rearrange("p k (h d) -> p (k h) d", d=D)
                own.order(pool.tensor_tensor(r, r, rot.rearrange("p (h d) -> p h d", d=D), ALU.add),
                           s["rot_used"], n(it, TT, i + 1))

            def normed(it, u, t):
                i = u * NT4 + t
                pool.wait_ge(s["inv_done"], n(it, TT, i + 1))
                r = qkr[:, i % 3, :, :].rearrange("p k (h d) -> p (k h) d", d=D)
                iv = inv[:, t % 2, :].rearrange("p (h o) -> p h o", o=1).to_broadcast([P, 2 * H, D])
                own.order(pool.tensor_tensor(r, r, iv, ALU.mult), s["qk_ready"], n(it, TT, i + 1))

            def take(it, u):
                per = 32 if lay == 0 else 16
                pool.wait_ge(x_in[u], it * per + per)
                pool.wait_ge(x_st[u], it * 16 + 16)
                pool.tensor_tensor(X[:, u, :, 1:], x_next[:, u, :, :], X[:, u, :, 0:1].to_broadcast([P, KC, T]), ALU.add)\
                    .then_inc(s["x_ready"], 1)

            with pool.Fori(0, B // 2) as it:
                take(it, 0)
                for i in range(TT + 1):
                    if i == 2:
                        take(it, 1)
                    if i >= 1:
                        normed(it, *divmod(i - 1, NT4))
                    if i < TT:
                        rotated(it, *divmod(i, NT4))

        @block.vector
        def _(dve):
            own = Own(dve, s["own_dve"])
            for name, k in (("ssq_done", TT), ("inv_done", TT), ("rope_done", TT), ("max_done", RR),
                            ("rinv_done", TT), ("o_done", TT), ("cn_done", 4), ("fin_done", 2)):
                dve.sem_inc(s[name], k)
            for hh in range(2):
                own.run(dve.memset(QZ[64 * (1 - hh):64 * (1 - hh) + 64, :, hh, :, :], 0.0))
            dve.wait_ge(s["loaded"], EARLY * 16)
            dve.wait_ge(s["consts"], 1)
            for t in range(NT4):
                own.run(dve.tensor_tensor(cos_t[:, t, :, :], cos_t[:, t, :, :], sc[:, 0, :, :], ALU.mult))
                own.run(dve.tensor_tensor(sin_t[:, t, :, :], sin_t[:, t, :, :], sc[:, 1, :, :], ALU.mult))
            own.chain.restart()

            def rope(it, u, t):
                i = u * NT4 + t
                mm(it, "q", u, t).released(dve)
                mm(it, "k", u, t).released(dve)
                if i >= 3:
                    tr(it, "kT", *divmod(i - 3, NT4)).written(dve)
                dve.wait_ge(s["rot_used"], n(it, TT, i))
                q = qk[:, t % 2, :, :].rearrange("p k (h d) -> p k h d", d=D)
                bc = lambda tab, lo, hi: tab[:, t, :, lo:hi].rearrange("p k (o d) -> p k o d", o=1).to_broadcast([P, 2, H, hi - lo])
                o_ = qkr[:, i % 3, :, :].rearrange("p k (h d) -> p k h d", d=D)
                ro = rot.rearrange("p (k h d) -> p k h d", k=2, d=D)
                own.run(dve.tensor_tensor(o_, q, bc(cos_t, 0, D), ALU.mult))
                own.run(dve.tensor_tensor(ro[:, :, :, 0:32], q[:, :, :, 32:64], bc(sin_t, 0, 32), ALU.mult))
                own.order(dve.tensor_tensor(ro[:, :, :, 32:64], q[:, :, :, 0:32], bc(sin_t, 32, 64), ALU.mult),
                           s["rope_done"], n(it, TT, i + 1))

            def square_sums(it, u, t):
                i = u * NT4 + t
                dve.wait_ge(s["sq_done"], n(it, 2 * TT, 2 * (i + 1)))
                dve.wait_ge(s["nrm_done"], n(it, TT, i - 1))
                own.order(dve.tensor_reduce(ssq[:, t % 2, :], sqr.rearrange("p (h d) -> p h d", d=D), AX.X, ALU.add),
                          s["ssq_done"], n(it, TT, i + 1))

            def inverse(it, u, t):
                i = u * NT4 + t
                dve.wait_ge(s["nrm_done"], n(it, TT, i + 1))
                dve.wait_ge(s["qk_ready"], n(it, TT, i - 1))
                v = inv[:, t % 2, :]
                own.run(dve.tensor_scalar(v, nrm[:, t % 2, :], 1e-12, None, ALU.max))
                own.run(dve.reciprocal(v, v))
                own.order(dve.tensor_scalar(v[:, 0:H], v[:, 0:H], 8.0, None, ALU.mult), s["inv_done"], n(it, TT, i + 1))

            def row_max(it, u, k):
                t, r = k // 2, k % 2
                idx = u * 2 * NT4 + k
                b = sim(it, u, t, r)
                b.written(dve)
                lo = P * halves(t)[0]
                dve.wait_ge(s["exp_done"], n(it, 4 * RR, 4 * (idx - 1)))
                own.order(dve.tensor_reduce(nmax[:, k % 2, :], b.ps[:, :, :, lo:].rearrange("p a b n -> p (a b) n"), AX.X,
                                             ALU.max, negate=True), s["max_done"], n(it, RR, idx + 1))

            def p_out(it, u, k):
                ub, kb = before(u, k)
                if kb is not None and kb % 2:
                    mm(it, "pv", ub, kb // 2).written(dve)
                elif kb is not None:
                    dve.wait_ge(s["pv_half"], n(it, TT, ub * NT4 + kb // 2 + 1))
                for half in halves(k // 2):
                    b = tr(it, "pT", u, k, half)
                    b.written(dve)
                    dve.tensor_copy(PT[:, k % 2, :, half, :], b.ps[:, :].rearrange("p (h n) -> p h n", h=4)).then_inc(b.free, 1)

            def o_out(it, u, t):
                i = u * NT4 + t
                dve.wait_ge(s["exp_done"], n(it, 4 * RR, 8 * (i + 1)))
                own.order(dve.reciprocal(rinv[:, t % 2, :, :], rsum[:, t % 2, :, :]), s["rinv_done"], n(it, TT, i + 1))
                b = mm(it, "pv", u, t)
                b.written(dve)
                ub, tb = before(u, t, per=NT4)
                if tb is not None:
                    tr(it, "oT", ub, tb).written(dve)
                for r in range(2):
                    o_ = o_sb[:, t % 2, r * 4 * D:(r + 1) * 4 * D].rearrange("p (i h d) -> p h i d", h=2, d=D)
                    p_ = b.ps[:, r * 4 * D:(r + 1) * 4 * D].rearrange("p (i h d) -> p h i d", h=2, d=D)
                    ri = rinv[:, t % 2, r, :].rearrange("p (h i o) -> p h i o", h=2, o=1).to_broadcast([P, 2, 2, D])
                    ins = dve.tensor_tensor(o_, p_, ri, ALU.mult)
                    own.run(ins) if r == 0 else own.order(ins, b.free, b.mine + 1)
                dve.sem_inc(s["o_done"], 1)

            def add_wo(it, u, m_):
                b = mm(it, "wo", u, m_)
                b.written(dve)
                xv = X[:, u, m_, 1:]
                own.order(dve.tensor_tensor(xv, b.ps[:, :], xv, ALU.add), b.free, b.mine + 1)

            def centre(it, u):
                b = mm(it, "mean", u)
                b.written(dve)
                for k in range(KC):
                    ins = dve.tensor_tensor(cen[:, u, k, :], X[:, u, k, 1 - k:1 - k + T], b.ps[:, :], ALU.subtract)
                    own.run(ins) if k == 0 else own.order(ins, b.free, b.mine + 1)

            def normalise(it, u):
                mm(it, "var", u).released(dve)
                own.run(dve.reciprocal(rstd[:, :], std[:, u, :]))
                for k in range(KC):
                    own.order(dve.tensor_tensor(cen[:, u, k, :], cen[:, u, k, :], rstd[:, :], ALU.mult),
                              s["cn_done"], n(it, 4, 2 * u + k + 1))

            with dve.Fori(0, B // 2) as it:
                own.chain.restart()
                for i in range(TT + 1):
                    if i >= 1:
                        inverse(it, *divmod(i - 1, NT4))
                    if i < TT:
                        square_sums(it, *divmod(i, NT4))
                        rope(it, *divmod(i, NT4))
                for u in U:
                    for k in range(K + 3):
                        if k >= 4 and k % 2 == 0:
                            o_out(it, u, k // 2 - 2)
                        if k < K:
                            row_max(it, u, k)
                        if 1 <= k <= K:
                            p_out(it, u, k - 1)
                own.chain.restart()
                dve.wait_ge(s["loaded_late"], LATE * 16)
                add_wo(it, 0, 0)
                add_wo(it, 0, 1)
                add_wo(it, 1, 0)
                centre(it, 0)
                add_wo(it, 1, 1)
                centre(it, 1)
                normalise(it, 0)
                normalise(it, 1)
                for u in U:
                    for i in range(HIDT):
                        b = mm(it, "a", u, i)
                        b.written(dve)
                        mm(it, "g", u, i).released(dve)
                        if u and i == 0:
                            mm(it, "w2", 0, 1).written(dve)
                        ins = dve.scalar_tensor_tensor(out=hid[:, i, :], in0=b.ps[:, :], scalar=b_1[:, i:i + 1], in1=gel[:, i % 2, :],
                                                       op0=ALU.add, op1=ALU.mult)
                        own.order(ins, b.free, b.mine + 1)
                    for m_ in range(KC):
                        b = mm(it, "w2", u, m_)
                        b.written(dve)
                        xv = X[:, u, m_, 1:]
                        own.order(dve.scalar_tensor_tensor(out=xv, in0=b.ps[:, :], scalar=b_2[:, m_:m_ + 1], in1=xv,
                                                            op0=ALU.add, op1=ALU.add), b.free, b.mine + 1)
                    if last:
                        dve.wait_ge(s["x2_in"], it * 64 + (u * 32 + 32))
                        xv = X[:, u, :, 1:]
                        own.order(dve.tensor_tensor(xv, xv, x2[:, :, :], ALU.add), s["fin_done"], n(it, 2, u + 1))
                own.chain.restart()


def program(nc, a, out):
    dram = lambda name, shape: nc.dram_tensor(name, shape, F32, kind="Internal").ap()
    xr_d = dram("xr_d", (NW + 1, P, KC, B, WT))
    xn_d = dram("xn_d", (NW + 2, P, KC, B, WT))
    beta_d = dram("beta_d", (NW + 1, 2, H // 2, B, WT))
    betak_d = dram("betak_d", (NW + 1, 2, H // 2, B, WT))
    o_d = dram("o_d", (NW + 2, P, 2, NC_, WT))
    x2_d = dram("x2_d", (NW, P, KC, B, WT))
    xf_d = dram("xf_d", (NW, P, KC, B, WT))
    x1_d = dram("x1_d", (B, P, KC, T))
    norm_and_beta(nc, a["x"], a["wb"], a["bb"], a["ident"], xr_d, xn_d, beta_d, betak_d, o_d)
    recurrence(nc, a["wq"], a["wk"], a["wv"], a["wa"], a["ba"], a["cw_qk"], a["cb_qk"], a["cw_v"], a["cb_v"],
               a["ident"], a["row_mask"], xn_d, beta_d, betak_d, o_d)
    gate_and_project(nc, a["wg"], a["wo"], a["ln_w"], a["ln_b"], a["w_centre"], xn_d, xr_d, o_d, x2_d, xf_d)
    for lay in range(2):
        last = lay == 1
        w = lambda name: a[f"{name}{lay}"]
        local_layer(nc, lay, last, w("wqkv"), w("wo"), w("w1"), w("b1"), w("w2"), w("b2"), w("lg"), w("lb"), w("scales"),
                    a["tables"], a["ident"], a["mask"], x1_d if last else xf_d, x1_d, x2_d, out)


def kernel(**inputs):
    import ml_dtypes
    import numpy as np
    import concourse.bacc as bacc
    from concourse.bass_utils import run_bass_kernel_spmd

    g = {k: np.asarray(v) for k, v in inputs.items()}
    f32 = np.float32
    hperm = [2 * j + hh for hh in range(2) for j in range(H // 2)]
    tile_cols = lambda v, n: np.ascontiguousarray(v.reshape((n, P) + v.shape[1:]).swapaxes(0, 1))

    row = np.arange(P)
    rb, rh, rs = row // (2 * CT), row // CT % 2, row % CT
    row_mask = np.zeros((P, NSUB - 1, 2, 4), f32)
    for j in range(1, NSUB):
        row_mask[row, j - 1, rh, rb] = rs // ST < j

    D, HID, HIDP = 64, g["L0_ffn_w2"].shape[1], 768
    half_idx = np.arange(0, D, 2, dtype=f32)
    t = np.arange(T, dtype=f32)
    freqs = t[:, None] * (1.0 / f32(10000.0) ** (half_idx / f32(D))).astype(f32)[None, :]
    scale = ((half_idx + 0.4 * D) / (1.4 * D)).astype(f32)[None, :] ** ((t - T // 2) / 64.0).astype(f32)[:, None]
    cos, sin = np.cos(freqs).astype(f32), np.sin(freqs).astype(f32)
    both = lambda lo, hi: np.stack([np.concatenate([lo * m, hi * m], 1) for m in (scale, 1.0 / scale)], 1)
    tiles = lambda v: v.reshape(T // P, P, 2 * D).transpose(1, 0, 2).reshape(P, -1)
    tables = np.concatenate([tiles(both(cos, cos)), tiles(both(-sin, sin))], 1).astype(f32)
    qi, kk = np.arange(P)[:, None], np.arange(2 * P)[None, :]
    mask = np.where((kk >= qi) & (kk - P <= qi), 0.0, -1e30)
    mask = np.concatenate([mask, np.eye(P)], 1).astype(ml_dtypes.bfloat16)

    def pad_halves(v):
        v = v.reshape(v.shape[:-1] + (2, HID))
        return np.pad(v, [(0, 0)] * (v.ndim - 1) + [(0, HIDP - HID)]).reshape(v.shape[:-2] + (2 * HIDP,))

    arrays = {
        "x": g["L0_attn_x"],
        "wq": g["L0_attn_Wq"].T, "wk": g["L0_attn_Wk"].T, "wv": g["L0_attn_Wv"].T, "wa": g["L0_attn_Wa"].T,
        "ba": tile_cols(g["L0_attn_ba"], H), "wb": g["L0_attn_Wb"].T[:, hperm], "bb": g["L0_attn_bb"][hperm][:, None],
        "cw_qk": np.concatenate([tile_cols(g["L0_attn_qc_w"][:, 0, :], 4), tile_cols(g["L0_attn_kc_w"][:, 0, :], 4)], 1),
        "cb_qk": np.concatenate([tile_cols(g["L0_attn_qc_b"], 4), tile_cols(g["L0_attn_kc_b"], 4)], 1),
        "cw_v": tile_cols(g["L0_attn_vc_w"][:, 0, :], 8), "cb_v": tile_cols(g["L0_attn_vc_b"], 8),
        "ident": np.eye(P, dtype=f32), "row_mask": row_mask,
        "wg": g["L0_attn_Wg"].T, "wo": g["L0_attn_Wo"].T,
        "ln_w": g["L0_attn_ln_w"][:, None], "ln_b": g["L0_attn_ln_b"][:, None],
        "w_centre": ((np.eye(P) - 1.0 / P) / DK ** 0.5).astype(f32),
        "tables": tables, "mask": mask,
    }
    for lay in range(2):
        w = lambda name: g["L0_ffn_" + name][lay]
        swap = lambda v: np.concatenate([v[D // 2:], v[:D // 2]])
        arrays.update({
            f"wqkv{lay}": w("wqkv"), f"wo{lay}": w("wo"),
            f"w1{lay}": pad_halves(w("w1")), f"b1{lay}": tile_cols(pad_halves(w("b1")), 2 * HIDP // P),
            f"w2{lay}": np.pad(w("w2"), ((0, HIDP - HID), (0, 0))), f"b2{lay}": tile_cols(w("b2"), KC),
            f"lg{lay}": tile_cols(w("ln_g"), KC), f"lb{lay}": tile_cols(w("ln_b"), KC),
            f"scales{lay}": np.concatenate([w("q_scale"), w("k_scale"), swap(w("q_scale")), swap(w("k_scale"))])[None, :],
        })
    arrays = {k: np.ascontiguousarray(v) for k, v in arrays.items()}
    nc = bacc.Bacc("TRN2", target_bir_lowering=False, num_devices=1)
    aps = {k: nc.dram_tensor("in_" + k, v.shape, mybir.dt.from_np(v.dtype), kind="ExternalInput").ap()
           for k, v in arrays.items()}
    out = nc.dram_tensor("out", (B, T, C), F32, kind="ExternalOutput").ap()
    program(nc, aps, out)
    r = run_bass_kernel_spmd(nc, [{"in_" + k: v for k, v in arrays.items()}], core_ids=[0])
    return r.results[0]["out"]
```
